# Optimizing a Trainium2 kernel written in Bass

```python
import numpy as np
import jax
import jax.numpy as jnp

def _softmax(x, axis=-1):
    return jax.nn.softmax(x, axis=axis)

def _gelu(x):
    return jax.nn.gelu(x, approximate=True)

def _silu(x):
    return jax.nn.silu(x)

def _sigmoid(x):
    return jax.nn.sigmoid(x)

def _layernorm(x, axis=-1, eps=1e-05):
    m = jnp.mean(x, axis=axis, keepdims=True)
    v = jnp.var(x, axis=axis, keepdims=True)
    return (x - m) / jnp.sqrt(v + eps)

def _scatter_add(tgt, idx, src, axis=0):
    return tgt.at[idx].add(src)

def _segment_sum(src, seg, n):
    return jax.ops.segment_sum(src, seg, n)
kernel_name = 'mk_gnn_preln_d4_gnn_r8_c96fd2'

def setup_inputs(seed: int=0):
    np.random.seed(seed)
    _w = jnp.asarray

    def _rec_inputs():
        import jax
        import jax.numpy as jnp
        _gk = jax.random.key(seed)
        x = -0.0001006 + 1 * jax.random.normal(jax.random.fold_in(_gk, 1), (12500, 96), jnp.float32)
        src = jax.random.randint(jax.random.fold_in(_gk, 2), (200000,), 0, 12500, jnp.int32)
        dst = jax.random.randint(jax.random.fold_in(_gk, 3), (200000,), 0, 12500, jnp.int32)
        _o = jnp.argsort(dst, stable=True)
        src = src[_o]
        dst = dst[_o]
        edge_attr_96 = jax.random.uniform(jax.random.fold_in(_gk, 12), (200000, 96), jnp.float32, 0.0, 1.11111)
        return (x, src, dst, edge_attr_96)
    x, src, dst, edge_attr_96 = _rec_inputs()

    def _L0_gnn_setup():
        import jax, jax.numpy as jnp
        import numpy as np
        N_NODES = 6250
        N_EDGES = 100000
        D = 96
        DEPTH = 2
        key = jax.random.key(seed)
        ks = jax.random.split(key, 8)
        scale = 1.0 / np.sqrt(D)
        x = jax.random.normal(ks[0], (N_NODES, D), dtype=jnp.float32)
        W0 = jax.random.normal(ks[1], (DEPTH, D, D), dtype=jnp.float32) * scale
        b0 = jnp.zeros((DEPTH, D), dtype=jnp.float32)
        W1 = jax.random.normal(ks[2], (DEPTH, D, D), dtype=jnp.float32) * scale
        b1 = jnp.zeros((DEPTH, D), dtype=jnp.float32)
        W2 = jax.random.normal(ks[3], (DEPTH, 2 * D, D), dtype=jnp.float32) * (1.0 / np.sqrt(2 * D))
        b2 = jnp.zeros((DEPTH, D), dtype=jnp.float32)
        edge_src = jax.random.randint(ks[4], (N_EDGES,), 0, N_NODES, dtype=jnp.int64 if jax.config.jax_enable_x64 else jnp.int32)
        edge_dst = jnp.sort(jax.random.randint(ks[5], (N_EDGES,), 0, N_NODES, dtype=jnp.int64 if jax.config.jax_enable_x64 else jnp.int32))
        return {'x': x, 'W0': W0, 'b0': b0, 'W1': W1, 'b1': b1, 'W2': W2, 'b2': b2, 'edge_src': edge_src, 'edge_dst': edge_dst}
    _L0_gnn_all = _L0_gnn_setup()
    _L0_gnn_in = {k: v for k, v in _L0_gnn_all.items() if k in ('W0', 'b0', 'W1', 'b1', 'W2', 'b2')}
    del _L0_gnn_all

    def _L1_gnn_setup():
        import jax, jax.numpy as jnp
        import numpy as np
        N_NODES = 6250
        N_EDGES = 100000
        D_IN = 96
        D_OUT = 96
        key = jax.random.key(seed)
        k1, k2, k3, k4 = jax.random.split(key, 4)
        x = jax.random.normal(k1, (N_NODES, D_IN), dtype=jnp.float32)
        edge_index = jax.random.randint(k2, (2, N_EDGES), 0, N_NODES, dtype=jnp.int64)
        W = jax.random.normal(k3, (D_IN, D_OUT), dtype=jnp.float32) * (1.0 / np.sqrt(D_IN))
        b = jax.random.normal(k4, (D_OUT,), dtype=jnp.float32) * 0.01
        return {'x': x, 'edge_index': edge_index, 'W': W, 'b': b}
    _L1_gnn_all = _L1_gnn_setup()
    _L1_gnn_in = {k: v for k, v in _L1_gnn_all.items() if k in ('W', 'b')}
    del _L1_gnn_all

    def _L2_gnn_setup():
        import jax, jax.numpy as jnp
        import numpy as np
        N_NODES = 6250
        N_EDGES = 100000
        D_IN = 96
        D_HID = 96
        D_OUT = 96

        def gcn_conv(x, W, b, src, dst, num_nodes):
            deg = jax.ops.segment_sum(jnp.ones_like(dst, dtype=x.dtype), dst, num_segments=num_nodes)
            dinv = jnp.where(deg > 0, jax.lax.rsqrt(deg), 0.0)
            norm = dinv[src] * dinv[dst]
            h = x @ W
            msg = h[src] * norm[:, None]
            out = jax.ops.segment_sum(msg, dst, num_segments=num_nodes)
            return out + b
        key = jax.random.key(seed)
        ks = jax.random.split(key, 8)
        x = jax.random.normal(ks[0], (N_NODES, D_IN), dtype=jnp.float32)
        edge_index = jax.random.randint(ks[1], (2, N_EDGES), 0, N_NODES, dtype=jnp.int64)
        s_in = 1.0 / np.sqrt(D_IN)
        s_h = 1.0 / np.sqrt(D_HID)
        W1 = jax.random.normal(ks[2], (D_IN, D_HID), dtype=jnp.float32) * s_in
        b1 = jnp.zeros((D_HID,), dtype=jnp.float32)
        W2 = jax.random.normal(ks[3], (D_HID, D_HID), dtype=jnp.float32) * s_h
        b2 = jnp.zeros((D_HID,), dtype=jnp.float32)
        W3 = jax.random.normal(ks[4], (D_HID, D_OUT), dtype=jnp.float32) * s_h
        b3 = jnp.zeros((D_OUT,), dtype=jnp.float32)
        return {'x': x, 'edge_index': edge_index, 'W1': W1, 'b1': b1, 'W2': W2, 'b2': b2, 'W3': W3, 'b3': b3}
    _L2_gnn_all = _L2_gnn_setup()
    _L2_gnn_in = {k: v for k, v in _L2_gnn_all.items() if k in ('W1', 'b1', 'W2', 'b2', 'W3', 'b3')}
    del _L2_gnn_all

    def _L3_gnn_setup():
        import jax, jax.numpy as jnp
        import numpy as np
        N_NODES = 6250
        N_EDGES = 100000
        D = 96
        EDGE_DROP = 0.1
        key = jax.random.key(seed)
        ks = jax.random.split(key, 12)
        d2 = 2 * D
        s1 = 1.0 / np.sqrt(d2)
        s2 = 1.0 / np.sqrt(D)
        h = jax.random.normal(ks[0], (N_NODES, D), dtype=jnp.float32)
        src = jax.random.randint(ks[1], (N_EDGES,), 0, N_NODES, dtype=jnp.int32)
        dst = jax.random.randint(ks[2], (N_EDGES,), 0, N_NODES, dtype=jnp.int32)
        Wm1 = jax.random.uniform(ks[3], (d2, D), jnp.float32, -s1, s1)
        bm1 = jnp.zeros((D,), jnp.float32)
        Wm2 = jax.random.uniform(ks[4], (D, D), jnp.float32, -s2, s2)
        bm2 = jnp.zeros((D,), jnp.float32)
        Wu1 = jax.random.uniform(ks[5], (d2, D), jnp.float32, -s1, s1)
        bu1 = jnp.zeros((D,), jnp.float32)
        Wu2 = jax.random.uniform(ks[6], (D, D), jnp.float32, -s2, s2)
        bu2 = jnp.zeros((D,), jnp.float32)
        keep = 1.0 - EDGE_DROP
        drop_mask = (jax.random.uniform(ks[7], (N_EDGES, D)) < keep).astype(jnp.float32) / keep
        return {'h': h, 'Wm1': Wm1, 'bm1': bm1, 'Wm2': Wm2, 'bm2': bm2, 'Wu1': Wu1, 'bu1': bu1, 'Wu2': Wu2, 'bu2': bu2, 'drop_mask': drop_mask, 'src': src, 'dst': dst}
    _L3_gnn_all = _L3_gnn_setup()
    _L3_gnn_in = {k: v for k, v in _L3_gnn_all.items() if k in ('Wm1', 'bm1', 'Wm2', 'bm2', 'Wu1', 'bu1', 'Wu2', 'bu2')}
    del _L3_gnn_all
    return {'x': x, 'src': src, 'dst': dst, 'edge_attr_96': edge_attr_96, 'L0_gnn_W0': _L0_gnn_in['W0'], 'L0_gnn_b0': _L0_gnn_in['b0'], 'L0_gnn_W1': _L0_gnn_in['W1'], 'L0_gnn_b1': _L0_gnn_in['b1'], 'L0_gnn_W2': _L0_gnn_in['W2'], 'L0_gnn_b2': _L0_gnn_in['b2'], 'L1_gnn_W': _L1_gnn_in['W'], 'L1_gnn_b': _L1_gnn_in['b'], 'L2_gnn_W1': _L2_gnn_in['W1'], 'L2_gnn_b1': _L2_gnn_in['b1'], 'L2_gnn_W2': _L2_gnn_in['W2'], 'L2_gnn_b2': _L2_gnn_in['b2'], 'L2_gnn_W3': _L2_gnn_in['W3'], 'L2_gnn_b3': _L2_gnn_in['b3'], 'L3_gnn_Wm1': _L3_gnn_in['Wm1'], 'L3_gnn_bm1': _L3_gnn_in['bm1'], 'L3_gnn_Wm2': _L3_gnn_in['Wm2'], 'L3_gnn_bm2': _L3_gnn_in['bm2'], 'L3_gnn_Wu1': _L3_gnn_in['Wu1'], 'L3_gnn_bu1': _L3_gnn_in['bu1'], 'L3_gnn_Wu2': _L3_gnn_in['Wu2'], 'L3_gnn_bu2': _L3_gnn_in['bu2']}

def reference(x, src, dst, edge_attr_96, L0_gnn_W0, L0_gnn_b0, L0_gnn_W1, L0_gnn_b1, L0_gnn_W2, L0_gnn_b2, L1_gnn_W, L1_gnn_b, L2_gnn_W1, L2_gnn_b1, L2_gnn_W2, L2_gnn_b2, L2_gnn_W3, L2_gnn_b3, L3_gnn_Wm1, L3_gnn_bm1, L3_gnn_Wm2, L3_gnn_bm2, L3_gnn_Wu1, L3_gnn_bu1, L3_gnn_Wu2, L3_gnn_bu2):
    import jax
    import jax.numpy as jnp

    def _L0_gnn_ref(x, W0, b0, W1, b1, W2, b2, edge_src, edge_dst):
        import jax, jax.numpy as jnp
        import numpy as np
        N_NODES = 6250
        N_EDGES = 100000
        D = 96
        DEPTH = 2
        n = x.shape[0]
        depth = W0.shape[0]
        for i in range(depth):
            h_self = x @ W1[i] + b1[i]
            h_nb = x @ W0[i] + b0[i]
            agg = jax.ops.segment_sum(h_nb[edge_src], edge_dst, num_segments=n)
            x = jnp.concatenate([h_self, agg], axis=-1) @ W2[i] + b2[i]
            x = x / jnp.std(x, axis=-1, ddof=1, keepdims=True)
        return x

    def _L1_gnn_ref(x, edge_index, W, b):
        import jax, jax.numpy as jnp
        import numpy as np
        N_NODES = 6250
        N_EDGES = 100000
        D_IN = 96
        D_OUT = 96
        num_nodes = x.shape[0]
        src, dst = (edge_index[0], edge_index[1])
        messages = x[src] @ W + b
        out = jax.ops.segment_sum(messages, dst, num_segments=num_nodes)
        deg = jax.ops.segment_sum(jnp.ones((dst.shape[0],), dtype=x.dtype), dst, num_segments=num_nodes)
        deg = jnp.clip(deg, 1.0, None)
        return out / deg[:, None]

    def _L2_gnn_ref(x, edge_index, W1, b1, W2, b2, W3, b3):
        import jax, jax.numpy as jnp
        import numpy as np
        N_NODES = 6250
        N_EDGES = 100000
        D_IN = 96
        D_HID = 96
        D_OUT = 96

        def gcn_conv(x, W, b, src, dst, num_nodes):
            deg = jax.ops.segment_sum(jnp.ones_like(dst, dtype=x.dtype), dst, num_segments=num_nodes)
            dinv = jnp.where(deg > 0, jax.lax.rsqrt(deg), 0.0)
            norm = dinv[src] * dinv[dst]
            h = x @ W
            msg = h[src] * norm[:, None]
            out = jax.ops.segment_sum(msg, dst, num_segments=num_nodes)
            return out + b
        num_nodes = x.shape[0]
        loop = jnp.arange(num_nodes, dtype=edge_index.dtype)
        src = jnp.concatenate([edge_index[0], loop])
        dst = jnp.concatenate([edge_index[1], loop])
        h = gcn_conv(x, W1, b1, src, dst, num_nodes)
        h = jax.nn.relu(h)
        h = gcn_conv(h, W2, b2, src, dst, num_nodes)
        h = jax.nn.relu(h)
        return gcn_conv(h, W3, b3, src, dst, num_nodes)

    def _L3_gnn_ref(h, Wm1, bm1, Wm2, bm2, Wu1, bu1, Wu2, bu2, drop_mask, src, dst):
        import jax, jax.numpy as jnp
        import numpy as np
        N_NODES = 6250
        N_EDGES = 100000
        D = 96
        EDGE_DROP = 0.1
        n = h.shape[0]
        e = jnp.concatenate([h[src], h[dst]], axis=-1)
        e = jax.nn.relu(e @ Wm1 + bm1) @ Wm2 + bm2
        e = e * drop_mask
        m = jax.ops.segment_sum(e, dst, num_segments=n)
        z = jnp.concatenate([h, m], axis=-1)
        h_new = jax.nn.relu(z @ Wu1 + bu1) @ Wu2 + bu2
        return h_new
    edge_index = jnp.stack([src, dst])
    h = jnp.maximum(_layernorm(x, axis=-1), 0.0)
    x = x + _L0_gnn_ref(h, L0_gnn_W0, L0_gnn_b0, L0_gnn_W1, L0_gnn_b1, L0_gnn_W2, L0_gnn_b2, src, dst)
    h = jnp.maximum(_layernorm(x, axis=-1), 0.0)
    x = x + _L1_gnn_ref(h, edge_index, L1_gnn_W, L1_gnn_b)
    h = jnp.maximum(_layernorm(x, axis=-1), 0.0)
    x = x + _L2_gnn_ref(h, edge_index, L2_gnn_W1, L2_gnn_b1, L2_gnn_W2, L2_gnn_b2, L2_gnn_W3, L2_gnn_b3)
    h = jnp.maximum(_layernorm(x, axis=-1), 0.0)
    x = x + _L3_gnn_ref(h, L3_gnn_Wm1, L3_gnn_bm1, L3_gnn_Wm2, L3_gnn_bm2, L3_gnn_Wu1, L3_gnn_bu1, L3_gnn_Wu2, L3_gnn_bu2, edge_attr_96, src, dst)
    return x

_drawn_inputs = setup_inputs


def setup_inputs(seed=0):
    import zlib

    import numpy as np

    out = dict(_drawn_inputs(seed))
    spreads = {'L0_gnn_b0': (0.0, 0.1),
     'L0_gnn_b1': (0.0, 0.585),
     'L0_gnn_b2': (0.0, 0.443),
     'L2_gnn_b1': (0.0, 0.272),
     'L2_gnn_b2': (0.0, 0.1),
     'L2_gnn_b3': (0.0, 0.1),
     'L3_gnn_bm1': (0.0, 0.1),
     'L3_gnn_bm2': (0.0, 0.1),
     'L3_gnn_bu1': (0.0, 0.33),
     'L3_gnn_bu2': (0.0, 0.1)}
    factors = {'L1_gnn_b': 8.0}
    for name, (base, spread) in spreads.items():
        noise = np.random.default_rng([zlib.crc32(name.encode()), seed]).standard_normal(out[name].shape)
        drawn = base * np.exp(spread * noise) if base else spread * noise
        out[name] = jnp.asarray(drawn.astype(out[name].dtype))
    for name, factor in factors.items():
        out[name] = (out[name] * factor).astype(out[name].dtype)
    return out
```

```python
from contextlib import ExitStack

import concourse.bass as bass
from concourse import mybir

F32 = mybir.dt.float32
I32 = mybir.dt.int32
ALU = mybir.AluOpType
ACT = mybir.ActivationFunctionType
AX = mybir.AxisListType.X

N, D = 12500, 96
E = 200000
NP, NJ = 125, 100
CH = 10
PAIRS = NJ // CH // 2
P = 128
TPG = 8
GE = P * TPG
GROUPS = -(-E // GE)
LAST = E - GE
MASKED = (GROUPS * GE - E) // TPG
WIN = 128
EXTRA = (N - 1) // WIN
FAR = -1.0e6
EPS = 1e-5
SETUP_ROWS = 10
SETUP_EXTRA = SETUP_ROWS + 4 + 16 + 4
SETUP_TURNED = SETUP_EXTRA + 3
DEGREES = SETUP_TURNED + 6 + 3


def build(nc, t, out):
    ctx = ExitStack()
    with ctx:
        def sb(name, shape, dt=F32):
            return ctx.enter_context(nc.sbuf_tensor(name, shape, dt))

        def sem(name):
            return ctx.enter_context(nc.semaphore(name))

        def dram(name, shape):
            return nc.dram_tensor(name, shape, F32, kind="Internal").ap()

        table = dram("table", (N, D))
        qtable = dram("qtable", (N + WIN, D))
        degs = dram("degs", (1, N))
        table_rows = table.rearrange("(p j) f -> p (j f)", j=NJ)
        q_rows = qtable[0:N, :].rearrange("(p j) f -> p (j f)", j=NJ)
        x_node_rows = t["x"].rearrange("(p j) f -> p (j f)", j=NJ)
        out_rows = out.rearrange("(p j) f -> p (j f)", j=NJ)

        X = sb("X", [P, NJ * D])
        AGG = sb("AGG", [D + 1, N + WIN])
        HT = sb("HT", [D + 1, N])
        SRC = sb("SRC", [P, GROUPS * TPG], I32)
        REL = sb("REL", [P, GROUPS * TPG])
        G = sb("G", [P, 2, TPG, D + 1])
        IDX = sb("IDX", [P, 2, TPG], I32)
        QW = sb("QW", [P, 2, D])
        work = sb("work", [P, 8840])
        CW = CH * D
        XC = work[:, 0:CW]
        SQ = work[:, CW:2 * CW]
        H = [work[:, (2 + k) * CW:(3 + k) * CW] for k in range(2)]
        SW = CH * NP
        AGS = [work[0:D + 1, 4 * CW + k * SW:4 * CW + (k + 1) * SW] for k in range(2)]
        HTS = [work[0:D + 1, 4 * CW + (2 + k) * SW:4 * CW + (3 + k) * SW] for k in range(2)]
        QB = G[:, :, :, :].rearrange("p k i f -> p (k i f)")[:, 0:CW]
        OH = [work[:, k * TPG * WIN:(k + 1) * TPG * WIN].rearrange("p (i w) -> p i w", i=TPG) for k in range(2)]
        ATTR = [work[:, 2048 + k * TPG * D:2048 + (k + 1) * TPG * D] for k in range(2)]
        OHT = work[:, 4 * CW:4 * CW + GE]
        MSG = work[:, 4 * CW + SW:4 * CW + SW + TPG * D].rearrange("p (i f) -> p i f", i=TPG)
        RT = work[0:D + 1, 4 * CW + 2 * SW:4 * CW + 2 * SW + GE]
        DSTI = work[:, 0:GROUPS * TPG].bitcast(I32)
        XTAB = work[:, 1600:1600 + 3 * GROUPS].rearrange("p (c g) -> p c g", c=3)
        XEQ = work[:, 2200:2200 + GROUPS]
        XM = work[:, 2400:2400 + GROUPS]
        XD = work[:, 2600:2600 + 4 * P].rearrange("p (c k) -> p c k", c=4)
        WR = work[:, 4 * CW:4 * CW + 11 * D].rearrange("p (c f) -> p c f", c=11)
        WTR = work[:, 4 * CW + 11 * D:4 * CW + 11 * D + 4 * P].rearrange("p (c k) -> p c k", c=4)
        IOI = work[:, 3200:3200 + GROUPS + 1].bitcast(I32)

        small = sb("small", [P, 2 * CH * 4])
        st = [small[:, c * 2 * CH:(c + 1) * 2 * CH] for c in range(4)]
        ident = sb("ident", [P, P])
        ones = sb("ones", [P, P])
        IOF = sb("IOF", [P, GROUPS])
        PCOL = sb("PCOL", [P, 1])
        SHIFT = sb("SHIFT", [P, P])
        XREL = sb("XREL", [P, TPG])
        col = sb("col", [P, 12])
        rowf = sb("rowf", [1, 4 * GROUPS])
        rowi = sb("rowi", [1, 2 * GROUPS], I32)
        XI = sb("XI", [1, 3 * P], I32)
        NX = sb("NX", [1, 1], I32)
        DEG = sb("DEG", [P, NJ])
        DINV = sb("DINV", [P, NJ])
        RDEG = sb("RDEG", [P, NJ])
        epsc = sb("epsc", [P, 1])
        zcol = sb("zcol", [P, 1])
        W = sb("W", [P, 18 * D])
        BASE_I, LAST_I = rowi[:, 0:GROUPS], rowi[:, GROUPS:2 * GROUPS]
        C_ROW, CX_ROW, BASE_F, NE_ROW = (rowf[:, k * GROUPS:(k + 1) * GROUPS] for k in range(4))

        def wt(k, rows=D + 1, n=1):
            return W[0:rows, k * D:(k + n) * D]

        w_self, w_nb = [wt(0), wt(1)], [wt(2), wt(3)]
        w_l1 = wt(4)
        w_l2 = [wt(5, D), wt(6, D), wt(7, D)]
        w_m1 = wt(8, D, 2)
        w_m2 = wt(10)
        w_u1 = [wt(11, D), wt(12, D)]
        w_u2 = wt(13)
        b_l2 = [wt(14 + k, P) for k in range(3)]
        bcols = sb("bcols", [D, 2])

        PS = ctx.enter_context(nc.psum_tensor("PS", [P, 8, 512], F32))

        s_edges = sem("s_edges")
        s_rows = sem("s_rows")
        s_x = sem("s_x")
        s_w = sem("s_w")
        s_const = sem("s_const")
        s_iof = sem("s_iof")
        s_dv = sem("s_dv")
        s_pe = sem("s_pe")
        s_ready = sem("s_ready")
        s_degd = sem("s_degd")
        s_degl = sem("s_degl")
        s_rt = sem("s_rt")
        n_chain = sem("n_chain")
        n_ags = sem("n_ags")
        n_cleared = sem("n_cleared")
        n_hts = sem("n_hts")
        n_out = sem("n_out")
        n_read = sem("n_read")
        n_xc = sem("n_xc")
        n_sq = sem("n_sq")
        n_var = sem("n_var")
        n_sd = sem("n_sd")
        n_h = sem("n_h")
        n_tr = sem("n_tr")
        n_ev = sem("n_ev")
        n_st = sem("n_st")
        n_pq = sem("n_pq")
        n_pqc = sem("n_pqc")
        n_hid = sem("n_hid")
        n_rel = sem("n_rel")
        s_store = sem("s_store")
        a_idx = sem("a_idx")
        a_rows = [[sem(f"a_rows{s}{k}") for k in range(2)] for s in range(2)]
        a_oh = sem("a_oh")
        a_sum = sem("a_sum")
        a_acc = sem("a_acc")
        e_attr = [sem(f"e_attr{k}") for k in range(2)]
        e_q = [sem(f"e_q{k}") for k in range(2)]
        e_turn = sem("e_turn")
        e_oht = sem("e_oht")
        e_pre = sem("e_pre")
        e_rel = sem("e_rel")
        e_out = sem("e_out")
        e_msg = sem("e_msg")
        x_rows = [sem("x_rows0"), sem("x_rows1")]
        x_idx, x_sub, x_oh, x_sum, x_acc = (
            sem(n) for n in ("x_idx", "x_sub", "x_oh", "x_sum", "x_acc"))
        x_ld, x_turn, x_oht, x_pre, x_rel, x_out, x_msg = (
            sem(n) for n in ("x_ld", "x_turn", "x_oht", "x_pre", "x_rel", "x_out", "x_msg"))

        PHASES = ["in", "l0a", "l0b", "l1", "l2a", "l2b", "l2c"]
        NCH = NJ // CH
        NONE = "the tables are built on the chip from destinations in range"

        def cols(view, j0, n=CH):
            return view[:, 0:N].rearrange("f (p j) -> f j p", j=NJ)[:, bass.ds(j0, n), :]

        def xchunk(c):
            return X[0:NP, bass.ds(c * CW, CW)]

        def c3(ap):
            return ap[0:NP, :].rearrange("p (j f) -> p j f", f=D)

        def banks(b):
            return PS[0:NP, b:b + 2, 0:5 * D].rearrange("p b (j f) -> p b j f", f=D)

        def c4(ap):
            return ap[0:NP, :].rearrange("p (b j f) -> p b j f", b=2, f=D)

        def per_block(v):
            return v.rearrange("p (b j) -> p b j", b=2).unsqueeze(3).to_broadcast([NP, 2, 5, D])

        def per_block3(v):
            return v.unsqueeze(2).to_broadcast([NP, CH, D])

        def load(eng, etype, ap, hi):
            return nc.values_load(ap, engines=[etype], min_val=0, max_val=hi,
                                  skip_runtime_bounds_check_because=NONE)

        block = ctx.enter_context(nc.Block())
        ET = mybir.EngineType

        @block.sync
        def _(sp):
            for name, dst in (("src", SRC[:, :]), ("dst", DSTI)):
                sp.dma_start(dst[:, 0:(GROUPS - 1) * TPG].rearrange("p (g i) -> p g i", i=TPG),
                             t[name][0:(GROUPS - 1) * GE].rearrange("(g p i) -> p g i", p=P, i=TPG)
                             ).then_inc(s_edges, 16)
                sp.dma_start(dst[:, (GROUPS - 1) * TPG:GROUPS * TPG],
                             t[name][LAST:E].rearrange("(p i) -> p i", i=TPG)).then_inc(s_edges, 16)
            d2 = t["dst"][0:(GROUPS - 1) * GE].rearrange("(a g k) -> a g k", a=1, k=GE)
            sp.dma_start(BASE_I[:, 0:GROUPS - 1], d2[:, :, 0], allow_slow_non_contiguous=True).then_inc(s_rows, 16)
            sp.dma_start(LAST_I[:, 0:GROUPS - 1], d2[:, :, GE - 1], allow_slow_non_contiguous=True).then_inc(s_rows, 16)
            first = (GROUPS - 1) * GE
            sp.dma_start(BASE_I[:, GROUPS - 1:GROUPS], t["dst"][first:first + 1].rearrange("(a k) -> a k", a=1)
                         ).then_inc(s_rows, 16)
            sp.dma_start(LAST_I[:, GROUPS - 1:GROUPS], t["dst"][E - 1:E].rearrange("(a k) -> a k", a=1)
                         ).then_inc(s_rows, 16)
            sp.dma_start(X[0:NP, :], x_node_rows).then_inc(s_x, 16)
            row = lambda ap: ap.rearrange("(a f) -> a f", a=1)
            for l in range(2):
                sp.dma_start(WR[0:D, l, :], t["L0_gnn_W1"][l]).then_inc(s_w, 16)
                sp.dma_start(WR[D:D + 1, l, :], t["L0_gnn_b1"][l:l + 1, :]).then_inc(s_w, 16)
                sp.dma_start(WR[0:D, 2 + l, :], t["L0_gnn_W0"][l]).then_inc(s_w, 16)
                sp.dma_start(WR[D:D + 1, 2 + l, :], t["L0_gnn_b0"][l:l + 1, :]).then_inc(s_w, 16)
                sp.dma_start(WR[0:D, 4 + l, :], t["L0_gnn_W2"][l, 0:D, :]).then_inc(s_w, 16)
                sp.dma_start(WR[0:D, 6 + l, :], t["L0_gnn_W2"][l, D:2 * D, :]).then_inc(s_w, 16)
                sp.dma_start(WR[D:D + 1, 8 + l, :], t["L0_gnn_b2"][l:l + 1, :]).then_inc(s_w, 16)
            for dst, src in ((w_l1[0:D], t["L1_gnn_W"]), (w_l1[D:D + 1], row(t["L1_gnn_b"])),
                             (w_l2[0], t["L2_gnn_W1"]), (w_l2[1], t["L2_gnn_W2"]), (w_l2[2], t["L2_gnn_W3"]),
                             (w_m1[:, 0:D], t["L3_gnn_Wm1"][0:D, :]), (w_m1[:, D:2 * D], t["L3_gnn_Wm1"][D:2 * D, :]),
                             (w_m2[0:D], t["L3_gnn_Wm2"]), (w_m2[D:D + 1], row(t["L3_gnn_bm2"])),
                             (w_u1[0], t["L3_gnn_Wu1"][0:D, :]), (w_u1[1], t["L3_gnn_Wu1"][D:2 * D, :]),
                             (w_u2[0:D], t["L3_gnn_Wu2"]), (w_u2[D:D + 1], row(t["L3_gnn_bu2"])),
                             (bcols[:, 0:1], t["L3_gnn_bm1"].rearrange("(f a) -> f a", a=1)),
                             (bcols[:, 1:2], t["L3_gnn_bu1"].rearrange("(f a) -> f a", a=1))):
                sp.dma_start(dst, src).then_inc(s_w, 16)
            for k, name in enumerate(("L2_gnn_b1", "L2_gnn_b2", "L2_gnn_b3")):
                sp.dma_start(b_l2[k], row(t[name]).to_broadcast([P, D])).then_inc(s_w, 16)

            def node_stores(phase):
                b = phase * NCH
                with sp.Fori(0, PAIRS) as i:
                    for k in range(2):
                        c = i * 2 + k
                        sp.wait_ge(n_h, c + (b + 1))
                        sp.dma_start(table_rows[:, bass.ds(c * CW, CW)], H[k][0:NP, :]).then_inc(s_store, 16)
                        sp.wait_ge(s_store, c * 16 + (b * 16 + 16))
                        sp.sem_inc(n_st, 1)

            sp.sem_inc(n_st, 2)
            node_stores(0)
            sp.wait_ge(s_ready, 1)
            n_extra = load(sp, ET.SP, NX[0:1, 0:1], EXTRA)
            sp.wait_ge(a_acc, 2 + GROUPS)
            with sp.If(n_extra > 0):
                sp.wait_ge(x_acc, 1 + EXTRA)
            sp.dma_start(degs, AGG[D:D + 1, 0:N]).then_inc(s_degd, 16)
            sp.wait_ge(s_degd, 16)
            sp.dma_start(DEG[0:NP, :], degs.rearrange("a (p j) -> (a p) j", j=NJ)).then_inc(s_degl, 16)
            for phase in range(1, 6):
                node_stores(phase)
            with sp.Fori(0, PAIRS) as i:
                for k in range(2):
                    c = i * 2 + k
                    sp.wait_ge(n_pqc, c + 3)
                    sp.dma_start(table_rows[:, bass.ds(c * CW, CW)], H[k][0:NP, :]).then_inc(s_store, 16)
                    sp.dma_start(q_rows[:, bass.ds(c * CW, CW)], QB[0:NP, :]).then_inc(s_store, 16)
                    sp.wait_ge(s_store, c * 32 + (6 * NCH * 16 + 32))
                    sp.sem_inc(n_st, 1)
            sp.wait_ge(s_const, 1)
            sp.dma_start(qtable[N:N + WIN, :], QW[:, 1, :]).then_inc(s_x, 16)
            sp.wait_ge(s_x, 32)

            def attributes(row):
                return t["edge_attr_96"][bass.ds(row, GE), :].rearrange("(p i) f -> p (i f)", i=TPG)

            def edge_loads(g, row, k):
                sp.wait_ge(a_sum, g + (6 * GROUPS + 1))
                base = load(sp, ET.SP, BASE_I[0:1, bass.ds(g, 1)], N - 1)
                sp.dma_start(ATTR[k], attributes(row)).then_inc(e_attr[k], 16)
                sp.dma_start(QW[:, k, :], qtable[bass.ds(base, WIN), :]).then_inc(e_q[k], 16)

            with sp.Fori(0, GROUPS // 2 - 1) as i:
                for k in range(2):
                    edge_loads(i * 2 + k, (i * 2 + k) * GE, k)
            edge_loads(GROUPS - 2, (GROUPS - 2) * GE, 0)
            edge_loads(GROUPS - 1, LAST, 1)
            with sp.If(n_extra > 0):
                sp.wait_ge(a_acc, 2 + 7 * GROUPS)
                with sp.Fori(0, EXTRA) as j:
                    sp.wait_ge(x_acc, j + (6 * EXTRA + 1))
                    base = load(sp, ET.SP, XI[0:1, bass.ds(j + P, 1)], N - 1)
                    row = load(sp, ET.SP, XI[0:1, bass.ds(j + 2 * P, 1)], LAST)
                    sp.dma_start(ATTR[0], attributes(row)).then_inc(x_ld, 16)
                    sp.dma_start(QW[:, 0, :], qtable[bass.ds(base, WIN), :]).then_inc(x_ld, 16)
            with sp.Fori(0, PAIRS) as i:
                for k in range(2):
                    c = i * 2 + k
                    sp.wait_ge(n_h, c + (7 * NCH + 1))
                    sp.dma_start(out_rows[:, bass.ds(c * CW, CW)], H[k][0:NP, :]).then_inc(s_store, 16)
                    sp.wait_ge(s_store, c * 16 + (8 * NCH * 16 + 16))
                    sp.sem_inc(n_st, 1)

        @block.gpsimd
        def _(pool):
            pool.memset(QW[:, :, :], 0.0).then_inc(s_const, 1)
            pool.memset(AGG[:, :], 0.0).then_inc(s_const, 1)
            pool.memset(G[:, :, :, D:D + 1], 1.0).then_inc(s_const, 1)
            pool.wait_ge(s_const, 3)
            pool.memset(HT[D:D + 1, :], 1.0).then_inc(s_const, 1)
            pool.wait_ge(s_const, 4)
            pool.memset(ones[:, :], 1.0).then_inc(s_const, 1)
            pool.memset(epsc[:, :], EPS).then_inc(s_const, 1)
            pool.memset(zcol[:, :], 0.0).then_inc(s_const, 1)
            pool.iota(IOI[:, 0:GROUPS], pattern=[[1, GROUPS]], base=0, channel_multiplier=0).then_inc(s_const, 1)
            pool.iota(IOI[:, GROUPS:GROUPS + 1], pattern=[[1, 1]], base=0, channel_multiplier=1).then_inc(s_const, 1)
            pool.memset(ident[:, :], 0.0).then_inc(s_const, 1)
            pool.wait_ge(s_const, 10)
            pool.affine_select(out=ident[:, :], in_=ident[:, :], compare_op=ALU.not_equal, fill=1.0,
                               base=0, pattern=[[-1, P]], channel_multiplier=1).then_inc(s_const, 1)
            pool.wait_ge(s_ready, 1)
            n_extra = load(pool, ET.Pool, NX[0:1, 0:1], EXTRA)

            def gathers(k, done):
                for i in range(TPG):
                    pool.indirect_dma_start(G[:, k, i, 0:D], None, table,
                                            bass.IndirectOffsetOnAxis(ap=IDX[:, k, i:i + 1], axis=0)
                                            ).then_inc(done, 16)

            def aggregation(a):
                pool.wait_ge(n_st, 2 + (a + 1) * NCH)
                pool.nop(nofuse=True)
                with pool.Fori(0, GROUPS // 2) as i:
                    for k in range(2):
                        g = i * 2 + k
                        pool.wait_ge(a_idx, g + (a * GROUPS + 1))
                        pool.nop(nofuse=True)
                        gathers(k, a_rows[a // 4][k])
                with pool.If(n_extra > 0):
                    with pool.Fori(0, EXTRA) as j:
                        pool.wait_ge(x_idx, j + (a * EXTRA + 1))
                        pool.nop(nofuse=True)
                        gathers(0, x_rows[a // 4])

            def staging(phase, clear):
                q0 = (phase - 1) * NCH
                pool.wait_ge(a_acc, 2 + phase * GROUPS)
                pool.nop(nofuse=True)
                with pool.If(n_extra > 0):
                    pool.wait_ge(x_acc, 1 + phase * EXTRA)
                    pool.nop(nofuse=True)
                if phase == 1:
                    pool.wait_ge(s_degd, 16)
                    pool.nop(nofuse=True)
                with pool.Fori(0, PAIRS) as i:
                    for k in range(2):
                        c = i * 2 + k
                        pool.wait_ge(n_out, c + (q0 + 1))
                        pool.nop(nofuse=True)
                        pool.tensor_copy(AGS[k].rearrange("f (j p) -> f j p", j=CH),
                                         cols(AGG, c * CH)).then_inc(n_ags, 1)
                        if clear:
                            pool.wait_ge(n_ags, c + (q0 + 1))
                            pool.nop(nofuse=True)
                            pool.tensor_copy(cols(AGG, c * CH), zcol[0:D + 1, 0:1].unsqueeze(2).to_broadcast([D + 1, CH, NP])
                                             ).then_inc(n_cleared, 1)

            for a in range(7):
                aggregation(a)
                if a < 6:
                    staging(a + 1, clear=PHASES[a + 1] in ("l0a", "l0b", "l2c"))

        @block.scalar
        def _(act):
            act.sem_inc(n_ev, 1)
            act.sem_inc(n_rel, 1)
            act.wait_ge(s_const, 11)
            n_extra = None
            count = {"xc": 0, "ev": 0, "hts": 0}

            def node(phase):
                name = PHASES[phase]
                stats = {"in": 1, "l0a": 1, "l0b": 2, "l1": 1, "l2a": 0, "l2b": 0, "l2c": 1}[name]
                turn = name != "l0b"
                xc0, ev0, hts0, q0 = count["xc"], count["ev"], count["hts"], (phase - 1) * NCH

                def stage(c, k):
                    act.wait_ge(n_out, c + (q0 + 1))
                    act.wait_ge(n_ev, 1 + ev0)
                    act.nop(nofuse=True)
                    act.activation(HTS[k].rearrange("f (j p) -> f j p", j=CH), cols(HT, c * CH), ACT.Copy).then_inc(n_hts, 1)

                def step(c, k):
                    for s in range(stats):
                        v = c * stats + (xc0 + s + 1)
                        act.wait_ge(n_xc, v)
                        act.activation(SQ[0:NP, :], XC[0:NP, :], ACT.Square).then_inc(n_sq, 1)
                        act.wait_ge(n_var, v)
                        if name == "l0a" or (name == "l0b" and s == 0):
                            act.activation(st[2][0:NP, 0:CH], st[1][0:NP, 0:CH], ACT.Sqrt, bias=0.0,
                                           scale=1.0 / (D - 1)).then_inc(n_sd, 1)
                        else:
                            act.activation(st[2][0:NP, 0:CH], st[1][0:NP, 0:CH], ACT.Sqrt, bias=epsc[0:NP, 0:1],
                                           scale=1.0 / D).then_inc(n_sd, 1)
                    if turn:
                        act.wait_ge(n_tr, c + (ev0 + 3))
                        if name == "l2c":
                            hs = HTS[k][0:D, :].rearrange("f (j p) -> f j p", j=CH)
                            act.wait_ge(n_pqc, c + 1)
                            dst = [hs[:, 0:4, :], hs[:, 4:8, :], hs[:, 8:10, :]]
                        else:
                            target = HT[0:D] if name in ("in", "l0a") else AGG[0:D]
                            dst = [cols(target, c * CH + b, n) for b, n in ((0, 4), (4, 4), (8, 2))]
                        act.nop(nofuse=True)
                        for b, n in ((0, 4), (1, 4), (2, 2)):
                            last = act.activation(dst[b], PS[0:D, 4 + b, 0:n * NP].rearrange(
                                "f (j p) -> f j p", j=n), ACT.Copy)
                        last.then_inc(n_ev, 1)
                        if name == "l2c":
                            act.nop(nofuse=True)
                            for b, n in ((0, 4), (1, 4), (2, 2)):
                                last = act.activation(cols(HT[0:D], c * CH + 4 * b, n),
                                                      PS[0:D, 4 + b, 0:n * NP].rearrange("f (j p) -> f j p", j=n),
                                                      ACT.Copy)
                            last.then_inc(n_hts, 1)

                if name in ("l0a", "l0b"):
                    stage(0, 0)
                    with act.Fori(0, PAIRS - 1) as i:
                        for k in range(2):
                            stage(i * 2 + k + 1, 1 - k)
                            step(i * 2 + k, k)
                    stage(NCH - 1, 1)
                    step(NCH - 2, 0)
                    step(NCH - 1, 1)
                    count["hts"] += NCH
                else:
                    with act.Fori(0, PAIRS) as i:
                        for k in range(2):
                            step(i * 2 + k, k)
                count["xc"] += stats * NCH
                count["ev"] += NCH * turn

            def indices(a):
                with act.Fori(0, GROUPS // 2) as i:
                    for k in range(2):
                        g = i * 2 + k
                        act.wait_ge(a_sum, g + (a * GROUPS + 1))
                        act.nop(nofuse=True)
                        act.activation(IDX[:, k, :], SRC[:, bass.ds(g * TPG, TPG)], ACT.Copy).then_inc(a_idx, 1)

            def turned_and_relu(oht_when, oht_sem, oht_done, pre_when, pre_sem, rel_done):
                act.wait_ge(oht_sem, oht_when)
                act.activation(OHT.rearrange("p (b k) -> p b k", b=2), PS[:, 4:6, :], ACT.Copy).then_inc(oht_done, 1)
                act.wait_ge(pre_sem, pre_when)
                act.activation(RT[0:D, :].rearrange("f (b k) -> f b k", b=2), PS[0:D, 2:4, :], ACT.Relu,
                               bias=bcols[:, 0:1]).then_inc(rel_done, 1)

            def edge_network():
                def idx(g, k):
                    act.wait_ge(a_sum, g + (6 * GROUPS + 1))
                    act.nop(nofuse=True)
                    act.activation(IDX[:, k, :], SRC[:, bass.ds(g * TPG, TPG)], ACT.Copy).then_inc(a_idx, 1)

                idx(0, 0)
                with act.Fori(0, GROUPS // 2 - 1) as i:
                    for k in range(2):
                        g = i * 2 + k
                        idx(g + 1, 1 - k)
                        turned_and_relu(g + 1, e_turn, e_oht, g + 1, e_pre, e_rel)
                idx(GROUPS - 1, 1)
                for g in (GROUPS - 2, GROUPS - 1):
                    turned_and_relu(g + 1, e_turn, e_oht, g + 1, e_pre, e_rel)

            def extras(a):
                with act.If(n_extra > 0):
                    act.wait_ge(a_sum, 2 + (a + 1) * GROUPS)
                    with act.Fori(0, EXTRA) as j:
                        act.wait_ge(x_acc, j + (a * EXTRA + 1))
                        g = load(act, ET.Activation, XI[0:1, bass.ds(j, 1)], GROUPS - 1)
                        act.nop(nofuse=True)
                        act.activation(IDX[:, 0, :], SRC[:, bass.ds(g * TPG, TPG)], ACT.Copy).then_inc(x_idx, 1)
                        if a == 6:
                            turned_and_relu(j + 1, x_turn, x_oht, j + 1, x_pre, x_rel)

            node(0)
            act.wait_ge(s_ready, 1)
            n_extra = load(act, ET.Activation, NX[0:1, 0:1], EXTRA)
            for a in range(6):
                indices(a)
                extras(a)
                if a == 0:
                    act.wait_ge(s_dv, DEGREES)
                    act.activation(DINV[0:NP, :], DEG[0:NP, :], ACT.Sqrt).then_inc(s_rt, 1)
                node(a + 1)
            edge_network()
            extras(6)
            act.wait_ge(s_w, 16 * 32)
            with act.Fori(0, PAIRS) as i:
                for k in range(2):
                    c = i * 2 + k
                    act.wait_ge(n_hid, c + 1)
                    act.wait_ge(n_out, c + (6 * NCH + 1))
                    act.nop(nofuse=True)
                    for b, n in ((0, 4), (1, 4), (2, 2)):
                        last = act.activation(HTS[k][0:D, 4 * b * NP:(4 * b + n) * NP], PS[0:D, 4 + b, 0:n * NP],
                                              ACT.Relu, bias=bcols[:, 1:2])
                    last.then_inc(n_rel, 1)

        @block.vector
        def _(dve):
            dve.sem_inc(n_read, 2)
            dve.sem_inc(a_acc, 2)
            dve.sem_inc(x_acc, 1)
            dve.sem_inc(n_pqc, 2)
            steps = [0]

            def link(ins):
                steps[0] += 1
                ins.then_inc(s_dv, 1)
                dve.wait_ge(s_dv, steps[0])

            dve.wait_ge(s_const, 11)
            link(dve.tensor_copy(IOF[:, :], IOI[:, 0:GROUPS]))
            link(dve.tensor_copy(PCOL[:, :], IOI[:, GROUPS:GROUPS + 1]))
            dve.wait_ge(s_edges, 64)
            dve.wait_ge(s_rows, 64)
            link(dve.tensor_copy(REL[:, :], DSTI))
            link(dve.tensor_copy(BASE_F, BASE_I))
            link(dve.tensor_tensor(LAST_I, LAST_I, BASE_I, ALU.subtract))
            link(dve.tensor_scalar(LAST_I, LAST_I, WIN.bit_length() - 1, None, ALU.arith_shift_right))
            link(dve.tensor_copy(NE_ROW, LAST_I))
            link(dve.tensor_tensor_scan(C_ROW, ones[0:1, 0:1].to_broadcast([1, GROUPS]), NE_ROW, 0.0,
                                        ALU.mult, ALU.add))
            link(dve.tensor_tensor(CX_ROW, C_ROW, NE_ROW, ALU.subtract))
            link(dve.tensor_copy(NX[0:1, 0:1], C_ROW[:, GROUPS - 1:GROUPS]))
            assert steps[0] == SETUP_ROWS
            dve.wait_ge(s_pe, 1)
            link(dve.tensor_copy(XTAB[:, 0:2, :], PS[:, 0, 0:2 * GROUPS].rearrange("p (c g) -> p c g", c=2)))
            link(dve.tensor_copy(XTAB[:, 2, :], PS[:, 1, 0:GROUPS]))
            link(dve.tensor_tensor(REL[:, :].rearrange("p (g i) -> p g i", i=TPG),
                                   REL[:, :].rearrange("p (g i) -> p g i", i=TPG),
                                   XTAB[:, 2, :].unsqueeze(2).to_broadcast([P, GROUPS, TPG]), ALU.subtract))
            link(dve.memset(REL[0:MASKED, (GROUPS - 1) * TPG:GROUPS * TPG], FAR))
            gj, cx, gb, used, shift = (col[:, k:k + 1] for k in range(5))
            four = [col[:, 8 + k:9 + k] for k in range(4)]
            link(dve.tensor_scalar(XEQ, XTAB[:, 0, :], PCOL[:, 0:1], None, ALU.is_le))
            link(dve.reduce_sum(gj, XEQ, AX))
            link(dve.tensor_scalar(XEQ, IOF[:, :], gj, None, ALU.is_equal))
            link(dve.tensor_tensor(XM, XEQ, XTAB[:, 1, :], ALU.mult))
            link(dve.reduce_sum(cx, XM, AX))
            link(dve.tensor_tensor(XM, XEQ, XTAB[:, 2, :], ALU.mult))
            link(dve.reduce_sum(gb, XM, AX))
            link(dve.tensor_tensor(used, PCOL[:, 0:1], XTAB[:, 0, GROUPS - 1:GROUPS], ALU.is_lt))
            link(dve.tensor_tensor(shift, PCOL[:, 0:1], cx, ALU.subtract))
            link(dve.tensor_scalar(shift, shift, 1.0, float(WIN), ALU.add, ALU.mult))
            link(dve.tensor_scalar(four[0], gj, float(GROUPS - 1), None, ALU.min))
            link(dve.tensor_tensor(gb, gb, shift, ALU.add))
            link(dve.tensor_tensor(four[1], gb, used, ALU.mult))
            link(dve.tensor_scalar(four[2], four[0], float(GE), float(LAST), ALU.mult, ALU.min))
            link(dve.tensor_scalar(used, used, -1.0, FAR, ALU.add, ALU.mult))
            link(dve.tensor_tensor(four[3], shift, used, ALU.add))
            for k in range(4):
                link(dve.tensor_scalar(XD[:, k, :], ident[:, :], four[k], None, ALU.mult))
            assert steps[0] == SETUP_EXTRA
            dve.wait_ge(s_pe, 2)
            link(dve.tensor_copy(XI[0:1, :], PS[0:1, 2, 0:3 * P]))
            link(dve.tensor_copy(SHIFT[:, :], PS[:, 2, 3 * P:4 * P]))
            dve.wait_ge(s_pe, 3)
            link(dve.tensor_copy(WTR[0:D, :, 0:D + 1], PS[0:D, 3, 0:4 * P].rearrange("f (c k) -> f c k", c=4)[:, :, 0:D + 1]))
            assert steps[0] == SETUP_TURNED
            dve.wait_ge(s_pe, 4)
            for l in range(2):
                link(dve.tensor_copy(w_self[l], PS[0:D + 1, 4, l * D:(l + 1) * D]))
                link(dve.tensor_tensor(w_self[l][D:D + 1, :], w_self[l][D:D + 1, :], WR[D:D + 1, 8 + l, :], ALU.add))
                link(dve.tensor_copy(w_nb[l], PS[0:D + 1, 4, (2 + l) * D:(3 + l) * D]))
            dve.sem_inc(s_ready, 1)

            count = {"chain": 0, "xc": 0, "tr": 0}

            def node(phase):
                name = PHASES[phase] if phase < 7 else "fin"
                ch0, xc0, tr0 = count["chain"], count["xc"], count["tr"]
                q0, h0 = (phase - 1) * NCH, phase * NCH
                stats_n = {"in": 1, "l0a": 1, "l0b": 2, "l1": 1, "l2a": 0, "l2b": 0, "l2c": 1, "fin": 0}[name]
                turn = name not in ("l0b", "fin")
                if name == "in":
                    dve.wait_ge(s_x, 16)

                chain_n = {"in": 3, "l0a": 3, "l0b": 7, "l1": 5, "l2a": 1, "l2b": 1, "l2c": 6, "fin": 0}[name]

                def chunk(c, k):
                    n = [0, 0]

                    def then(ins):
                        n[0] += 1
                        ins.then_inc(n_chain, 1)
                        dve.wait_ge(n_chain, c * chain_n + (ch0 + n[0]))

                    def stats(src, view):
                        n[1] += 1
                        v = c * stats_n + (xc0 + n[1])
                        mean = st[0][0:NP, 0:CH]
                        if view == 4:
                            then(dve.reduce_sum(mean.rearrange("p (b j) -> p b j", b=2), src, AX))
                        else:
                            dve.nop(nofuse=True)
                            then(dve.reduce_sum(mean, src, AX))
                        then(dve.tensor_scalar(mean, mean, -1.0 / D, None, ALU.mult))
                        if view == 4:
                            dve.tensor_tensor(c4(XC), src, per_block(mean), ALU.add).then_inc(n_xc, 1)
                        else:
                            dve.tensor_tensor(c3(XC), src, per_block3(mean), ALU.add).then_inc(n_xc, 1)
                        dve.wait_ge(n_sq, v)
                        dve.reduce_sum(st[1][0:NP, 0:CH], c3(SQ), AX).then_inc(n_var, 1)
                        dve.wait_ge(n_sd, v)
                        then(dve.reciprocal(st[3][0:NP, 0:CH], st[2][0:NP, 0:CH]))

                    def h_free():
                        dve.wait_ge(n_st, c + (h0 + 1))
                        dve.wait_ge(n_tr, c + (tr0 + 1) if turn else tr0 + 2)

                    inv = st[3][0:NP, 0:CH]
                    xk = X[0:NP, bass.ds(c * CW, CW)]
                    dinv = DINV[0:NP, bass.ds(c * CH, CH)]
                    if name != "in":
                        dve.wait_ge(n_out, c + (q0 + 3))
                        prod = banks(2 * k)
                    if name == "l0a":
                        stats(prod, 4)
                        h_free()
                        dve.tensor_tensor(c4(H[k]), prod, per_block(inv), ALU.mult).then_inc(n_h, 1)
                        dve.wait_ge(n_h, c + (h0 + 1))
                        dve.sem_inc(n_read, 1)
                    elif name == "fin":
                        h_free()
                        dve.tensor_tensor(c4(H[k]), xk.rearrange("p (b j f) -> p b j f", b=2, f=D), prod,
                                          ALU.add).then_inc(n_h, 1)
                        dve.wait_ge(n_h, c + (h0 + 1))
                        dve.sem_inc(n_read, 1)
                    else:
                        if name == "l0b":
                            stats(prod, 4)
                            dve.tensor_tensor(c4(XC), prod, per_block(inv), ALU.mult).then_inc(n_read, 1)
                        elif name == "l1":
                            dve.tensor_tensor(c4(XC), prod, per_block(RDEG[0:NP, bass.ds(c * CH, CH)]),
                                              ALU.mult).then_inc(n_read, 1)
                        elif name != "in":
                            dve.tensor_tensor(c4(XC), prod, per_block(dinv), ALU.mult).then_inc(n_read, 1)
                        if name != "in":
                            dve.wait_ge(n_read, c + (q0 + 3))
                        if name in ("l2a", "l2b", "l2c"):
                            bias = b_l2[("l2a", "l2b", "l2c").index(name)][0:NP, :]
                            then(dve.tensor_tensor(c3(XC), c3(XC), bias.unsqueeze(1).to_broadcast([NP, CH, D]),
                                                   ALU.add))
                        if name in ("l0b", "l1", "l2c"):
                            then(dve.tensor_tensor(xk, xk, XC[0:NP, :], ALU.add))
                        if name in ("l2a", "l2b"):
                            scale = dinv
                        else:
                            stats(xk.rearrange("p (j f) -> p j f", f=D), 3)
                            if name == "l1":
                                then(dve.tensor_tensor(inv, inv, dinv, ALU.mult))
                            scale = inv
                        h_free()
                        dve.scalar_tensor_tensor(out=c3(H[k]), in0=c3(XC), scalar=0.0, in1=per_block3(scale),
                                                 op0=ALU.max, op1=ALU.mult).then_inc(n_h, 1)
                        dve.wait_ge(n_h, c + (h0 + 1))
                        if name == "l2c":
                            dve.wait_ge(n_pq, c + 1)
                            dve.wait_ge(n_st, c + (h0 + 2))
                            then(dve.tensor_copy(c4(H[k]), banks(2 * k)))
                            dve.tensor_copy(c4(QB), banks(4)).then_inc(n_pqc, 1)
                    assert n[0] == chain_n, (name, n[0])

                with dve.Fori(0, PAIRS) as i:
                    for k in range(2):
                        chunk(i * 2 + k, k)
                count["chain"] += chain_n * NCH
                count["xc"] += stats_n * NCH
                count["tr"] += turn * NCH

            def one_hot(dst, rel):
                return dve.tensor_tensor(dst, IOF[:, 0:WIN].unsqueeze(1).to_broadcast([P, TPG, WIN]),
                                         rel.unsqueeze(2).to_broadcast([P, TPG, WIN]), ALU.is_equal)

            def accumulate(rows, base, k):
                window = AGG[0:rows, bass.ds(base, WIN)]
                return dve.tensor_tensor(window, window, PS[0:rows, k, 0:WIN], ALU.add)

            def messages(k):
                return dve.tensor_tensor(MSG.rearrange("p (b i) f -> p b i f", b=2),
                                         PS[:, 6:8, 0:4 * D].rearrange("p b (i f) -> p b i f", f=D),
                                         ATTR[k].rearrange("p (b i f) -> p b i f", b=2, f=D), ALU.mult)

            def aggregation(a):
                g0, rows, net = a * GROUPS, D + 1 if a < 6 else D, a == 6
                dve.wait_ge(n_st, 2 + (a + 1) * NCH)
                dve.wait_ge(n_tr, 2 + count["tr"])
                dve.wait_ge(n_ev, 1 + count["tr"])
                if a:
                    dve.wait_ge(n_cleared, {1: 1, 2: 2, 6: 3}.get(a, 2) * NCH)

                def make(g, k):
                    dve.wait_ge(a_sum, g + (g0 + 1))
                    one_hot(OH[k], REL[:, bass.ds(g * TPG, TPG)]).then_inc(a_oh, 1)

                def add(g, k, pair):
                    if net:
                        dve.wait_ge(e_out, g + 1)
                        dve.wait_ge(e_attr[k], pair * 16 + 16)
                        messages(k).then_inc(e_msg, 1)
                    base = load(dve, ET.DVE, BASE_I[0:1, bass.ds(g, 1)], N - 1)
                    dve.wait_ge(a_sum, g + (g0 + 3))
                    dve.wait_ge(a_acc, g + (g0 + 2))
                    accumulate(rows, base, k).then_inc(a_acc, 1)

                make(0, 0)
                with dve.Fori(0, GROUPS // 2 - 1) as i:
                    for k in range(2):
                        make(i * 2 + k + 1, 1 - k)
                        add(i * 2 + k, k, i)
                make(GROUPS - 1, 1)
                add(GROUPS - 2, 0, GROUPS // 2 - 1)
                add(GROUPS - 1, 1, GROUPS // 2 - 1)
                with dve.If(n_extra > 0):
                    with dve.Fori(0, EXTRA) as j:
                        v = j + (a * EXTRA + 1)
                        g = load(dve, ET.DVE, XI[0:1, bass.ds(j, 1)], GROUPS - 1)
                        base = load(dve, ET.DVE, XI[0:1, bass.ds(j + P, 1)], N - 1)
                        dve.wait_ge(x_acc, v)
                        dve.tensor_scalar(XREL[:, :], REL[:, bass.ds(g * TPG, TPG)], SHIFT[:, bass.ds(j, 1)], None,
                                          ALU.subtract).then_inc(x_sub, 1)
                        dve.wait_ge(x_sub, v)
                        one_hot(OH[0], XREL[:, :]).then_inc(x_oh, 1)
                        if net:
                            dve.wait_ge(x_out, j + 1)
                            dve.wait_ge(x_ld, j * 32 + 32)
                            messages(0).then_inc(x_msg, 1)
                        dve.wait_ge(x_sum, v)
                        accumulate(rows, base, 0).then_inc(x_acc, 1)
                    dve.wait_ge(x_acc, (a + 1) * EXTRA + 1)

            node(0)
            n_extra = load(dve, ET.DVE, NX[0:1, 0:1], EXTRA)
            for a in range(6):
                aggregation(a)
                if a == 0:
                    dve.wait_ge(s_degl, 16)
                    link(dve.tensor_scalar(RDEG[0:NP, :], DEG[0:NP, :], 1.0, None, ALU.max))
                    link(dve.reciprocal(RDEG[0:NP, :], RDEG[0:NP, :]))
                    link(dve.tensor_scalar(DEG[0:NP, :], DEG[0:NP, :], 1.0, None, ALU.add))
                    assert steps[0] == DEGREES
                    dve.wait_ge(s_rt, 1)
                    link(dve.reciprocal(DINV[0:NP, :], DINV[0:NP, :]))
                if a == 3:
                    dve.wait_ge(s_w, 16 * 32)
                node(a + 1)
            aggregation(6)
            node(7)

        @block.tensor
        def _(pe):
            pe.sem_inc(n_out, 2)
            pe.sem_inc(n_tr, 2)
            pe.sem_inc(a_sum, 2)
            pe.wait_ge(s_const, 11)
            pe.wait_ge(s_dv, SETUP_ROWS)
            pe.matmul(PS[:, 0, 0:2 * GROUPS], ones[0:1, :], rowf[:, 0:2 * GROUPS], start=True, stop=True)
            pe.matmul(PS[:, 1, 0:GROUPS], ones[0:1, :], BASE_F, start=True, stop=True).then_inc(s_pe, 1)
            pe.wait_ge(s_dv, SETUP_EXTRA)
            pe.matmul(PS[:, 2, :], ones[:, :], XD, start=True, stop=True).then_inc(s_pe, 1)
            pe.wait_ge(s_w, 16 * 32)
            for m in range(4):
                last = pe.transpose(PS[0:D, 3, m * P:m * P + D + 1], WR[0:D + 1, m, :], ident[0:D + 1, 0:D + 1])
            last.then_inc(s_pe, 1)
            pe.wait_ge(s_dv, SETUP_TURNED)
            for m in range(4):
                last = pe.matmul(PS[0:D + 1, 4, m * D:(m + 1) * D], WTR[0:D, m, 0:D + 1], WR[0:D, 4 + m, :],
                                 start=True, stop=True)
            last.then_inc(s_pe, 1)
            pe.wait_ge(s_ready, 1)
            n_extra = load(pe, ET.PE, NX[0:1, 0:1], EXTRA)
            count = {"tr": 0, "hts": 0}

            def node(phase):
                name = PHASES[phase] if phase < 7 else "fin"
                q0, h0, tr0, hts0 = (phase - 1) * NCH, phase * NCH, count["tr"], count["hts"]
                turn = name not in ("l0b", "fin")

                def product(c, k):
                    if name == "fin":
                        pe.wait_ge(n_rel, c + 1)
                        for b, n in ((0, 4), (1, 4), (2, 2)):
                            o = PS[0:D, 4 + b, 0:n * NP].rearrange("f (j p) -> f j p", j=n)
                            pe.matmul(o, w_u1[0], cols(HT[0:D], c * CH + 4 * b, n), start=True, stop=False)
                            last = pe.matmul(o, w_u1[1], cols(AGG[0:D], c * CH + 4 * b, n), start=False, stop=True)
                        last.then_inc(n_hid, 1)
                        pe.wait_ge(n_rel, c + 2)
                        parts = [(HTS[k], w_u2, D + 1)]
                    else:
                        pe.wait_ge(n_ags, c + (q0 + 1))
                        if name in ("l0a", "l0b"):
                            l = name == "l0b"
                            pe.wait_ge(n_hts, c + (hts0 + 1))
                            parts = [(HTS[k], w_self[l], D + 1), (AGS[k], w_nb[l], D + 1)]
                        elif name == "l1":
                            parts = [(AGS[k], w_l1, D + 1)]
                        else:
                            parts = [(AGS[k], w_l2[("l2a", "l2b", "l2c").index(name)], D)]
                    pe.wait_ge(n_read, c + (q0 + 1))
                    if name == "l2c":
                        pe.wait_ge(n_pqc, c + 1)
                    for j in range(CH):
                        o = PS[0:NP, 2 * k + j // 5, (j % 5) * D:(j % 5 + 1) * D]
                        for m, (stage, w, rows) in enumerate(parts):
                            last = pe.matmul(o, stage[0:rows, j * NP:(j + 1) * NP], w,
                                             start=(m == 0), stop=(m == len(parts) - 1))
                    last.then_inc(n_out, 1)

                def turned(c, k):
                    pe.wait_ge(n_h, c + (h0 + 1))
                    pe.wait_ge(n_ev, c + (tr0 + 1))
                    if name == "l2c":
                        pe.wait_ge(n_pqc, c + 2)
                    for j in range(CH):
                        last = pe.transpose(PS[0:D, 4 + j // 4, (j % 4) * NP:(j % 4 + 1) * NP],
                                            H[k][0:NP, j * D:(j + 1) * D], ident[0:NP, 0:NP])
                    last.then_inc(n_tr, 1)
                    if name == "l2c":
                        pe.wait_ge(n_ev, c + (tr0 + 2))
                        pe.wait_ge(n_hts, c + (hts0 + 1))
                        for half, b0 in ((0, 2 * k), (1, 4)):
                            for j in range(CH):
                                last = pe.matmul(PS[0:NP, b0 + j // 5, (j % 5) * D:(j % 5 + 1) * D],
                                                 HTS[k][0:D, j * NP:(j + 1) * NP],
                                                 w_m1[:, half * D:(half + 1) * D], start=True, stop=True)
                        last.then_inc(n_pq, 1)

                if name == "in":
                    with pe.Fori(0, PAIRS) as i:
                        for k in range(2):
                            turned(i * 2 + k, k)
                elif not turn:
                    if name == "fin":
                        pe.wait_ge(a_acc, 2 + 7 * GROUPS)
                        with pe.If(n_extra > 0):
                            pe.wait_ge(x_acc, 1 + 7 * EXTRA)
                    with pe.Fori(0, PAIRS) as i:
                        for k in range(2):
                            product(i * 2 + k, k)
                else:
                    product(0, 0)
                    with pe.Fori(0, PAIRS - 1) as i:
                        for k in range(2):
                            product(i * 2 + k + 1, 1 - k)
                            turned(i * 2 + k, k)
                    product(NCH - 1, 1)
                    turned(NCH - 2, 0)
                    turned(NCH - 1, 1)
                count["tr"] += turn * NCH
                count["hts"] += NCH * (name in ("l0a", "l0b", "l2c"))

            def window_sums(k, done):
                for i in range(TPG):
                    last = pe.matmul(PS[0:D + 1, k, 0:WIN], G[:, k, i, :], OH[k][:, i, :],
                                     start=(i == 0), stop=(i == TPG - 1))
                last.then_inc(done, 1)

            def turn_one_hots(k, done):
                for i in range(TPG):
                    last = pe.transpose(PS[:, 4 + i // 4, (i % 4) * P:(i % 4 + 1) * P], OH[k][:, i, :], ident[:, :])
                last.then_inc(done, 1)

            def hidden(k, done):
                for i in range(TPG):
                    o = PS[0:D, 2 + i // 4, (i % 4) * P:(i % 4 + 1) * P]
                    pe.matmul(o, QW[:, k, :], OHT[:, i * P:(i + 1) * P], start=True, stop=False)
                    last = pe.matmul(o, G[:, k, i, 0:D], ident[:, :], start=False, stop=True)
                last.then_inc(done, 1)

            def edge_out(done):
                for i in range(TPG):
                    last = pe.matmul(PS[:, 6 + i // 4, (i % 4) * D:(i % 4 + 1) * D], RT[:, i * P:(i + 1) * P],
                                     w_m2, start=True, stop=True)
                last.then_inc(done, 1)

            def message_sums(k, done):
                for i in range(TPG):
                    last = pe.matmul(PS[0:D, k, 0:WIN], MSG[:, i, :], OH[k][:, i, :],
                                     start=(i == 0), stop=(i == TPG - 1))
                last.then_inc(done, 1)

            def aggregation(a):
                g0 = a * GROUPS
                with pe.Fori(0, GROUPS // 2) as i:
                    for k in range(2):
                        g = i * 2 + k
                        pe.wait_ge(a_oh, g + (g0 + 1))
                        if a == 6:
                            turn_one_hots(k, e_turn)
                            pe.wait_ge(e_oht, g + 1)
                            pe.wait_ge(e_q[k], i * 16 + 16)
                        pe.wait_ge(a_rows[a // 4][k], i * (16 * TPG) + (a % 4 * GROUPS // 2 + 1) * 16 * TPG)
                        if a == 6:
                            hidden(k, e_pre)
                            pe.wait_ge(e_rel, g + 1)
                            edge_out(e_out)
                            pe.wait_ge(e_msg, g + 1)
                        pe.wait_ge(a_acc, g + (g0 + 1))
                        if a == 6:
                            message_sums(k, a_sum)
                        else:
                            window_sums(k, a_sum)
                with pe.If(n_extra > 0):
                    pe.wait_ge(a_acc, 2 + (a + 1) * GROUPS)
                    with pe.Fori(0, EXTRA) as j:
                        v = j + (a * EXTRA + 1)
                        pe.wait_ge(x_oh, v)
                        if a == 6:
                            turn_one_hots(0, x_turn)
                            pe.wait_ge(x_oht, j + 1)
                            pe.wait_ge(x_ld, j * 32 + 32)
                        pe.wait_ge(x_rows[a // 4], j * (16 * TPG) + (a % 4 * EXTRA + 1) * 16 * TPG)
                        if a == 6:
                            hidden(0, x_pre)
                            pe.wait_ge(x_rel, j + 1)
                            edge_out(x_out)
                            pe.wait_ge(x_msg, j + 1)
                            message_sums(0, x_sum)
                        else:
                            window_sums(0, x_sum)

            node(0)
            for a in range(6):
                aggregation(a)
                node(a + 1)
            aggregation(6)
            node(7)


_INS = ["x", "src", "dst", "edge_attr_96", "L0_gnn_W0", "L0_gnn_b0", "L0_gnn_W1", "L0_gnn_b1", "L0_gnn_W2",
        "L0_gnn_b2", "L1_gnn_W", "L1_gnn_b", "L2_gnn_W1", "L2_gnn_b1", "L2_gnn_W2", "L2_gnn_b2", "L2_gnn_W3",
        "L2_gnn_b3", "L3_gnn_Wm1", "L3_gnn_bm1", "L3_gnn_Wm2", "L3_gnn_bm2", "L3_gnn_Wu1", "L3_gnn_bu1",
        "L3_gnn_Wu2", "L3_gnn_bu2"]


def kernel(**inputs):
    import numpy as _np
    import concourse.bacc as _bacc
    from concourse import mybir as _mybir
    from concourse.bass_utils import run_bass_kernel_spmd as _run

    nc = _bacc.Bacc("TRN2", target_bir_lowering=False, num_devices=1)
    arrays, tensors = {}, {}
    for name in _INS:
        a = _np.ascontiguousarray(inputs[name])
        arrays[f"in_{name}_dram"] = a
        tensors[name] = nc.dram_tensor(f"in_{name}_dram", a.shape, _mybir.dt.from_np(a.dtype),
                                       kind="ExternalInput").ap()
    out = nc.dram_tensor("out_0_dram", (N, D), F32, kind="ExternalOutput").ap()
    build(nc, tensors, out)
    r = _run(nc, [arrays], core_ids=[0])
    return r.results[0]["out_0_dram"]
```

```python
from contextlib import ExitStack

import concourse.bass as bass
from concourse import mybir

F32 = mybir.dt.float32
I32 = mybir.dt.int32
ALU = mybir.AluOpType
ACT = mybir.ActivationFunctionType
AX = mybir.AxisListType.X

N, D = 12500, 96
E = 200000
NP, NJ = 125, 100
CH = 10
PAIRS = NJ // CH // 2
P = 128
TPG = 8
GE = P * TPG
GROUPS = -(-E // GE)
LAST = E - GE
MASKED = (GROUPS * GE - E) // TPG
WIN = 128
EXTRA = (N - 1) // WIN
FAR = -1.0e6
EPS = 1e-5
SETUP_ROWS = 10
SETUP_EXTRA = SETUP_ROWS + 4 + 16 + 4
SETUP_TURNED = SETUP_EXTRA + 3
DEGREES = SETUP_TURNED + 6 + 3


def build(nc, t, out):
    ctx = ExitStack()
    with ctx:
        def sb(name, shape, dt=F32):
            return ctx.enter_context(nc.sbuf_tensor(name, shape, dt))

        def sem(name):
            return ctx.enter_context(nc.semaphore(name))

        def dram(name, shape):
            return nc.dram_tensor(name, shape, F32, kind="Internal").ap()

        table = dram("table", (N, D))
        qtable = dram("qtable", (N + WIN, D))
        degs = dram("degs", (1, N))
        table_rows = table.rearrange("(p j) f -> p (j f)", j=NJ)
        q_rows = qtable[0:N, :].rearrange("(p j) f -> p (j f)", j=NJ)
        x_node_rows = t["x"].rearrange("(p j) f -> p (j f)", j=NJ)
        out_rows = out.rearrange("(p j) f -> p (j f)", j=NJ)

        X = sb("X", [P, NJ * D])
        AGG = sb("AGG", [D + 1, N + WIN])
        HT = sb("HT", [D + 1, N])
        SRC = sb("SRC", [P, GROUPS * TPG], I32)
        REL = sb("REL", [P, GROUPS * TPG])
        G = sb("G", [P, 2, TPG, D + 1])
        IDX = sb("IDX", [P, 2, TPG], I32)
        QW = sb("QW", [P, 2, D])
        work = sb("work", [P, 8840])
        CW = CH * D
        XC = work[:, 0:CW]
        SQ = work[:, CW:2 * CW]
        H = [work[:, (2 + k) * CW:(3 + k) * CW] for k in range(2)]
        SW = CH * NP
        AGS = [work[0:D + 1, 4 * CW + k * SW:4 * CW + (k + 1) * SW] for k in range(2)]
        HTS = [work[0:D + 1, 4 * CW + (2 + k) * SW:4 * CW + (3 + k) * SW] for k in range(2)]
        QB = G[:, :, :, :].rearrange("p k i f -> p (k i f)")[:, 0:CW]
        OH = [work[:, k * TPG * WIN:(k + 1) * TPG * WIN].rearrange("p (i w) -> p i w", i=TPG) for k in range(2)]
        ATTR = [work[:, 2048 + k * TPG * D:2048 + (k + 1) * TPG * D] for k in range(2)]
        OHT = work[:, 3584:3584 + GE]
        MSG = work[:, 4608:4608 + TPG * D].rearrange("p (i f) -> p i f", i=TPG)
        PRE = work[:, 5376:5376 + TPG * D].rearrange("p (i f) -> p i f", i=TPG)
        RT = work[0:D + 1, 4 * CW + 2 * SW:4 * CW + 2 * SW + GE]
        DSTI = work[:, 0:GROUPS * TPG].bitcast(I32)
        XTAB = work[:, 1600:1600 + 3 * GROUPS].rearrange("p (c g) -> p c g", c=3)
        XEQ = work[:, 2200:2200 + GROUPS]
        XM = work[:, 2400:2400 + GROUPS]
        XD = work[:, 2600:2600 + 4 * P].rearrange("p (c k) -> p c k", c=4)
        WR = work[:, 4 * CW:4 * CW + 11 * D].rearrange("p (c f) -> p c f", c=11)
        WTR = work[:, 4 * CW + 11 * D:4 * CW + 11 * D + 4 * P].rearrange("p (c k) -> p c k", c=4)
        IOI = work[:, 3200:3200 + GROUPS + 1].bitcast(I32)

        small = sb("small", [P, 2 * CH * 4])
        st = [small[:, c * 2 * CH:(c + 1) * 2 * CH] for c in range(4)]
        ident = sb("ident", [P, P])
        ones = sb("ones", [P, P])
        IOF = sb("IOF", [P, GROUPS])
        PCOL = sb("PCOL", [P, 1])
        SHIFT = sb("SHIFT", [P, P])
        XREL = sb("XREL", [P, TPG])
        col = sb("col", [P, 12])
        rowf = sb("rowf", [1, 4 * GROUPS])
        rowi = sb("rowi", [1, 2 * GROUPS], I32)
        XI = sb("XI", [1, 3 * P], I32)
        NX = sb("NX", [1, 1], I32)
        DEG = sb("DEG", [P, NJ])
        DINV = sb("DINV", [P, NJ])
        RDEG = sb("RDEG", [P, NJ])
        epsc = sb("epsc", [P, 1])
        zcol = sb("zcol", [P, 1])
        W = sb("W", [P, 18 * D])
        BASE_I, LAST_I = rowi[:, 0:GROUPS], rowi[:, GROUPS:2 * GROUPS]
        C_ROW, CX_ROW, BASE_F, NE_ROW = (rowf[:, k * GROUPS:(k + 1) * GROUPS] for k in range(4))

        def wt(k, rows=D + 1, n=1):
            return W[0:rows, k * D:(k + n) * D]

        w_self, w_nb = [wt(0), wt(1)], [wt(2), wt(3)]
        w_l1 = wt(4)
        w_l2 = [wt(5, D), wt(6, D), wt(7, D)]
        w_m1 = wt(8, D, 2)
        w_m2 = wt(10)
        w_u1 = [wt(11, D), wt(12, D)]
        w_u2 = wt(13)
        b_l2 = [wt(14 + k, P) for k in range(3)]
        bcols = sb("bcols", [D, 2])

        PS = ctx.enter_context(nc.psum_tensor("PS", [P, 8, 512], F32))

        s_edges = sem("s_edges")
        s_rows = sem("s_rows")
        s_x = sem("s_x")
        s_w = sem("s_w")
        s_const = sem("s_const")
        s_iof = sem("s_iof")
        s_dv = sem("s_dv")
        s_pe = sem("s_pe")
        s_ready = sem("s_ready")
        s_degd = sem("s_degd")
        s_degl = sem("s_degl")
        s_rt = sem("s_rt")
        n_chain = sem("n_chain")
        n_ags = sem("n_ags")
        n_cleared = sem("n_cleared")
        n_hts = sem("n_hts")
        n_out = sem("n_out")
        n_read = sem("n_read")
        n_xc = sem("n_xc")
        n_sq = sem("n_sq")
        n_var = sem("n_var")
        n_sd = sem("n_sd")
        n_h = sem("n_h")
        n_tr = sem("n_tr")
        n_ev = sem("n_ev")
        n_st = sem("n_st")
        n_pq = sem("n_pq")
        n_pqc = sem("n_pqc")
        n_hid = sem("n_hid")
        n_rel = sem("n_rel")
        s_store = sem("s_store")
        a_idx = sem("a_idx")
        a_rows = [[sem(f"a_rows{s}{k}") for k in range(2)] for s in range(2)]
        a_oh = sem("a_oh")
        a_sum = sem("a_sum")
        a_acc = sem("a_acc")
        e_attr = [sem(f"e_attr{k}") for k in range(2)]
        e_q = [sem(f"e_q{k}") for k in range(2)]
        e_turn = sem("e_turn")
        e_oht = sem("e_oht")
        e_q2e = sem("e_q2e")
        e_add = sem("e_add")
        e_pre = sem("e_pre")
        e_rel = sem("e_rel")
        e_out = sem("e_out")
        e_msg = sem("e_msg")
        x_rows = [sem("x_rows0"), sem("x_rows1")]
        x_idx, x_sub, x_oh, x_sum, x_acc = (
            sem(n) for n in ("x_idx", "x_sub", "x_oh", "x_sum", "x_acc"))
        x_ld, x_turn, x_oht, x_q2e, x_add, x_pre, x_rel, x_out, x_msg = (
            sem(n) for n in ("x_ld", "x_turn", "x_oht", "x_q2e", "x_add", "x_pre", "x_rel", "x_out", "x_msg"))

        TURN_B, Q_B, PRE_B, OUT_B = (0, 4), (2, 3), (5, 6), (1, 7)
        EWIN = PS[0:D, OUT_B[0], 4 * D:4 * D + WIN]
        HE = GE // 2

        PHASES = ["in", "l0a", "l0b", "l1", "l2a", "l2b", "l2c"]
        NCH = NJ // CH
        NONE = "the tables are built on the chip from destinations in range"

        def cols(view, j0, n=CH):
            return view[:, 0:N].rearrange("f (p j) -> f j p", j=NJ)[:, bass.ds(j0, n), :]

        def xchunk(c):
            return X[0:NP, bass.ds(c * CW, CW)]

        def c3(ap):
            return ap[0:NP, :].rearrange("p (j f) -> p j f", f=D)

        def banks(b):
            return PS[0:NP, b:b + 2, 0:5 * D].rearrange("p b (j f) -> p b j f", f=D)

        def c4(ap):
            return ap[0:NP, :].rearrange("p (b j f) -> p b j f", b=2, f=D)

        def per_block(v):
            return v.rearrange("p (b j) -> p b j", b=2).unsqueeze(3).to_broadcast([NP, 2, 5, D])

        def per_block3(v):
            return v.unsqueeze(2).to_broadcast([NP, CH, D])

        def load(eng, etype, ap, hi):
            return nc.values_load(ap, engines=[etype], min_val=0, max_val=hi,
                                  skip_runtime_bounds_check_because=NONE)

        block = ctx.enter_context(nc.Block())
        ET = mybir.EngineType

        @block.sync
        def _(sp):
            for name, dst in (("src", SRC[:, :]), ("dst", DSTI)):
                sp.dma_start(dst[:, 0:(GROUPS - 1) * TPG].rearrange("p (g i) -> p g i", i=TPG),
                             t[name][0:(GROUPS - 1) * GE].rearrange("(g p i) -> p g i", p=P, i=TPG)
                             ).then_inc(s_edges, 16)
                sp.dma_start(dst[:, (GROUPS - 1) * TPG:GROUPS * TPG],
                             t[name][LAST:E].rearrange("(p i) -> p i", i=TPG)).then_inc(s_edges, 16)
            d2 = t["dst"][0:(GROUPS - 1) * GE].rearrange("(a g k) -> a g k", a=1, k=GE)
            sp.dma_start(BASE_I[:, 0:GROUPS - 1], d2[:, :, 0], allow_slow_non_contiguous=True).then_inc(s_rows, 16)
            sp.dma_start(LAST_I[:, 0:GROUPS - 1], d2[:, :, GE - 1], allow_slow_non_contiguous=True).then_inc(s_rows, 16)
            first = (GROUPS - 1) * GE
            sp.dma_start(BASE_I[:, GROUPS - 1:GROUPS], t["dst"][first:first + 1].rearrange("(a k) -> a k", a=1)
                         ).then_inc(s_rows, 16)
            sp.dma_start(LAST_I[:, GROUPS - 1:GROUPS], t["dst"][E - 1:E].rearrange("(a k) -> a k", a=1)
                         ).then_inc(s_rows, 16)
            sp.dma_start(X[0:NP, :], x_node_rows).then_inc(s_x, 16)
            row = lambda ap: ap.rearrange("(a f) -> a f", a=1)
            for l in range(2):
                sp.dma_start(WR[0:D, l, :], t["L0_gnn_W1"][l]).then_inc(s_w, 16)
                sp.dma_start(WR[D:D + 1, l, :], t["L0_gnn_b1"][l:l + 1, :]).then_inc(s_w, 16)
                sp.dma_start(WR[0:D, 2 + l, :], t["L0_gnn_W0"][l]).then_inc(s_w, 16)
                sp.dma_start(WR[D:D + 1, 2 + l, :], t["L0_gnn_b0"][l:l + 1, :]).then_inc(s_w, 16)
                sp.dma_start(WR[0:D, 4 + l, :], t["L0_gnn_W2"][l, 0:D, :]).then_inc(s_w, 16)
                sp.dma_start(WR[0:D, 6 + l, :], t["L0_gnn_W2"][l, D:2 * D, :]).then_inc(s_w, 16)
                sp.dma_start(WR[D:D + 1, 8 + l, :], t["L0_gnn_b2"][l:l + 1, :]).then_inc(s_w, 16)
            for dst, src in ((w_l1[0:D], t["L1_gnn_W"]), (w_l1[D:D + 1], row(t["L1_gnn_b"])),
                             (w_l2[0], t["L2_gnn_W1"]), (w_l2[1], t["L2_gnn_W2"]), (w_l2[2], t["L2_gnn_W3"]),
                             (w_m1[:, 0:D], t["L3_gnn_Wm1"][0:D, :]), (w_m1[:, D:2 * D], t["L3_gnn_Wm1"][D:2 * D, :]),
                             (w_m2[0:D], t["L3_gnn_Wm2"]), (w_m2[D:D + 1], row(t["L3_gnn_bm2"])),
                             (w_u1[0], t["L3_gnn_Wu1"][0:D, :]), (w_u1[1], t["L3_gnn_Wu1"][D:2 * D, :]),
                             (w_u2[0:D], t["L3_gnn_Wu2"]), (w_u2[D:D + 1], row(t["L3_gnn_bu2"])),
                             (bcols[:, 0:1], t["L3_gnn_bm1"].rearrange("(f a) -> f a", a=1)),
                             (bcols[:, 1:2], t["L3_gnn_bu1"].rearrange("(f a) -> f a", a=1))):
                sp.dma_start(dst, src).then_inc(s_w, 16)
            for k, name in enumerate(("L2_gnn_b1", "L2_gnn_b2", "L2_gnn_b3")):
                sp.dma_start(b_l2[k], row(t[name]).to_broadcast([P, D])).then_inc(s_w, 16)

            def node_stores(phase):
                b = phase * NCH
                with sp.Fori(0, PAIRS) as i:
                    for k in range(2):
                        c = i * 2 + k
                        sp.wait_ge(n_h, c + (b + 1))
                        sp.dma_start(table_rows[:, bass.ds(c * CW, CW)], H[k][0:NP, :]).then_inc(s_store, 16)
                        sp.wait_ge(s_store, c * 16 + (b * 16 + 16))
                        sp.sem_inc(n_st, 1)

            sp.sem_inc(n_st, 2)
            node_stores(0)
            sp.wait_ge(s_ready, 1)
            n_extra = load(sp, ET.SP, NX[0:1, 0:1], EXTRA)
            sp.wait_ge(a_acc, 2 + GROUPS)
            with sp.If(n_extra > 0):
                sp.wait_ge(x_acc, 1 + EXTRA)
            sp.dma_start(degs, AGG[D:D + 1, 0:N]).then_inc(s_degd, 16)
            sp.wait_ge(s_degd, 16)
            sp.dma_start(DEG[0:NP, :], degs.rearrange("a (p j) -> (a p) j", j=NJ)).then_inc(s_degl, 16)
            for phase in range(1, 6):
                node_stores(phase)
            with sp.Fori(0, PAIRS) as i:
                for k in range(2):
                    c = i * 2 + k
                    sp.wait_ge(n_pqc, c + 3)
                    sp.dma_start(table_rows[:, bass.ds(c * CW, CW)], H[k][0:NP, :]).then_inc(s_store, 16)
                    sp.dma_start(q_rows[:, bass.ds(c * CW, CW)], QB[0:NP, :]).then_inc(s_store, 16)
                    sp.wait_ge(s_store, c * 32 + (6 * NCH * 16 + 32))
                    sp.sem_inc(n_st, 1)
            sp.wait_ge(s_const, 1)
            sp.dma_start(qtable[N:N + WIN, :], QW[:, 1, :]).then_inc(s_x, 16)
            sp.wait_ge(s_x, 32)

            def attributes(row):
                return t["edge_attr_96"][bass.ds(row, GE), :].rearrange("(p i) f -> p (i f)", i=TPG)

            def edge_loads(g, row, k):
                sp.wait_ge(a_sum, g + (6 * GROUPS + 1))
                base = load(sp, ET.SP, BASE_I[0:1, bass.ds(g, 1)], N - 1)
                sp.dma_start(ATTR[k], attributes(row)).then_inc(e_attr[k], 16)
                sp.dma_start(QW[:, k, :], qtable[bass.ds(base, WIN), :]).then_inc(e_q[k], 16)

            with sp.Fori(0, GROUPS // 2 - 1) as i:
                for k in range(2):
                    edge_loads(i * 2 + k, (i * 2 + k) * GE, k)
            edge_loads(GROUPS - 2, (GROUPS - 2) * GE, 0)
            edge_loads(GROUPS - 1, LAST, 1)
            with sp.If(n_extra > 0):
                sp.wait_ge(a_acc, 2 + 7 * GROUPS)
                with sp.Fori(0, EXTRA) as j:
                    sp.wait_ge(x_acc, j + (6 * EXTRA + 1))
                    base = load(sp, ET.SP, XI[0:1, bass.ds(j + P, 1)], N - 1)
                    row = load(sp, ET.SP, XI[0:1, bass.ds(j + 2 * P, 1)], LAST)
                    sp.dma_start(ATTR[0], attributes(row)).then_inc(x_ld, 16)
                    sp.dma_start(QW[:, 0, :], qtable[bass.ds(base, WIN), :]).then_inc(x_ld, 16)
            with sp.Fori(0, PAIRS) as i:
                for k in range(2):
                    c = i * 2 + k
                    sp.wait_ge(n_h, c + (7 * NCH + 1))
                    sp.dma_start(out_rows[:, bass.ds(c * CW, CW)], H[k][0:NP, :]).then_inc(s_store, 16)
                    sp.wait_ge(s_store, c * 16 + (8 * NCH * 16 + 16))
                    sp.sem_inc(n_st, 1)

        @block.gpsimd
        def _(pool):
            pool.memset(QW[:, :, :], 0.0).then_inc(s_const, 1)
            pool.memset(AGG[:, :], 0.0).then_inc(s_const, 1)
            pool.memset(G[:, :, :, D:D + 1], 1.0).then_inc(s_const, 1)
            pool.wait_ge(s_const, 3)
            pool.memset(HT[D:D + 1, :], 1.0).then_inc(s_const, 1)
            pool.wait_ge(s_const, 4)
            pool.memset(ones[:, :], 1.0).then_inc(s_const, 1)
            pool.memset(epsc[:, :], EPS).then_inc(s_const, 1)
            pool.memset(zcol[:, :], 0.0).then_inc(s_const, 1)
            pool.iota(IOI[:, 0:GROUPS], pattern=[[1, GROUPS]], base=0, channel_multiplier=0).then_inc(s_const, 1)
            pool.iota(IOI[:, GROUPS:GROUPS + 1], pattern=[[1, 1]], base=0, channel_multiplier=1).then_inc(s_const, 1)
            pool.memset(ident[:, :], 0.0).then_inc(s_const, 1)
            pool.wait_ge(s_const, 10)
            pool.affine_select(out=ident[:, :], in_=ident[:, :], compare_op=ALU.not_equal, fill=1.0,
                               base=0, pattern=[[-1, P]], channel_multiplier=1).then_inc(s_const, 1)
            pool.wait_ge(s_ready, 1)
            n_extra = load(pool, ET.Pool, NX[0:1, 0:1], EXTRA)

            def gathers(k, done):
                for i in range(TPG):
                    pool.indirect_dma_start(G[:, k, i, 0:D], None, table,
                                            bass.IndirectOffsetOnAxis(ap=IDX[:, k, i:i + 1], axis=0)
                                            ).then_inc(done, 16)

            def aggregation(a):
                pool.wait_ge(n_st, 2 + (a + 1) * NCH)
                pool.nop(nofuse=True)
                with pool.Fori(0, GROUPS // 2) as i:
                    for k in range(2):
                        g = i * 2 + k
                        pool.wait_ge(a_idx, g + (a * GROUPS + 1))
                        pool.nop(nofuse=True)
                        gathers(k, a_rows[a // 4][k])
                with pool.If(n_extra > 0):
                    with pool.Fori(0, EXTRA) as j:
                        pool.wait_ge(x_idx, j + (a * EXTRA + 1))
                        pool.nop(nofuse=True)
                        gathers(0, x_rows[a // 4])

            def staging(phase, clear):
                q0 = (phase - 1) * NCH
                pool.wait_ge(a_acc, 2 + phase * GROUPS)
                pool.nop(nofuse=True)
                with pool.If(n_extra > 0):
                    pool.wait_ge(x_acc, 1 + phase * EXTRA)
                    pool.nop(nofuse=True)
                if phase == 1:
                    pool.wait_ge(s_degd, 16)
                    pool.nop(nofuse=True)
                with pool.Fori(0, PAIRS) as i:
                    for k in range(2):
                        c = i * 2 + k
                        pool.wait_ge(n_out, c + (q0 + 1))
                        pool.nop(nofuse=True)
                        pool.tensor_copy(AGS[k].rearrange("f (j p) -> f j p", j=CH),
                                         cols(AGG, c * CH)).then_inc(n_ags, 1)
                        if clear:
                            pool.wait_ge(n_ags, c + (q0 + 1))
                            pool.nop(nofuse=True)
                            pool.tensor_copy(cols(AGG, c * CH), zcol[0:D + 1, 0:1].unsqueeze(2).to_broadcast([D + 1, CH, NP])
                                             ).then_inc(n_cleared, 1)

            for a in range(7):
                aggregation(a)
                if a < 6:
                    staging(a + 1, clear=PHASES[a + 1] in ("l0a", "l0b", "l2c"))

        @block.scalar
        def _(act):
            act.sem_inc(n_ev, 1)
            act.sem_inc(n_rel, 1)
            act.wait_ge(s_const, 11)
            n_extra = None
            count = {"xc": 0, "ev": 0, "hts": 0}

            def node(phase):
                name = PHASES[phase]
                stats = {"in": 1, "l0a": 1, "l0b": 2, "l1": 1, "l2a": 0, "l2b": 0, "l2c": 1}[name]
                turn = name != "l0b"
                xc0, ev0, hts0, q0 = count["xc"], count["ev"], count["hts"], (phase - 1) * NCH

                def stage(c, k):
                    act.wait_ge(n_out, c + (q0 + 1))
                    act.wait_ge(n_ev, 1 + ev0)
                    act.nop(nofuse=True)
                    act.activation(HTS[k].rearrange("f (j p) -> f j p", j=CH), cols(HT, c * CH), ACT.Copy).then_inc(n_hts, 1)

                def step(c, k):
                    for s in range(stats):
                        v = c * stats + (xc0 + s + 1)
                        act.wait_ge(n_xc, v)
                        act.activation(SQ[0:NP, :], XC[0:NP, :], ACT.Square).then_inc(n_sq, 1)
                        act.wait_ge(n_var, v)
                        if name == "l0a" or (name == "l0b" and s == 0):
                            act.activation(st[2][0:NP, 0:CH], st[1][0:NP, 0:CH], ACT.Sqrt, bias=0.0,
                                           scale=1.0 / (D - 1)).then_inc(n_sd, 1)
                        else:
                            act.activation(st[2][0:NP, 0:CH], st[1][0:NP, 0:CH], ACT.Sqrt, bias=epsc[0:NP, 0:1],
                                           scale=1.0 / D).then_inc(n_sd, 1)
                    if turn:
                        act.wait_ge(n_tr, c + (ev0 + 3))
                        if name == "l2c":
                            hs = HTS[k][0:D, :].rearrange("f (j p) -> f j p", j=CH)
                            act.wait_ge(n_pqc, c + 1)
                            dst = [hs[:, 0:4, :], hs[:, 4:8, :], hs[:, 8:10, :]]
                        else:
                            target = HT[0:D] if name in ("in", "l0a") else AGG[0:D]
                            dst = [cols(target, c * CH + b, n) for b, n in ((0, 4), (4, 4), (8, 2))]
                        act.nop(nofuse=True)
                        for b, n in ((0, 4), (1, 4), (2, 2)):
                            last = act.activation(dst[b], PS[0:D, 4 + b, 0:n * NP].rearrange(
                                "f (j p) -> f j p", j=n), ACT.Copy)
                        last.then_inc(n_ev, 1)
                        if name == "l2c":
                            act.nop(nofuse=True)
                            for b, n in ((0, 4), (1, 4), (2, 2)):
                                last = act.activation(cols(HT[0:D], c * CH + 4 * b, n),
                                                      PS[0:D, 4 + b, 0:n * NP].rearrange("f (j p) -> f j p", j=n),
                                                      ACT.Copy)
                            last.then_inc(n_hts, 1)

                if name in ("l0a", "l0b"):
                    stage(0, 0)
                    with act.Fori(0, PAIRS - 1) as i:
                        for k in range(2):
                            stage(i * 2 + k + 1, 1 - k)
                            step(i * 2 + k, k)
                    stage(NCH - 1, 1)
                    step(NCH - 2, 0)
                    step(NCH - 1, 1)
                    count["hts"] += NCH
                else:
                    with act.Fori(0, PAIRS) as i:
                        for k in range(2):
                            step(i * 2 + k, k)
                count["xc"] += stats * NCH
                count["ev"] += NCH * turn

            def indices(a):
                with act.Fori(0, GROUPS // 2) as i:
                    for k in range(2):
                        g = i * 2 + k
                        act.wait_ge(a_sum, g + (a * GROUPS + 1))
                        act.nop(nofuse=True)
                        act.activation(IDX[:, k, :], SRC[:, bass.ds(g * TPG, TPG)], ACT.Copy).then_inc(a_idx, 1)

            def copy_turned(when, turned, done):
                act.wait_ge(turned, when)
                for b in range(2):
                    last = act.activation(OHT[:, b * HE:(b + 1) * HE], PS[:, TURN_B[b], :], ACT.Copy)
                last.then_inc(done, 1)

            def relu(v, pre, done):
                for b in range(2):
                    act.wait_ge(pre, v + (b + 1))
                    act.activation(RT[0:D, b * HE:(b + 1) * HE], PS[0:D, PRE_B[b], :], ACT.Relu,
                                   bias=bcols[:, 0:1]).then_inc(done, 1)

            def edge_network():
                def idx(g, k, used):
                    act.wait_ge(*used)
                    act.nop(nofuse=True)
                    act.activation(IDX[:, k, :], SRC[:, bass.ds(g * TPG, TPG)], ACT.Copy).then_inc(a_idx, 1)

                idx(0, 0, (a_sum, 2 + 6 * GROUPS))
                idx(1, 1, (a_sum, 2 + 6 * GROUPS))
                copy_turned(1, e_turn, e_oht)
                with act.Fori(0, GROUPS // 2 - 1) as i:
                    for k in range(2):
                        g = i * 2 + k
                        relu(g * 2, e_pre, e_rel)
                        idx(g + 2, k, (e_add, g * 2 + 2))
                        copy_turned(g + 2, e_turn, e_oht)
                relu(GROUPS * 2 - 4, e_pre, e_rel)
                copy_turned(GROUPS, e_turn, e_oht)
                relu(GROUPS * 2 - 2, e_pre, e_rel)

            def extras(a):
                with act.If(n_extra > 0):
                    act.wait_ge(a_sum, 2 + (a + 1) * GROUPS)
                    with act.Fori(0, EXTRA) as j:
                        act.wait_ge(x_acc, j + (a * EXTRA + 1))
                        g = load(act, ET.Activation, XI[0:1, bass.ds(j, 1)], GROUPS - 1)
                        act.nop(nofuse=True)
                        act.activation(IDX[:, 0, :], SRC[:, bass.ds(g * TPG, TPG)], ACT.Copy).then_inc(x_idx, 1)
                        if a == 6:
                            copy_turned(j + 1, x_turn, x_oht)
                            relu(j * 2, x_pre, x_rel)

            node(0)
            act.wait_ge(s_ready, 1)
            n_extra = load(act, ET.Activation, NX[0:1, 0:1], EXTRA)
            for a in range(6):
                indices(a)
                extras(a)
                if a == 0:
                    act.wait_ge(s_dv, DEGREES)
                    act.activation(DINV[0:NP, :], DEG[0:NP, :], ACT.Sqrt).then_inc(s_rt, 1)
                node(a + 1)
            edge_network()
            extras(6)
            act.wait_ge(s_w, 16 * 32)
            with act.Fori(0, PAIRS) as i:
                for k in range(2):
                    c = i * 2 + k
                    act.wait_ge(n_hid, c + 1)
                    act.wait_ge(n_out, c + (6 * NCH + 1))
                    act.nop(nofuse=True)
                    for b, n in ((0, 4), (1, 4), (2, 2)):
                        last = act.activation(HTS[k][0:D, 4 * b * NP:(4 * b + n) * NP], PS[0:D, 4 + b, 0:n * NP],
                                              ACT.Relu, bias=bcols[:, 1:2])
                    last.then_inc(n_rel, 1)

        @block.vector
        def _(dve):
            dve.sem_inc(n_read, 2)
            dve.sem_inc(a_acc, 2)
            dve.sem_inc(x_acc, 1)
            dve.sem_inc(n_pqc, 2)
            steps = [0]

            def link(ins):
                steps[0] += 1
                ins.then_inc(s_dv, 1)
                dve.wait_ge(s_dv, steps[0])

            dve.wait_ge(s_const, 11)
            link(dve.tensor_copy(IOF[:, :], IOI[:, 0:GROUPS]))
            link(dve.tensor_copy(PCOL[:, :], IOI[:, GROUPS:GROUPS + 1]))
            dve.wait_ge(s_edges, 64)
            dve.wait_ge(s_rows, 64)
            link(dve.tensor_copy(REL[:, :], DSTI))
            link(dve.tensor_copy(BASE_F, BASE_I))
            link(dve.tensor_tensor(LAST_I, LAST_I, BASE_I, ALU.subtract))
            link(dve.tensor_scalar(LAST_I, LAST_I, WIN.bit_length() - 1, None, ALU.arith_shift_right))
            link(dve.tensor_copy(NE_ROW, LAST_I))
            link(dve.tensor_tensor_scan(C_ROW, ones[0:1, 0:1].to_broadcast([1, GROUPS]), NE_ROW, 0.0,
                                        ALU.mult, ALU.add))
            link(dve.tensor_tensor(CX_ROW, C_ROW, NE_ROW, ALU.subtract))
            link(dve.tensor_copy(NX[0:1, 0:1], C_ROW[:, GROUPS - 1:GROUPS]))
            assert steps[0] == SETUP_ROWS
            dve.wait_ge(s_pe, 1)
            link(dve.tensor_copy(XTAB[:, 0:2, :], PS[:, 0, 0:2 * GROUPS].rearrange("p (c g) -> p c g", c=2)))
            link(dve.tensor_copy(XTAB[:, 2, :], PS[:, 1, 0:GROUPS]))
            link(dve.tensor_tensor(REL[:, :].rearrange("p (g i) -> p g i", i=TPG),
                                   REL[:, :].rearrange("p (g i) -> p g i", i=TPG),
                                   XTAB[:, 2, :].unsqueeze(2).to_broadcast([P, GROUPS, TPG]), ALU.subtract))
            link(dve.memset(REL[0:MASKED, (GROUPS - 1) * TPG:GROUPS * TPG], FAR))
            gj, cx, gb, used, shift = (col[:, k:k + 1] for k in range(5))
            four = [col[:, 8 + k:9 + k] for k in range(4)]
            link(dve.tensor_scalar(XEQ, XTAB[:, 0, :], PCOL[:, 0:1], None, ALU.is_le))
            link(dve.reduce_sum(gj, XEQ, AX))
            link(dve.tensor_scalar(XEQ, IOF[:, :], gj, None, ALU.is_equal))
            link(dve.tensor_tensor(XM, XEQ, XTAB[:, 1, :], ALU.mult))
            link(dve.reduce_sum(cx, XM, AX))
            link(dve.tensor_tensor(XM, XEQ, XTAB[:, 2, :], ALU.mult))
            link(dve.reduce_sum(gb, XM, AX))
            link(dve.tensor_tensor(used, PCOL[:, 0:1], XTAB[:, 0, GROUPS - 1:GROUPS], ALU.is_lt))
            link(dve.tensor_tensor(shift, PCOL[:, 0:1], cx, ALU.subtract))
            link(dve.tensor_scalar(shift, shift, 1.0, float(WIN), ALU.add, ALU.mult))
            link(dve.tensor_scalar(four[0], gj, float(GROUPS - 1), None, ALU.min))
            link(dve.tensor_tensor(gb, gb, shift, ALU.add))
            link(dve.tensor_tensor(four[1], gb, used, ALU.mult))
            link(dve.tensor_scalar(four[2], four[0], float(GE), float(LAST), ALU.mult, ALU.min))
            link(dve.tensor_scalar(used, used, -1.0, FAR, ALU.add, ALU.mult))
            link(dve.tensor_tensor(four[3], shift, used, ALU.add))
            for k in range(4):
                link(dve.tensor_scalar(XD[:, k, :], ident[:, :], four[k], None, ALU.mult))
            assert steps[0] == SETUP_EXTRA
            dve.wait_ge(s_pe, 2)
            link(dve.tensor_copy(XI[0:1, :], PS[0:1, 2, 0:3 * P]))
            link(dve.tensor_copy(SHIFT[:, :], PS[:, 2, 3 * P:4 * P]))
            dve.wait_ge(s_pe, 3)
            link(dve.tensor_copy(WTR[0:D, :, 0:D + 1], PS[0:D, 3, 0:4 * P].rearrange("f (c k) -> f c k", c=4)[:, :, 0:D + 1]))
            assert steps[0] == SETUP_TURNED
            dve.wait_ge(s_pe, 4)
            for l in range(2):
                link(dve.tensor_copy(w_self[l], PS[0:D + 1, 4, l * D:(l + 1) * D]))
                link(dve.tensor_tensor(w_self[l][D:D + 1, :], w_self[l][D:D + 1, :], WR[D:D + 1, 8 + l, :], ALU.add))
                link(dve.tensor_copy(w_nb[l], PS[0:D + 1, 4, (2 + l) * D:(3 + l) * D]))
            dve.sem_inc(s_ready, 1)

            count = {"chain": 0, "xc": 0, "tr": 0}

            def node(phase):
                name = PHASES[phase] if phase < 7 else "fin"
                ch0, xc0, tr0 = count["chain"], count["xc"], count["tr"]
                q0, h0 = (phase - 1) * NCH, phase * NCH
                stats_n = {"in": 1, "l0a": 1, "l0b": 2, "l1": 1, "l2a": 0, "l2b": 0, "l2c": 1, "fin": 0}[name]
                turn = name not in ("l0b", "fin")
                if name == "in":
                    dve.wait_ge(s_x, 16)

                chain_n = {"in": 3, "l0a": 3, "l0b": 7, "l1": 5, "l2a": 1, "l2b": 1, "l2c": 6, "fin": 0}[name]

                def chunk(c, k):
                    n = [0, 0]

                    def then(ins):
                        n[0] += 1
                        ins.then_inc(n_chain, 1)
                        dve.wait_ge(n_chain, c * chain_n + (ch0 + n[0]))

                    def stats(src, view):
                        n[1] += 1
                        v = c * stats_n + (xc0 + n[1])
                        mean = st[0][0:NP, 0:CH]
                        if view == 4:
                            then(dve.reduce_sum(mean.rearrange("p (b j) -> p b j", b=2), src, AX))
                        else:
                            dve.nop(nofuse=True)
                            then(dve.reduce_sum(mean, src, AX))
                        then(dve.tensor_scalar(mean, mean, -1.0 / D, None, ALU.mult))
                        if view == 4:
                            dve.tensor_tensor(c4(XC), src, per_block(mean), ALU.add).then_inc(n_xc, 1)
                        else:
                            dve.tensor_tensor(c3(XC), src, per_block3(mean), ALU.add).then_inc(n_xc, 1)
                        dve.wait_ge(n_sq, v)
                        dve.reduce_sum(st[1][0:NP, 0:CH], c3(SQ), AX).then_inc(n_var, 1)
                        dve.wait_ge(n_sd, v)
                        then(dve.reciprocal(st[3][0:NP, 0:CH], st[2][0:NP, 0:CH]))

                    def h_free():
                        dve.wait_ge(n_st, c + (h0 + 1))
                        dve.wait_ge(n_tr, c + (tr0 + 1) if turn else tr0 + 2)

                    inv = st[3][0:NP, 0:CH]
                    xk = X[0:NP, bass.ds(c * CW, CW)]
                    dinv = DINV[0:NP, bass.ds(c * CH, CH)]
                    if name != "in":
                        dve.wait_ge(n_out, c + (q0 + 3))
                        prod = banks(2 * k)
                    if name == "l0a":
                        stats(prod, 4)
                        h_free()
                        dve.tensor_tensor(c4(H[k]), prod, per_block(inv), ALU.mult).then_inc(n_h, 1)
                        dve.wait_ge(n_h, c + (h0 + 1))
                        dve.sem_inc(n_read, 1)
                    elif name == "fin":
                        h_free()
                        dve.tensor_tensor(c4(H[k]), xk.rearrange("p (b j f) -> p b j f", b=2, f=D), prod,
                                          ALU.add).then_inc(n_h, 1)
                        dve.wait_ge(n_h, c + (h0 + 1))
                        dve.sem_inc(n_read, 1)
                    else:
                        if name == "l0b":
                            stats(prod, 4)
                            dve.tensor_tensor(c4(XC), prod, per_block(inv), ALU.mult).then_inc(n_read, 1)
                        elif name == "l1":
                            dve.tensor_tensor(c4(XC), prod, per_block(RDEG[0:NP, bass.ds(c * CH, CH)]),
                                              ALU.mult).then_inc(n_read, 1)
                        elif name != "in":
                            dve.tensor_tensor(c4(XC), prod, per_block(dinv), ALU.mult).then_inc(n_read, 1)
                        if name != "in":
                            dve.wait_ge(n_read, c + (q0 + 3))
                        if name in ("l2a", "l2b", "l2c"):
                            bias = b_l2[("l2a", "l2b", "l2c").index(name)][0:NP, :]
                            then(dve.tensor_tensor(c3(XC), c3(XC), bias.unsqueeze(1).to_broadcast([NP, CH, D]),
                                                   ALU.add))
                        if name in ("l0b", "l1", "l2c"):
                            then(dve.tensor_tensor(xk, xk, XC[0:NP, :], ALU.add))
                        if name in ("l2a", "l2b"):
                            scale = dinv
                        else:
                            stats(xk.rearrange("p (j f) -> p j f", f=D), 3)
                            if name == "l1":
                                then(dve.tensor_tensor(inv, inv, dinv, ALU.mult))
                            scale = inv
                        h_free()
                        dve.scalar_tensor_tensor(out=c3(H[k]), in0=c3(XC), scalar=0.0, in1=per_block3(scale),
                                                 op0=ALU.max, op1=ALU.mult).then_inc(n_h, 1)
                        dve.wait_ge(n_h, c + (h0 + 1))
                        if name == "l2c":
                            dve.wait_ge(n_pq, c + 1)
                            dve.wait_ge(n_st, c + (h0 + 2))
                            then(dve.tensor_copy(c4(H[k]), banks(2 * k)))
                            dve.tensor_copy(c4(QB), banks(4)).then_inc(n_pqc, 1)
                    assert n[0] == chain_n, (name, n[0])

                with dve.Fori(0, PAIRS) as i:
                    for k in range(2):
                        chunk(i * 2 + k, k)
                count["chain"] += chain_n * NCH
                count["xc"] += stats_n * NCH
                count["tr"] += turn * NCH

            def one_hot(dst, rel):
                return dve.tensor_tensor(dst, IOF[:, 0:WIN].unsqueeze(1).to_broadcast([P, TPG, WIN]),
                                         rel.unsqueeze(2).to_broadcast([P, TPG, WIN]), ALU.is_equal)

            def accumulate(rows, base, sums):
                window = AGG[0:rows, bass.ds(base, WIN)]
                return dve.tensor_tensor(window, window, sums, ALU.add)

            def hidden_sum(k, v, q2e, done):
                for b in range(2):
                    dve.wait_ge(q2e, v + (b + 1))
                    dve.tensor_tensor(PRE[:, 4 * b:4 * b + 4, :],
                                      PS[:, Q_B[b], 0:4 * D].rearrange("p (i f) -> p i f", f=D),
                                      G[:, k, 4 * b:4 * b + 4, 0:D], ALU.add).then_inc(done, 1)

            def messages(k, v, outs, done):
                for b in range(2):
                    dve.wait_ge(outs, v + (b + 1))
                    dve.tensor_tensor(MSG[:, 4 * b:4 * b + 4, :],
                                      PS[:, OUT_B[b], 0:4 * D].rearrange("p (i f) -> p i f", f=D),
                                      ATTR[k][:, 4 * b * D:4 * (b + 1) * D].rearrange("p (i f) -> p i f", f=D),
                                      ALU.mult).then_inc(done, 1)

            def aggregation(a):
                g0, rows, net = a * GROUPS, D + 1 if a < 6 else D, a == 6
                dve.wait_ge(n_st, 2 + (a + 1) * NCH)
                dve.wait_ge(n_tr, 2 + count["tr"])
                dve.wait_ge(n_ev, 1 + count["tr"])
                if a:
                    dve.wait_ge(n_cleared, {1: 1, 2: 2, 6: 3}.get(a, 2) * NCH)

                def make(g, k):
                    dve.wait_ge(a_sum, g + (g0 + 1))
                    one_hot(OH[k], REL[:, bass.ds(g * TPG, TPG)]).then_inc(a_oh, 1)

                def add(g, k):
                    base = load(dve, ET.DVE, BASE_I[0:1, bass.ds(g, 1)], N - 1)
                    dve.wait_ge(a_sum, g + (g0 + 3))
                    dve.wait_ge(a_acc, g + (g0 + 2))
                    accumulate(rows, base, EWIN if net else PS[0:rows, k, 0:WIN]).then_inc(a_acc, 1)

                if not net:
                    make(0, 0)
                    with dve.Fori(0, GROUPS // 2 - 1) as i:
                        for k in range(2):
                            make(i * 2 + k + 1, 1 - k)
                            add(i * 2 + k, k)
                    make(GROUPS - 1, 1)
                    add(GROUPS - 2, 0)
                    add(GROUPS - 1, 1)
                else:
                    def hidden(g, k, pair):
                        dve.wait_ge(a_rows[1][k], pair * (16 * TPG) + (2 * GROUPS // 2 + 1) * 16 * TPG)
                        hidden_sum(k, g * 2, e_q2e, e_add)

                    def message(g, k, pair):
                        dve.wait_ge(e_attr[k], pair * 16 + 16)
                        messages(k, g * 2, e_out, e_msg)

                    make(0, 0)
                    make(1, 1)
                    hidden(0, 0, 0)
                    with dve.Fori(0, GROUPS // 2 - 1) as i:
                        for k in range(2):
                            g = i * 2 + k
                            message(g, k, i)
                            hidden(g + 1, 1 - k, i + k)
                            add(g, k)
                            make(g + 2, k)
                    message(GROUPS - 2, 0, GROUPS // 2 - 1)
                    hidden(GROUPS - 1, 1, GROUPS // 2 - 1)
                    add(GROUPS - 2, 0)
                    message(GROUPS - 1, 1, GROUPS // 2 - 1)
                    add(GROUPS - 1, 1)
                with dve.If(n_extra > 0):
                    with dve.Fori(0, EXTRA) as j:
                        v = j + (a * EXTRA + 1)
                        g = load(dve, ET.DVE, XI[0:1, bass.ds(j, 1)], GROUPS - 1)
                        base = load(dve, ET.DVE, XI[0:1, bass.ds(j + P, 1)], N - 1)
                        dve.wait_ge(x_acc, v)
                        dve.tensor_scalar(XREL[:, :], REL[:, bass.ds(g * TPG, TPG)], SHIFT[:, bass.ds(j, 1)], None,
                                          ALU.subtract).then_inc(x_sub, 1)
                        dve.wait_ge(x_sub, v)
                        one_hot(OH[0], XREL[:, :]).then_inc(x_oh, 1)
                        if net:
                            dve.wait_ge(x_rows[1], j * (16 * TPG) + (2 * EXTRA + 1) * 16 * TPG)
                            hidden_sum(0, j * 2, x_q2e, x_add)
                            dve.wait_ge(x_ld, j * 32 + 32)
                            messages(0, j * 2, x_out, x_msg)
                        dve.wait_ge(x_sum, v)
                        accumulate(rows, base, EWIN if net else PS[0:rows, 0, 0:WIN]).then_inc(x_acc, 1)
                    dve.wait_ge(x_acc, (a + 1) * EXTRA + 1)

            node(0)
            n_extra = load(dve, ET.DVE, NX[0:1, 0:1], EXTRA)
            for a in range(6):
                aggregation(a)
                if a == 0:
                    dve.wait_ge(s_degl, 16)
                    link(dve.tensor_scalar(RDEG[0:NP, :], DEG[0:NP, :], 1.0, None, ALU.max))
                    link(dve.reciprocal(RDEG[0:NP, :], RDEG[0:NP, :]))
                    link(dve.tensor_scalar(DEG[0:NP, :], DEG[0:NP, :], 1.0, None, ALU.add))
                    assert steps[0] == DEGREES
                    dve.wait_ge(s_rt, 1)
                    link(dve.reciprocal(DINV[0:NP, :], DINV[0:NP, :]))
                if a == 3:
                    dve.wait_ge(s_w, 16 * 32)
                node(a + 1)
            aggregation(6)
            node(7)

        @block.tensor
        def _(pe):
            pe.sem_inc(n_out, 2)
            pe.sem_inc(n_tr, 2)
            pe.sem_inc(a_sum, 2)
            pe.wait_ge(s_const, 11)
            pe.wait_ge(s_dv, SETUP_ROWS)
            pe.matmul(PS[:, 0, 0:2 * GROUPS], ones[0:1, :], rowf[:, 0:2 * GROUPS], start=True, stop=True)
            pe.matmul(PS[:, 1, 0:GROUPS], ones[0:1, :], BASE_F, start=True, stop=True).then_inc(s_pe, 1)
            pe.wait_ge(s_dv, SETUP_EXTRA)
            pe.matmul(PS[:, 2, :], ones[:, :], XD, start=True, stop=True).then_inc(s_pe, 1)
            pe.wait_ge(s_w, 16 * 32)
            for m in range(4):
                last = pe.transpose(PS[0:D, 3, m * P:m * P + D + 1], WR[0:D + 1, m, :], ident[0:D + 1, 0:D + 1])
            last.then_inc(s_pe, 1)
            pe.wait_ge(s_dv, SETUP_TURNED)
            for m in range(4):
                last = pe.matmul(PS[0:D + 1, 4, m * D:(m + 1) * D], WTR[0:D, m, 0:D + 1], WR[0:D, 4 + m, :],
                                 start=True, stop=True)
            last.then_inc(s_pe, 1)
            pe.wait_ge(s_ready, 1)
            n_extra = load(pe, ET.PE, NX[0:1, 0:1], EXTRA)
            count = {"tr": 0, "hts": 0}

            def node(phase):
                name = PHASES[phase] if phase < 7 else "fin"
                q0, h0, tr0, hts0 = (phase - 1) * NCH, phase * NCH, count["tr"], count["hts"]
                turn = name not in ("l0b", "fin")

                def product(c, k):
                    if name == "fin":
                        pe.wait_ge(n_rel, c + 1)
                        for b, n in ((0, 4), (1, 4), (2, 2)):
                            o = PS[0:D, 4 + b, 0:n * NP].rearrange("f (j p) -> f j p", j=n)
                            pe.matmul(o, w_u1[0], cols(HT[0:D], c * CH + 4 * b, n), start=True, stop=False)
                            last = pe.matmul(o, w_u1[1], cols(AGG[0:D], c * CH + 4 * b, n), start=False, stop=True)
                        last.then_inc(n_hid, 1)
                        pe.wait_ge(n_rel, c + 2)
                        parts = [(HTS[k], w_u2, D + 1)]
                    else:
                        pe.wait_ge(n_ags, c + (q0 + 1))
                        if name in ("l0a", "l0b"):
                            l = name == "l0b"
                            pe.wait_ge(n_hts, c + (hts0 + 1))
                            parts = [(HTS[k], w_self[l], D + 1), (AGS[k], w_nb[l], D + 1)]
                        elif name == "l1":
                            parts = [(AGS[k], w_l1, D + 1)]
                        else:
                            parts = [(AGS[k], w_l2[("l2a", "l2b", "l2c").index(name)], D)]
                    pe.wait_ge(n_read, c + (q0 + 1))
                    if name == "l2c":
                        pe.wait_ge(n_pqc, c + 1)
                    for j in range(CH):
                        o = PS[0:NP, 2 * k + j // 5, (j % 5) * D:(j % 5 + 1) * D]
                        for m, (stage, w, rows) in enumerate(parts):
                            last = pe.matmul(o, stage[0:rows, j * NP:(j + 1) * NP], w,
                                             start=(m == 0), stop=(m == len(parts) - 1))
                    last.then_inc(n_out, 1)

                def turned(c, k):
                    pe.wait_ge(n_h, c + (h0 + 1))
                    pe.wait_ge(n_ev, c + (tr0 + 1))
                    if name == "l2c":
                        pe.wait_ge(n_pqc, c + 2)
                    for j in range(CH):
                        last = pe.transpose(PS[0:D, 4 + j // 4, (j % 4) * NP:(j % 4 + 1) * NP],
                                            H[k][0:NP, j * D:(j + 1) * D], ident[0:NP, 0:NP])
                    last.then_inc(n_tr, 1)
                    if name == "l2c":
                        pe.wait_ge(n_ev, c + (tr0 + 2))
                        pe.wait_ge(n_hts, c + (hts0 + 1))
                        for half, b0 in ((0, 2 * k), (1, 4)):
                            for j in range(CH):
                                last = pe.matmul(PS[0:NP, b0 + j // 5, (j % 5) * D:(j % 5 + 1) * D],
                                                 HTS[k][0:D, j * NP:(j + 1) * NP],
                                                 w_m1[:, half * D:(half + 1) * D], start=True, stop=True)
                        last.then_inc(n_pq, 1)

                if name == "in":
                    with pe.Fori(0, PAIRS) as i:
                        for k in range(2):
                            turned(i * 2 + k, k)
                elif not turn:
                    if name == "fin":
                        pe.wait_ge(a_acc, 2 + 7 * GROUPS)
                        with pe.If(n_extra > 0):
                            pe.wait_ge(x_acc, 1 + 7 * EXTRA)
                    with pe.Fori(0, PAIRS) as i:
                        for k in range(2):
                            product(i * 2 + k, k)
                else:
                    product(0, 0)
                    with pe.Fori(0, PAIRS - 1) as i:
                        for k in range(2):
                            product(i * 2 + k + 1, 1 - k)
                            turned(i * 2 + k, k)
                    product(NCH - 1, 1)
                    turned(NCH - 2, 0)
                    turned(NCH - 1, 1)
                count["tr"] += turn * NCH
                count["hts"] += NCH * (name in ("l0a", "l0b", "l2c"))

            def window_sums(k, done):
                for i in range(TPG):
                    last = pe.matmul(PS[0:D + 1, k, 0:WIN], G[:, k, i, :], OH[k][:, i, :],
                                     start=(i == 0), stop=(i == TPG - 1))
                last.then_inc(done, 1)

            def turn_one_hots(k, done):
                for i in range(TPG):
                    last = pe.transpose(PS[:, TURN_B[i // 4], (i % 4) * P:(i % 4 + 1) * P], OH[k][:, i, :],
                                        ident[:, :])
                last.then_inc(done, 1)

            def q_to_edges(k, done):
                for i in range(TPG):
                    last = pe.matmul(PS[:, Q_B[i // 4], (i % 4) * D:(i % 4 + 1) * D], OHT[:, i * P:(i + 1) * P],
                                     QW[:, k, :], start=True, stop=True)
                    if i % 4 == 3:
                        last.then_inc(done, 1)

            def turn_hidden(v, added, done):
                for i in range(TPG):
                    if i % 4 == 0:
                        pe.wait_ge(added, v + (i // 4 + 1))
                    last = pe.transpose(PS[0:D, PRE_B[i // 4], (i % 4) * P:(i % 4 + 1) * P], PRE[:, i, :],
                                        ident[:, :])
                    if i % 4 == 3:
                        last.then_inc(done, 1)

            def edge_out(v, rel, done):
                for b in range(2):
                    pe.wait_ge(rel, v + (b + 1))
                    for i in range(4 * b, 4 * b + 4):
                        last = pe.matmul(PS[:, OUT_B[b], (i % 4) * D:(i % 4 + 1) * D], RT[:, i * P:(i + 1) * P],
                                         w_m2, start=True, stop=True)
                    last.then_inc(done, 1)

            def message_sums(k, v, msg, done):
                for i in range(TPG):
                    if i % 4 == 0:
                        pe.wait_ge(msg, v + (i // 4 + 1))
                    last = pe.matmul(EWIN, MSG[:, i, :], OH[k][:, i, :], start=(i == 0), stop=(i == TPG - 1))
                last.then_inc(done, 1)

            def aggregation(a):
                g0 = a * GROUPS
                with pe.Fori(0, GROUPS // 2) as i:
                    for k in range(2):
                        g = i * 2 + k
                        pe.wait_ge(a_oh, g + (g0 + 1))
                        pe.wait_ge(a_rows[a // 4][k], i * (16 * TPG) + (a % 4 * GROUPS // 2 + 1) * 16 * TPG)
                        pe.wait_ge(a_acc, g + (g0 + 1))
                        window_sums(k, a_sum)
                with pe.If(n_extra > 0):
                    pe.wait_ge(a_acc, 2 + (a + 1) * GROUPS)
                    with pe.Fori(0, EXTRA) as j:
                        pe.wait_ge(x_oh, j + (a * EXTRA + 1))
                        pe.wait_ge(x_rows[a // 4], j * (16 * TPG) + (a % 4 * EXTRA + 1) * 16 * TPG)
                        window_sums(0, x_sum)

            def edge_network():
                g0 = 6 * GROUPS

                def q_part(g, k, pair):
                    pe.wait_ge(e_oht, g + 1)
                    pe.wait_ge(e_q[k], pair * 16 + 16)
                    q_to_edges(k, e_q2e)

                def group(g, k, pair, last=False):
                    turn_hidden(g * 2, e_add, e_pre)
                    if not last:
                        pe.wait_ge(a_oh, g + (g0 + 2))
                        turn_one_hots(1 - k, e_turn)
                    pe.wait_ge(a_acc, g + (g0 + 2))
                    edge_out(g * 2, e_rel, e_out)
                    if not last:
                        q_part(g + 1, 1 - k, pair + k)
                    message_sums(k, g * 2, e_msg, a_sum)

                pe.wait_ge(a_oh, g0 + 1)
                turn_one_hots(0, e_turn)
                q_part(0, 0, 0)
                with pe.Fori(0, GROUPS // 2 - 1) as i:
                    for k in range(2):
                        group(i * 2 + k, k, i)
                group(GROUPS - 2, 0, GROUPS // 2 - 1)
                group(GROUPS - 1, 1, GROUPS // 2 - 1, last=True)
                with pe.If(n_extra > 0):
                    pe.wait_ge(a_acc, 2 + 7 * GROUPS)
                    with pe.Fori(0, EXTRA) as j:
                        pe.wait_ge(x_oh, j + (6 * EXTRA + 1))
                        turn_one_hots(0, x_turn)
                        pe.wait_ge(x_oht, j + 1)
                        pe.wait_ge(x_ld, j * 32 + 32)
                        q_to_edges(0, x_q2e)
                        turn_hidden(j * 2, x_add, x_pre)
                        edge_out(j * 2, x_rel, x_out)
                        message_sums(0, j * 2, x_msg, x_sum)

            node(0)
            for a in range(6):
                aggregation(a)
                node(a + 1)
            edge_network()
            node(7)


_INS = ["x", "src", "dst", "edge_attr_96", "L0_gnn_W0", "L0_gnn_b0", "L0_gnn_W1", "L0_gnn_b1", "L0_gnn_W2",
        "L0_gnn_b2", "L1_gnn_W", "L1_gnn_b", "L2_gnn_W1", "L2_gnn_b1", "L2_gnn_W2", "L2_gnn_b2", "L2_gnn_W3",
        "L2_gnn_b3", "L3_gnn_Wm1", "L3_gnn_bm1", "L3_gnn_Wm2", "L3_gnn_bm2", "L3_gnn_Wu1", "L3_gnn_bu1",
        "L3_gnn_Wu2", "L3_gnn_bu2"]


def kernel(**inputs):
    import numpy as _np
    import concourse.bacc as _bacc
    from concourse import mybir as _mybir
    from concourse.bass_utils import run_bass_kernel_spmd as _run

    nc = _bacc.Bacc("TRN2", target_bir_lowering=False, num_devices=1)
    arrays, tensors = {}, {}
    for name in _INS:
        a = _np.ascontiguousarray(inputs[name])
        arrays[f"in_{name}_dram"] = a
        tensors[name] = nc.dram_tensor(f"in_{name}_dram", a.shape, _mybir.dt.from_np(a.dtype),
                                       kind="ExternalInput").ap()
    out = nc.dram_tensor("out_0_dram", (N, D), F32, kind="ExternalOutput").ap()
    build(nc, tensors, out)
    r = _run(nc, [arrays], core_ids=[0])
    return r.results[0]["out_0_dram"]
```

```python
from contextlib import ExitStack

import concourse.bass as bass
from concourse import mybir

F32 = mybir.dt.float32
I32 = mybir.dt.int32
I16 = mybir.dt.int16
BF16 = mybir.dt.bfloat16
ALU = mybir.AluOpType
ACT = mybir.ActivationFunctionType
AX = mybir.AxisListType.X

N, D = 12500, 96
E = 200000
NP, NJ = 125, 100
CH = 10
PAIRS = NJ // CH // 2
P = 128
TPG = 8
GE = P * TPG
GROUPS = -(-E // GE)
LAST = E - GE
MASKED = (GROUPS * GE - E) // TPG
WIN = 128
EXTRA = (N - 1) // WIN
DG = GROUPS // 2
DT = DG * TPG
DB = 50
MB, MR = 7, DT // 7
AC = 5
ACW = NJ // AC * WIN
KW = GE + 2 * P
FAR = -1.0e6
EPS = 1e-5
SETUP_ROWS = 10
SETUP_EXTRA = SETUP_ROWS + 4 + 16 + 4
SETUP_TURNED = SETUP_EXTRA + 3
SETUP_KEYS = SETUP_TURNED + 6 + 1 + 4
SETUP_PLACES = SETUP_KEYS + 16
SETUP_ADDR = SETUP_PLACES + 9
SETUP_DONE = SETUP_ADDR + 7 + 2
DEGREES = SETUP_DONE + 4

EARLY, PLAIN = 12, 26
MG, ME, MIXED = 14, 8, 12


def mixed_order(groups, eights):
    order, done = [], 0
    for n in range(eights * TPG):
        order.append(("scatter", n))
        upto = -(-(n + 1) * groups // eights)
        order += [("gather", m) for m in range(done, upto)]
        done = upto
    return order


def build(nc, t, out):
    ctx = ExitStack()
    with ctx:
        def sb(name, shape, dt=F32):
            return ctx.enter_context(nc.sbuf_tensor(name, shape, dt))

        def sem(name):
            return ctx.enter_context(nc.semaphore(name))

        def dram(name, shape):
            return nc.dram_tensor(name, shape, F32, kind="Internal").ap()

        table = dram("table", (N, D))
        qtable = dram("qtable", (N + WIN, D))
        degs = dram("degs", (1, N))
        table_rows = table.rearrange("(p j) f -> p (j f)", j=NJ)
        q_rows = qtable[0:N, :].rearrange("(p j) f -> p (j f)", j=NJ)
        x_node_rows = t["x"].rearrange("(p j) f -> p (j f)", j=NJ)
        xres = dram("xres", (N, D)).rearrange("(p j) f -> p (j f)", j=NJ)
        keys = dram("keys", (1, DT * P + 2 * P))
        amat = nc.dram_tensor("amat", (DB * P * NJ * WIN, 1), BF16, kind="Internal").ap()
        amat_rows = amat.rearrange("(r n) a -> r (n a)", n=NJ * WIN)
        out_rows = out.rearrange("(p j) f -> p (j f)", j=NJ)

        AGG = sb("AGG", [D + 1, N + WIN])
        PARTS = sb("PARTS", [P, NJ * 3 * D], BF16)
        SRC = sb("SRC", [P, GROUPS * TPG], I32)
        REL = sb("REL", [P, GROUPS * TPG])
        G = sb("G", [P, 2, TPG, D + 1])
        IDX = sb("IDX", [P, 2, TPG], I32)
        QW = sb("QW", [P, 2, D])
        work = sb("work", [P, 11720])
        CW = CH * D
        XC = work[:, 0:CW]
        SQ = work[:, CW:2 * CW]
        H = [work[:, (2 + k) * CW:(3 + k) * CW] for k in range(2)]
        SW = CH * NP
        AGS = [work[0:D + 1, 4 * CW + k * SW:4 * CW + (k + 1) * SW] for k in range(2)]
        HTS = [work[0:D + 1, 4 * CW + (2 + k) * SW:4 * CW + (3 + k) * SW] for k in range(2)]
        QB = G[:, :, :, :].rearrange("p k i f -> p (k i f)")[:, 0:CW]
        R1 = work[:, 8840:9800]
        XL = [work[:, 9800 + k * CW:9800 + (k + 1) * CW] for k in range(2)]
        AB = [work[:, a:a + ACW // 2].bitcast(BF16) for a in (2048, 3328, 4608, 8840, 10120)]
        DSB = work[:, 5888:5888 + 3 * D]
        KB = [work[:, 8840 + k * KW:8840 + (k + 1) * KW] for k in range(2)]
        JUNK = work[:, 2048:2048 + 3 * P // 2].bitcast(BF16)
        ZERO = work[:, 5408:5408 + ACW // 4].bitcast(BF16)
        OH = [work[:, k * TPG * WIN:(k + 1) * TPG * WIN].rearrange("p (i w) -> p i w", i=TPG) for k in range(2)]
        ATTR = [work[:, 2048 + k * TPG * D:2048 + (k + 1) * TPG * D] for k in range(2)]
        OHT = work[:, 3584:3584 + GE]
        MSG = work[:, 4608:4608 + TPG * D].rearrange("p (i f) -> p i f", i=TPG)
        PRE = work[:, 5376:5376 + TPG * D].rearrange("p (i f) -> p i f", i=TPG)
        RT = work[0:D + 1, 4 * CW + 2 * SW:4 * CW + 2 * SW + GE]
        DSTI = work[:, 0:GROUPS * TPG].bitcast(I32)
        XTAB = work[:, 1600:1600 + 3 * GROUPS].rearrange("p (c g) -> p c g", c=3)
        XEQ = work[:, 2200:2200 + GROUPS]
        XM = work[:, 2400:2400 + GROUPS]
        XD = work[:, 2600:2600 + 4 * P].rearrange("p (c k) -> p c k", c=4)
        WR = work[:, 4 * CW:4 * CW + 11 * D].rearrange("p (c f) -> p c f", c=11)
        WTR = work[:, 4 * CW + 11 * D:4 * CW + 11 * D + 4 * P].rearrange("p (c k) -> p c k", c=4)
        MS, MD, MF0, MF1, MF2, MF3 = (work[:, 6300 + k * MB * P:6300 + (k + 1) * MB * P] for k in range(6))
        MT = work[:, 2048:2048 + 2 * DT].rearrange("p (c t) -> p c t", c=2)
        IOI = work[:, 3200:3200 + GROUPS + 1].bitcast(I32)

        small = sb("small", [P, 2 * CH * 4])
        st = [small[:, c * 2 * CH:(c + 1) * 2 * CH] for c in range(4)]
        ident = sb("ident", [P, P])
        ones = sb("ones", [P, P])
        IOF = sb("IOF", [P, GROUPS])
        PCOL = sb("PCOL", [P, 1])
        SHIFT = sb("SHIFT", [P, P])
        XREL = sb("XREL", [P, TPG])
        col = sb("col", [P, 12])
        rowf = sb("rowf", [1, 4 * GROUPS])
        rowi = sb("rowi", [1, 2 * GROUPS], I32)
        XI = sb("XI", [1, 3 * P], I32)
        NX = sb("NX", [1, 1], I32)
        DEG = sb("DEG", [P, NJ])
        DINV = sb("DINV", [P, NJ])
        RDEG = sb("RDEG", [P, NJ])
        epsc = sb("epsc", [P, 1])
        zcol = sb("zcol", [P, 1])
        mones = sb("mones", [1, P])
        identb = sb("identb", [P, P], BF16)
        KEYC = sb("KEYC", [P, DT])
        ADDR = sb("ADDR", [P, DT], I32)
        MULT = sb("MULT", [P, DT])
        SIDX = sb("SIDX", [P, 2, TPG], I32)
        SVAL = sb("SVAL", [P, 2, TPG], BF16)
        FAST = sb("FAST", [1, 1], I32)
        okrow = sb("okrow", [1, 8])
        W = sb("W", [P, 18 * D])
        BASE_I, LAST_I = rowi[:, 0:GROUPS], rowi[:, GROUPS:2 * GROUPS]
        C_ROW, CX_ROW, BASE_F, NE_ROW = (rowf[:, k * GROUPS:(k + 1) * GROUPS] for k in range(4))

        def wt(k, rows=D + 1, n=1):
            return W[0:rows, k * D:(k + n) * D]

        w_self, w_nb = [wt(0), wt(1)], [wt(2), wt(3)]
        w_l1 = wt(4)
        w_l2 = [wt(5, D), wt(6, D), wt(7, D)]
        w_m1 = wt(8, D, 2)
        w_m2 = wt(10)
        w_u1 = [wt(11, D), wt(12, D)]
        w_u2 = wt(13)
        b_l2 = [wt(14 + k, P) for k in range(3)]
        bcols = sb("bcols", [D, 2])

        PS = ctx.enter_context(nc.psum_tensor("PS", [P, 8, 512], F32))

        s_edges = sem("s_edges")
        s_rows = sem("s_rows")
        s_x = sem("s_x")
        s_w = sem("s_w")
        s_const = sem("s_const")
        s_dv = sem("s_dv")
        s_pe = sem("s_pe")
        s_ready = sem("s_ready")
        s_degd = sem("s_degd")
        s_degl = sem("s_degl")
        s_rt = sem("s_rt")
        n_chain = sem("n_chain")
        n_ags = sem("n_ags")
        n_cleared = sem("n_cleared")
        n_uns = sem("n_uns")
        n_hts = sem("n_hts")
        n_xl = [sem(f"n_xl{k}") for k in range(2)]
        n_hi = sem("n_hi")
        n_r1 = sem("n_r1")
        n_mid = sem("n_mid")
        n_lo = sem("n_lo")
        n_out = sem("n_out")
        n_read = sem("n_read")
        n_xc = sem("n_xc")
        n_sq = sem("n_sq")
        n_var = sem("n_var")
        n_sd = sem("n_sd")
        n_h = sem("n_h")
        n_tr = sem("n_tr")
        n_ev = sem("n_ev")
        n_st = sem("n_st")
        n_pq = sem("n_pq")
        n_pqc = sem("n_pqc")
        n_hid = sem("n_hid")
        n_rel = sem("n_rel")
        s_store = sem("s_store")
        a_idx = sem("a_idx")
        a_rows = [[sem(f"a_rows{s}{k}") for k in range(2)] for s in range(2)]
        a_oh = sem("a_oh")
        a_sum = sem("a_sum")
        a_acc = sem("a_acc")
        e_attr = [sem(f"e_attr{k}") for k in range(2)]
        e_q = [sem(f"e_q{k}") for k in range(2)]
        e_turn = sem("e_turn")
        e_oht = sem("e_oht")
        e_q2e = sem("e_q2e")
        e_add = sem("e_add")
        e_pre = sem("e_pre")
        e_rel = sem("e_rel")
        e_out = sem("e_out")
        e_msg = sem("e_msg")
        e_idx, e_oh, e_sum, e_acc = (sem(n) for n in ("e_idx", "e_oh", "e_sum", "e_acc"))
        e_rows = [sem(f"e_rows{k}") for k in range(2)]
        f_idx, f_oh, f_sum, f_acc = (sem(n) for n in ("f_idx", "f_oh", "f_sum", "f_acc"))
        f_rows = [sem(f"f_rows{k}") for k in range(2)]
        s_zero = sem("s_zero")
        s_m = sem("s_m")
        s_key = sem("s_key")
        s_addr = sem("s_addr")
        s_kb = [sem(f"s_kb{k}") for k in range(2)]
        s_cnt = sem("s_cnt")
        s_fill = sem("s_fill")
        s_scat = sem("s_scat")
        s_fast = sem("s_fast")
        s_zmem = sem("s_zmem")
        d_ld = [sem(f"d_ld{m}") for m in range(AC)]
        d_mm = sem("d_mm")
        d_cp = sem("d_cp")
        d_turn = sem("d_turn")
        d_add = sem("d_add")
        x_rows = [sem("x_rows0"), sem("x_rows1")]
        x_idx, x_sub, x_oh, x_sum, x_acc = (
            sem(n) for n in ("x_idx", "x_sub", "x_oh", "x_sum", "x_acc"))
        x_ld, x_turn, x_oht, x_q2e, x_add, x_pre, x_rel, x_out, x_msg = (
            sem(n) for n in ("x_ld", "x_turn", "x_oht", "x_q2e", "x_add", "x_pre", "x_rel", "x_out", "x_msg"))

        TURN_B, Q_B, PRE_B, OUT_B = (0, 4), (2, 3), (5, 6), (1, 7)
        EWIN = PS[0:D, OUT_B[0], 4 * D:4 * D + WIN]
        HE = GE // 2

        PHASES = ["in", "l0a", "l0b", "l1", "l2a", "l2b", "l2c"]
        NCH = NJ // CH
        NONE = "the tables are built on the chip from destinations in range"

        def cols(view, j0, n=CH):
            return view[:, 0:N].rearrange("f (p j) -> f j p", j=NJ)[:, bass.ds(j0, n), :]

        def c3(ap):
            return ap[0:NP, :].rearrange("p (j f) -> p j f", f=D)

        def banks(b):
            return PS[0:NP, b:b + 2, 0:5 * D].rearrange("p b (j f) -> p b j f", f=D)

        def c4(ap):
            return ap[0:NP, :].rearrange("p (b j f) -> p b j f", b=2, f=D)

        def per_block(v):
            return v.rearrange("p (b j) -> p b j", b=2).unsqueeze(3).to_broadcast([NP, 2, 5, D])

        def per_block3(v):
            return v.unsqueeze(2).to_broadcast([NP, CH, D])

        def load(eng, etype, ap, hi):
            return nc.values_load(ap, engines=[etype], min_val=0, max_val=hi,
                                  skip_runtime_bounds_check_because=NONE)

        block = ctx.enter_context(nc.Block())
        ET = mybir.EngineType

        @block.sync
        def _(sp):
            for name, dst in (("src", SRC[:, :]), ("dst", DSTI)):
                sp.dma_start(dst[:, 0:(GROUPS - 1) * TPG].rearrange("p (g i) -> p g i", i=TPG),
                             t[name][0:(GROUPS - 1) * GE].rearrange("(g p i) -> p g i", p=P, i=TPG)
                             ).then_inc(s_edges, 16)
                sp.dma_start(dst[:, (GROUPS - 1) * TPG:GROUPS * TPG],
                             t[name][LAST:E].rearrange("(p i) -> p i", i=TPG)).then_inc(s_edges, 16)
            d2 = t["dst"][0:(GROUPS - 1) * GE].rearrange("(a g k) -> a g k", a=1, k=GE)
            sp.dma_start(BASE_I[:, 0:GROUPS - 1], d2[:, :, 0], allow_slow_non_contiguous=True).then_inc(s_rows, 16)
            sp.dma_start(LAST_I[:, 0:GROUPS - 1], d2[:, :, GE - 1], allow_slow_non_contiguous=True).then_inc(s_rows, 16)
            first = (GROUPS - 1) * GE
            sp.dma_start(BASE_I[:, GROUPS - 1:GROUPS], t["dst"][first:first + 1].rearrange("(a k) -> a k", a=1)
                         ).then_inc(s_rows, 16)
            sp.dma_start(LAST_I[:, GROUPS - 1:GROUPS], t["dst"][E - 1:E].rearrange("(a k) -> a k", a=1)
                         ).then_inc(s_rows, 16)
            for dst, name in ((MS, "src"), (MD, "dst")):
                sp.dma_start(dst[0:MR, :].bitcast(I32).rearrange("r (b e) -> r b e", b=MB),
                             t[name][0:DT * P].rearrange("(b r e) -> r b e", b=MB, e=P)).then_inc(s_m, 16)
            row = lambda ap: ap.rearrange("(a f) -> a f", a=1)
            for l in range(2):
                sp.dma_start(WR[0:D, l, :], t["L0_gnn_W1"][l]).then_inc(s_w, 16)
                sp.dma_start(WR[D:D + 1, l, :], t["L0_gnn_b1"][l:l + 1, :]).then_inc(s_w, 16)
                sp.dma_start(WR[0:D, 2 + l, :], t["L0_gnn_W0"][l]).then_inc(s_w, 16)
                sp.dma_start(WR[D:D + 1, 2 + l, :], t["L0_gnn_b0"][l:l + 1, :]).then_inc(s_w, 16)
                sp.dma_start(WR[0:D, 4 + l, :], t["L0_gnn_W2"][l, 0:D, :]).then_inc(s_w, 16)
                sp.dma_start(WR[0:D, 6 + l, :], t["L0_gnn_W2"][l, D:2 * D, :]).then_inc(s_w, 16)
                sp.dma_start(WR[D:D + 1, 8 + l, :], t["L0_gnn_b2"][l:l + 1, :]).then_inc(s_w, 16)
            for dst, src in ((w_l1[0:D], t["L1_gnn_W"]), (w_l1[D:D + 1], row(t["L1_gnn_b"])),
                             (w_l2[0], t["L2_gnn_W1"]), (w_l2[1], t["L2_gnn_W2"]), (w_l2[2], t["L2_gnn_W3"]),
                             (w_m1[:, 0:D], t["L3_gnn_Wm1"][0:D, :]), (w_m1[:, D:2 * D], t["L3_gnn_Wm1"][D:2 * D, :]),
                             (w_m2[0:D], t["L3_gnn_Wm2"]), (w_m2[D:D + 1], row(t["L3_gnn_bm2"])),
                             (w_u1[0], t["L3_gnn_Wu1"][0:D, :]), (w_u1[1], t["L3_gnn_Wu1"][D:2 * D, :]),
                             (w_u2[0:D], t["L3_gnn_Wu2"]), (w_u2[D:D + 1], row(t["L3_gnn_bu2"])),
                             (bcols[:, 0:1], t["L3_gnn_bm1"].rearrange("(f a) -> f a", a=1)),
                             (bcols[:, 1:2], t["L3_gnn_bu1"].rearrange("(f a) -> f a", a=1))):
                sp.dma_start(dst, src).then_inc(s_w, 16)
            for k, name in enumerate(("L2_gnn_b1", "L2_gnn_b2", "L2_gnn_b3")):
                sp.dma_start(b_l2[k], row(t[name]).to_broadcast([P, D])).then_inc(s_w, 16)

            stores = [0]

            def node_stores(phase):
                b, m = phase * NCH, 1 + (PHASES[phase] in ("l0b", "l1"))
                with sp.Fori(0, PAIRS) as i:
                    for k in range(2):
                        c = i * 2 + k
                        sp.wait_ge(n_h, c + (b + 1))
                        sp.dma_start(table_rows[:, bass.ds(c * CW, CW)], H[k][0:NP, :]).then_inc(s_store, 16)
                        if m == 2:
                            sp.dma_start(xres[:, bass.ds(c * CW, CW)], XL[k][0:NP, :]).then_inc(s_store, 16)
                        sp.wait_ge(s_store, c * (16 * m) + (stores[0] + m) * 16)
                        sp.sem_inc(n_st, 1)
                stores[0] += m * NCH

            sp.sem_inc(n_st, 2)
            sp.wait_ge(s_dv, SETUP_KEYS)
            sp.wait_ge(s_const, 11)
            for at in (0, P + DT * P):
                sp.dma_start(keys[:, at:at + P], mones[:, :]).then_inc(s_key, 16)
            sp.dma_start(keys[0, P:P + DT * P].rearrange("(b r e) -> r b e", b=MB, e=P),
                         MF1[0:MR, :].rearrange("r (b e) -> r b e", b=MB)).then_inc(s_key, 16)
            sp.wait_ge(s_key, 48)
            node_stores(0)
            sp.wait_ge(s_ready, 1)
            n_extra = load(sp, ET.SP, NX[0:1, 0:1], EXTRA)
            sp.wait_ge(n_lo, 2 + NCH)
            with sp.Fori(0, DG // 2) as i:
                for k in range(2):
                    sp.wait_ge(s_cnt, i * 16 + (8 * k + 8))
                    sp.dma_start(KB[k], keys[:, bass.ds((i * 2 + k) * GE, KW)].to_broadcast([P, KW])
                                 ).then_inc(s_kb[k], 16)
            sp.wait_ge(a_acc, 2 + GROUPS)
            with sp.If(n_extra > 0):
                sp.wait_ge(x_acc, 1 + EXTRA)
            sp.dma_start(degs, AGG[D:D + 1, 0:N]).then_inc(s_degd, 16)
            sp.wait_ge(s_degd, 16)
            sp.dma_start(DEG[0:NP, :], degs.rearrange("a (p j) -> (a p) j", j=NJ)).then_inc(s_degl, 16)
            sp.wait_ge(s_fast, 1)
            fast = load(sp, ET.SP, FAST[0:1, 0:1], 1)
            for phase in range(1, 6):
                node_stores(phase)
                b0 = (phase - 1) * DB
                with sp.If(fast > 0):
                    sp.wait_ge(n_lo, 2 + (phase + 1) * NCH)
                    sp.wait_ge(n_tr, 2 + NCH * max(0, phase - 2))
                    sp.wait_ge(s_scat, 16 * DT)
                    with sp.Fori(0, DB) as d:
                        for m in range(AC):
                            sp.wait_ge(d_mm, d * AC + (b0 * AC + m + 1))
                            sp.dma_start(AB[m], amat_rows[bass.ds(d * P, P), m * ACW:(m + 1) * ACW]
                                         ).then_inc(d_ld[m], 16)
            with sp.Fori(0, PAIRS) as i:
                for k in range(2):
                    c = i * 2 + k
                    sp.wait_ge(n_pqc, c + 3)
                    sp.dma_start(table_rows[:, bass.ds(c * CW, CW)], H[k][0:NP, :]).then_inc(s_store, 16)
                    sp.dma_start(q_rows[:, bass.ds(c * CW, CW)], QB[0:NP, :]).then_inc(s_store, 16)
                    sp.dma_start(xres[:, bass.ds(c * CW, CW)], XL[k][0:NP, :]).then_inc(s_store, 16)
                    sp.wait_ge(s_store, c * 48 + (stores[0] + 3) * 16)
                    sp.sem_inc(n_st, 1)
            stores[0] += 3 * NCH
            sp.wait_ge(s_const, 1)
            sp.dma_start(qtable[N:N + WIN, :], QW[:, 1, :]).then_inc(s_x, 16)
            sp.wait_ge(s_x, 16)

            def attributes(row):
                return t["edge_attr_96"][bass.ds(row, GE), :].rearrange("(p i) f -> p (i f)", i=TPG)

            def edge_loads(g, row, k):
                sp.wait_ge(e_sum, g + 1)
                base = load(sp, ET.SP, BASE_I[0:1, bass.ds(g, 1)], N - 1)
                sp.dma_start(ATTR[k], attributes(row)).then_inc(e_attr[k], 16)
                sp.dma_start(QW[:, k, :], qtable[bass.ds(base, WIN), :]).then_inc(e_q[k], 16)

            with sp.Fori(0, GROUPS // 2 - 1) as i:
                for k in range(2):
                    edge_loads(i * 2 + k, (i * 2 + k) * GE, k)
            edge_loads(GROUPS - 2, (GROUPS - 2) * GE, 0)
            edge_loads(GROUPS - 1, LAST, 1)
            with sp.If(n_extra > 0):
                sp.wait_ge(e_acc, 2 + GROUPS)
                with sp.Fori(0, EXTRA) as j:
                    sp.wait_ge(x_acc, j + (6 * EXTRA + 1))
                    base = load(sp, ET.SP, XI[0:1, bass.ds(j + P, 1)], N - 1)
                    row = load(sp, ET.SP, XI[0:1, bass.ds(j + 2 * P, 1)], LAST)
                    sp.dma_start(ATTR[0], attributes(row)).then_inc(x_ld, 16)
                    sp.dma_start(QW[:, 0, :], qtable[bass.ds(base, WIN), :]).then_inc(x_ld, 16)
            with sp.Fori(0, PAIRS) as i:
                for k in range(2):
                    c = i * 2 + k
                    sp.wait_ge(n_h, c + (7 * NCH + 1))
                    sp.dma_start(out_rows[:, bass.ds(c * CW, CW)], H[k][0:NP, :]).then_inc(s_store, 16)
                    sp.wait_ge(s_store, c * 16 + (stores[0] + 1) * 16)
                    sp.sem_inc(n_st, 1)

        @block.gpsimd
        def _(pool):
            pool.memset(QW[:, :, :], 0.0).then_inc(s_const, 1)
            pool.memset(AGG[:, :], 0.0).then_inc(s_const, 1)
            pool.memset(G[:, :, :, D:D + 1], 1.0).then_inc(s_const, 1)
            pool.memset(mones[:, :], -1.0).then_inc(s_const, 1)
            pool.wait_ge(s_const, 4)
            pool.memset(ones[:, :], 1.0).then_inc(s_const, 1)
            pool.memset(epsc[:, :], EPS).then_inc(s_const, 1)
            pool.memset(zcol[:, :], 0.0).then_inc(s_const, 1)
            pool.iota(IOI[:, 0:GROUPS], pattern=[[1, GROUPS]], base=0, channel_multiplier=0).then_inc(s_const, 1)
            pool.iota(IOI[:, GROUPS:GROUPS + 1], pattern=[[1, 1]], base=0, channel_multiplier=1).then_inc(s_const, 1)
            pool.memset(ident[:, :], 0.0).then_inc(s_const, 1)
            pool.wait_ge(s_const, 10)
            pool.affine_select(out=ident[:, :], in_=ident[:, :], compare_op=ALU.not_equal, fill=1.0,
                               base=0, pattern=[[-1, P]], channel_multiplier=1).then_inc(s_const, 1)
            pool.wait_ge(s_dv, SETUP_ADDR)
            pool.tensor_tensor(ADDR[:, :], MT[:, 0, :].bitcast(I32), MT[:, 1, :].bitcast(I32), ALU.add
                               ).then_inc(s_addr, 1)
            pool.wait_ge(s_ready, 1)
            n_extra = load(pool, ET.Pool, NX[0:1, 0:1], EXTRA)

            def gather(k, i, done):
                pool.indirect_dma_start(G[:, k, i, 0:D], None, table,
                                        bass.IndirectOffsetOnAxis(ap=IDX[:, k, i:i + 1], axis=0)).then_inc(done, 16)

            def group(k, when, idx, done):
                pool.wait_ge(idx, when)
                pool.nop(nofuse=True)
                for i in range(TPG):
                    gather(k, i, done)

            def extras(a):
                with pool.If(n_extra > 0):
                    with pool.Fori(0, EXTRA) as j:
                        group(0, j + (a * EXTRA + 1), x_idx, x_rows[a // 4])

            def first_aggregation():
                pool.wait_ge(n_st, 2 + NCH)
                pool.nop(nofuse=True)
                with pool.Fori(0, PLAIN // 2) as i:
                    for k in range(2):
                        group(k, i * 2 + (k + 1), a_idx, a_rows[0][k])

                def mixed(i, groups, eights):
                    for kind, n in mixed_order(groups, eights):
                        if kind == "gather":
                            g = n // TPG
                            if n % TPG == 0:
                                pool.wait_ge(a_idx, i * MG + (PLAIN + g + 1))
                                pool.nop(nofuse=True)
                            gather(g % 2, n % TPG, a_rows[0][g % 2])
                        else:
                            e = n // TPG
                            if n % TPG == 0:
                                pool.wait_ge(s_fill, i * ME + (e + 1))
                                pool.nop(nofuse=True)
                            if n:
                                pool.wait_ge(s_scat, i * (16 * TPG * ME) + 16 * n)
                                pool.nop(nofuse=True)
                            pool.indirect_dma_start(
                                amat, bass.IndirectOffsetOnAxis(ap=SIDX[:, e % 2, n % TPG:n % TPG + 1], axis=0),
                                SVAL[:, e % 2, n % TPG:n % TPG + 1], None).then_inc(s_scat, 16)
                    pool.wait_ge(s_scat, i * (16 * TPG * ME) + 16 * TPG * eights)
                    pool.nop(nofuse=True)

                pool.wait_ge(s_zero, 16 * DB)
                pool.nop(nofuse=True)
                with pool.Fori(0, MIXED) as i:
                    mixed(i, MG, ME)
                mixed(MIXED, GROUPS - PLAIN - MIXED * MG, DG - MIXED * ME)
                extras(0)

            def aggregation(a):
                pool.wait_ge(n_st, 2 + (a + 1) * NCH)
                pool.nop(nofuse=True)
                with pool.If(fast > 0):
                    with pool.Fori(0, DG // 2) as i:
                        for k in range(2):
                            group(k, i * 2 + ((a - 1) * DG + k + 1), f_idx, f_rows[k])
                with pool.Else():
                    with pool.Fori(0, GROUPS // 2) as i:
                        for k in range(2):
                            group(k, i * 2 + (a * GROUPS + k + 1), a_idx, a_rows[a // 4][k])
                    extras(a)

            def edge_network():
                pool.wait_ge(n_st, 2 + 7 * NCH)
                pool.nop(nofuse=True)
                with pool.Fori(0, GROUPS // 2) as i:
                    for k in range(2):
                        group(k, i * 2 + (k + 1), e_idx, e_rows[k])
                extras(6)

            loads = [0]

            def node(phase):
                name = PHASES[phase] if phase < 7 else "fin"
                h0 = phase * NCH
                src = {"in": x_node_rows, "l0b": x_node_rows, "l1": xres, "l2c": xres, "fin": xres}.get(name)

                def load_x(c, k):
                    pool.wait_ge(n_st, c + (h0 + 1))
                    pool.nop(nofuse=True)
                    pool.dma_start(XL[k][0:NP, :], src[:, bass.ds(c * CW, CW)]).then_inc(n_xl[k], 16)

                def split(c, k):
                    if name == "fin":
                        return
                    parts = PARTS[0:NP, bass.ds(c * (3 * CW), 3 * CW)].rearrange("p (j m f) -> p j m f", m=3, f=D)
                    pool.wait_ge(n_hi, c + (h0 + 1))
                    pool.wait_ge(n_lo, c + (h0 + 2))
                    pool.nop(nofuse=True)
                    pool.tensor_tensor(c3(R1), c3(H[k]), parts[:, :, 0, :], ALU.subtract).then_inc(n_r1, 1)
                    pool.wait_ge(n_mid, c + (h0 + 1))
                    pool.nop(nofuse=True)
                    pool.tensor_tensor(parts[:, :, 2, :], c3(R1), parts[:, :, 1, :], ALU.subtract).then_inc(n_lo, 1)

                if src is None:
                    with pool.Fori(0, PAIRS) as i:
                        for k in range(2):
                            split(i * 2 + k, k)
                    return
                if phase > 1 and name != "fin":
                    with pool.If(fast > 0):
                        pool.wait_ge(d_add, 1 + (phase - 1) * DB)
                load_x(0, 0)
                with pool.Fori(0, PAIRS - 1) as i:
                    for k in range(2):
                        load_x(i * 2 + k + 1, 1 - k)
                        split(i * 2 + k, k)
                load_x(NCH - 1, 1)
                split(NCH - 2, 0)
                split(NCH - 1, 1)

            pool.sem_inc(n_lo, 2)
            node(0)
            first_aggregation()
            pool.wait_ge(s_fast, 1)
            fast = load(pool, ET.Pool, FAST[0:1, 0:1], 1)
            for a in range(1, 6):
                node(a)
                aggregation(a)
            node(6)
            edge_network()
            node(7)

        @block.scalar
        def _(act):
            act.sem_inc(n_ev, 1)
            act.sem_inc(n_rel, 1)
            act.sem_inc(n_hts, 1)
            act.wait_ge(s_const, 11)
            act.wait_ge(s_zmem, 1)
            def clear_block(d):
                act.dma_start(amat_rows[bass.ds(d * P, P), :].rearrange("p (m n) -> p m n", m=2 * AC),
                              ZERO.unsqueeze(1).to_broadcast([P, 2 * AC, ACW // 2])).then_inc(s_zero, 16)

            with act.Fori(0, EARLY) as d:
                clear_block(d)
            count = {"xc": 0, "ev": 0, "uns": 0}

            def aggregated(a):
                if a == 0:
                    act.wait_ge(a_acc, 2 + GROUPS)
                    with act.If(n_extra > 0):
                        act.wait_ge(x_acc, 1 + EXTRA)
                else:
                    with act.If(fast > 0):
                        act.wait_ge(f_acc, 2 + a * DG)
                        act.wait_ge(d_add, 1 + a * DB)
                    with act.Else():
                        act.wait_ge(a_acc, 2 + (a + 1) * GROUPS)
                        with act.If(n_extra > 0):
                            act.wait_ge(x_acc, 1 + (a + 1) * EXTRA)

            def node(phase):
                name = PHASES[phase]
                stats = {"in": 1, "l0a": 1, "l0b": 2, "l1": 1, "l2a": 0, "l2b": 0, "l2c": 1}[name]
                turn = name in ("l1", "l2a", "l2b", "l2c")
                unsplit = name in ("l0a", "l0b")
                clear = name in ("l0a", "l0b", "l2c")
                xc0, ev0, uns0, q0, h0 = count["xc"], count["ev"], count["uns"], (phase - 1) * NCH, phase * NCH

                def stage(c, k):
                    if name == "in":
                        return
                    act.wait_ge(n_out, c + (q0 + 1))
                    act.nop(nofuse=True)
                    act.activation(AGS[k].rearrange("f (j p) -> f j p", j=CH), cols(AGG, c * CH), ACT.Copy
                                   ).then_inc(n_ags, 1)
                    if clear:
                        act.wait_ge(n_ags, c + (q0 + 1))
                        act.nop(nofuse=True)
                        act.activation(cols(AGG[0:D], c * CH), zcol[0:D, 0:1].unsqueeze(2).to_broadcast([D, CH, NP]),
                                       ACT.Copy).then_inc(n_cleared, 1)
                    if unsplit:
                        stage_input(c + (uns0 + 1), k)

                def step(c, k):
                    for s in range(stats):
                        v = c * stats + (xc0 + s + 1)
                        act.wait_ge(n_xc, v)
                        act.activation(SQ[0:NP, :], XC[0:NP, :], ACT.Square).then_inc(n_sq, 1)
                        act.wait_ge(n_var, v)
                        if name == "l0a" or (name == "l0b" and s == 0):
                            act.activation(st[2][0:NP, 0:CH], st[1][0:NP, 0:CH], ACT.Sqrt, bias=0.0,
                                           scale=1.0 / (D - 1)).then_inc(n_sd, 1)
                        else:
                            act.activation(st[2][0:NP, 0:CH], st[1][0:NP, 0:CH], ACT.Sqrt, bias=epsc[0:NP, 0:1],
                                           scale=1.0 / D).then_inc(n_sd, 1)
                    parts = PARTS[0:NP, bass.ds(c * (3 * CW), 3 * CW)].rearrange("p (j m f) -> p j m f", m=3, f=D)
                    act.wait_ge(n_h, c + (h0 + 1))
                    act.nop(nofuse=True)
                    act.activation(parts[:, :, 0, :], c3(H[k]), ACT.Copy).then_inc(n_hi, 1)
                    if turn:
                        act.wait_ge(n_tr, c + (ev0 + 3))
                        if name == "l2c":
                            hs = HTS[k][0:D, :].rearrange("f (j p) -> f j p", j=CH)
                            act.wait_ge(n_pqc, c + 1)
                            dst = [hs[:, 0:4, :], hs[:, 4:8, :], hs[:, 8:10, :]]
                        else:
                            dst = [cols(AGG[0:D], c * CH + b, n) for b, n in ((0, 4), (4, 4), (8, 2))]
                        act.nop(nofuse=True)
                        for b, n in ((0, 4), (1, 4), (2, 2)):
                            last = act.activation(dst[b], PS[0:D, 4 + b, 0:n * NP].rearrange(
                                "f (j p) -> f j p", j=n), ACT.Copy)
                        last.then_inc(n_ev, 1)

                def second_part(c):
                    if name == "in":
                        clear_block(c + EARLY)
                    parts = PARTS[0:NP, bass.ds(c * (3 * CW), 3 * CW)].rearrange("p (j m f) -> p j m f", m=3, f=D)
                    act.wait_ge(n_r1, c + (h0 + 1))
                    act.nop(nofuse=True)
                    act.activation(parts[:, :, 1, :], c3(R1), ACT.Copy).then_inc(n_mid, 1)

                stage(0, 0)
                stage(1, 1)
                with act.Fori(0, PAIRS - 1) as i:
                    for k in range(2):
                        c = i * 2 + k
                        step(c, k)
                        stage(c + 2, k)
                        second_part(c)
                for c in (NCH - 2, NCH - 1):
                    step(c, c % 2)
                    second_part(c)
                count["xc"] += stats * NCH
                count["ev"] += NCH * turn
                count["uns"] += NCH * unsplit

            def stage_input(v, k):
                act.wait_ge(n_uns, v)
                for b, n in ((0, 4), (1, 4), (2, 2)):
                    last = act.activation(HTS[k][0:D, 4 * b * NP:(4 * b + n) * NP], PS[0:D, 4 + b, 0:n * NP], ACT.Copy)
                last.then_inc(n_hts, 1)

            def index(g, k, when, used, done, first=0):
                act.wait_ge(used, when)
                act.nop(nofuse=True)
                act.activation(IDX[:, k, :], SRC[:, bass.ds(g * TPG + first * TPG, TPG)], ACT.Copy).then_inc(done, 1)

            def first_indices():
                for lo, hi, clear in ((0, (DB - EARLY - NCH) // 4, True), ((DB - EARLY - NCH) // 4, PLAIN // 2, False)):
                    with act.Fori(lo, hi) as i:
                        for k in range(2):
                            index(i * 2 + k, k, i * 2 + (k + 1), a_sum, a_idx)
                            for n in range(2 * clear):
                                clear_block(i * 4 + (EARLY + NCH + 2 * k + n))

                def fill(s, k, landed):
                    act.wait_ge(s_cnt, s * TPG + 24)
                    if landed is not None:
                        act.wait_ge(s_scat, landed)
                    act.nop(nofuse=True)
                    act.activation(SIDX[:, k, :].bitcast(I16), ADDR[:, bass.ds(s * TPG, TPG)].bitcast(I16), ACT.Copy)
                    act.activation(SVAL[:, k, :], MULT[:, bass.ds(s * TPG, TPG)], ACT.Copy).then_inc(s_fill, 1)

                def mixed(i, groups, eights):
                    index(i * MG + PLAIN, 0, i * MG + (PLAIN + 1), a_sum, a_idx)
                    for kind, n in mixed_order(groups, eights):
                        if kind == "gather" and n % TPG == 0 and n:
                            g = n // TPG
                            index(i * MG + (PLAIN + g), g % 2, i * MG + (PLAIN + g + 1), a_sum, a_idx)
                        if kind == "scatter" and n % TPG == 0:
                            e = n // TPG
                            fill(i * ME + e, e % 2, None if e == 0 else i * (16 * TPG * ME) + (
                                16 if e == 1 else 16 * TPG * (e - 1)))

                act.wait_ge(s_addr, 1)
                with act.Fori(0, MIXED) as i:
                    mixed(i, MG, ME)
                mixed(MIXED, GROUPS - PLAIN - MIXED * MG, DG - MIXED * ME)

            def indices(a):
                with act.Fori(0, GROUPS // 2) as i:
                    for k in range(2):
                        index(i * 2 + k, k, i * 2 + (a * GROUPS + k + 1), a_sum, a_idx)

            def beside_dense(a):
                g0, b0 = (a - 1) * DG, (a - 1) * DB

                def copy_sums(d):
                    act.wait_ge(d_mm, d * AC + (b0 + 2) * AC)
                    act.activation(DSB, PS[:, 2, 0:3 * D], ACT.Copy).then_inc(d_cp, 1)

                for k in range(2):
                    index(k, k, g0 + k + 1, f_sum, f_idx, first=DG)
                with act.Fori(0, DG // 2 - 1) as i:
                    copy_sums(i)
                    for k in range(2):
                        index(i * 2 + (k + 2), k, i * 2 + (g0 + k + 3), f_sum, f_idx, first=DG)
                copy_sums(DG // 2 - 1)
                copy_sums(DG // 2)

            def copy_turned(when, turned, done):
                act.wait_ge(turned, when)
                for b in range(2):
                    last = act.activation(OHT[:, b * HE:(b + 1) * HE], PS[:, TURN_B[b], :], ACT.Copy)
                last.then_inc(done, 1)

            def relu(v, pre, done):
                for b in range(2):
                    act.wait_ge(pre, v + (b + 1))
                    act.activation(RT[0:D, b * HE:(b + 1) * HE], PS[0:D, PRE_B[b], :], ACT.Relu,
                                   bias=bcols[:, 0:1]).then_inc(done, 1)

            def edge_network():
                index(0, 0, 2, e_sum, e_idx)
                index(1, 1, 2, e_sum, e_idx)
                copy_turned(1, e_turn, e_oht)
                with act.Fori(0, GROUPS // 2 - 1) as i:
                    for k in range(2):
                        g = i * 2 + k
                        relu(g * 2, e_pre, e_rel)
                        index(g + 2, k, g * 2 + 2, e_add, e_idx)
                        copy_turned(g + 2, e_turn, e_oht)
                relu(GROUPS * 2 - 4, e_pre, e_rel)
                copy_turned(GROUPS, e_turn, e_oht)
                relu(GROUPS * 2 - 2, e_pre, e_rel)

            def extras(a):
                with act.If(n_extra > 0):
                    if a < 6:
                        act.wait_ge(a_sum, 2 + (a + 1) * GROUPS)
                    else:
                        act.wait_ge(e_sum, 2 + GROUPS)
                    with act.Fori(0, EXTRA) as j:
                        act.wait_ge(x_acc, j + (a * EXTRA + 1))
                        g = load(act, ET.Activation, XI[0:1, bass.ds(j, 1)], GROUPS - 1)
                        act.nop(nofuse=True)
                        act.activation(IDX[:, 0, :], SRC[:, bass.ds(g * TPG, TPG)], ACT.Copy).then_inc(x_idx, 1)
                        if a == 6:
                            copy_turned(j + 1, x_turn, x_oht)
                            relu(j * 2, x_pre, x_rel)

            node(0)
            act.wait_ge(s_ready, 1)
            n_extra = load(act, ET.Activation, NX[0:1, 0:1], EXTRA)
            first_indices()
            extras(0)
            act.wait_ge(s_dv, DEGREES)
            act.activation(DINV[0:NP, :], DEG[0:NP, :], ACT.Sqrt).then_inc(s_rt, 1)
            act.wait_ge(s_fast, 1)
            fast = load(act, ET.Activation, FAST[0:1, 0:1], 1)
            for a in range(1, 6):
                aggregated(a - 1)
                node(a)
                with act.If(fast > 0):
                    beside_dense(a)
                with act.Else():
                    indices(a)
                    extras(a)
            aggregated(5)
            node(6)
            edge_network()
            extras(6)
            act.wait_ge(s_w, 16 * 32)
            with act.Fori(0, PAIRS) as i:
                for k in range(2):
                    c = i * 2 + k
                    act.wait_ge(n_out, c + (6 * NCH + 1))
                    stage_input(c + (count["uns"] + 1), k)
                    act.wait_ge(n_hid, c + 1)
                    for b, n in ((0, 4), (1, 4), (2, 2)):
                        last = act.activation(HTS[k][0:D, 4 * b * NP:(4 * b + n) * NP], PS[0:D, 4 + b, 0:n * NP],
                                              ACT.Relu, bias=bcols[:, 1:2])
                    last.then_inc(n_rel, 1)

        @block.vector
        def _(dve):
            dve.sem_inc(n_read, 2)
            dve.sem_inc(a_acc, 2)
            dve.memset(ZERO, 0.0).then_inc(s_zmem, 1)
            dve.sem_inc(x_acc, 1)
            dve.sem_inc(n_pqc, 2)
            for s, v in ((e_acc, 2), (f_acc, 2), (d_add, 1), (s_cnt, 2 * TPG)):
                dve.sem_inc(s, v)
            steps = [0]

            def link(ins):
                steps[0] += 1
                ins.then_inc(s_dv, 1)
                dve.wait_ge(s_dv, steps[0])

            dve.wait_ge(s_const, 11)
            link(dve.tensor_copy(IOF[:, :], IOI[:, 0:GROUPS]))
            link(dve.tensor_copy(PCOL[:, :], IOI[:, GROUPS:GROUPS + 1]))
            dve.wait_ge(s_edges, 64)
            dve.wait_ge(s_rows, 64)
            link(dve.tensor_copy(REL[:, :], DSTI))
            link(dve.tensor_copy(BASE_F, BASE_I))
            link(dve.tensor_tensor(LAST_I, LAST_I, BASE_I, ALU.subtract))
            link(dve.tensor_scalar(LAST_I, LAST_I, WIN.bit_length() - 1, None, ALU.arith_shift_right))
            link(dve.tensor_copy(NE_ROW, LAST_I))
            link(dve.tensor_tensor_scan(C_ROW, ones[0:1, 0:1].to_broadcast([1, GROUPS]), NE_ROW, 0.0,
                                        ALU.mult, ALU.add))
            link(dve.tensor_tensor(CX_ROW, C_ROW, NE_ROW, ALU.subtract))
            link(dve.tensor_copy(NX[0:1, 0:1], C_ROW[:, GROUPS - 1:GROUPS]))
            assert steps[0] == SETUP_ROWS
            dve.wait_ge(s_pe, 1)
            link(dve.tensor_copy(XTAB[:, 0:2, :], PS[:, 0, 0:2 * GROUPS].rearrange("p (c g) -> p c g", c=2)))
            link(dve.tensor_copy(XTAB[:, 2, :], PS[:, 1, 0:GROUPS]))
            link(dve.tensor_tensor(REL[:, :].rearrange("p (g i) -> p g i", i=TPG),
                                   REL[:, :].rearrange("p (g i) -> p g i", i=TPG),
                                   XTAB[:, 2, :].unsqueeze(2).to_broadcast([P, GROUPS, TPG]), ALU.subtract))
            link(dve.memset(REL[0:MASKED, (GROUPS - 1) * TPG:GROUPS * TPG], FAR))
            gj, cx, gb, used, shift = (col[:, k:k + 1] for k in range(5))
            four = [col[:, 8 + k:9 + k] for k in range(4)]
            link(dve.tensor_scalar(XEQ, XTAB[:, 0, :], PCOL[:, 0:1], None, ALU.is_le))
            link(dve.reduce_sum(gj, XEQ, AX))
            link(dve.tensor_scalar(XEQ, IOF[:, :], gj, None, ALU.is_equal))
            link(dve.tensor_tensor(XM, XEQ, XTAB[:, 1, :], ALU.mult))
            link(dve.reduce_sum(cx, XM, AX))
            link(dve.tensor_tensor(XM, XEQ, XTAB[:, 2, :], ALU.mult))
            link(dve.reduce_sum(gb, XM, AX))
            link(dve.tensor_tensor(used, PCOL[:, 0:1], XTAB[:, 0, GROUPS - 1:GROUPS], ALU.is_lt))
            link(dve.tensor_tensor(shift, PCOL[:, 0:1], cx, ALU.subtract))
            link(dve.tensor_scalar(shift, shift, 1.0, float(WIN), ALU.add, ALU.mult))
            link(dve.tensor_scalar(four[0], gj, float(GROUPS - 1), None, ALU.min))
            link(dve.tensor_tensor(gb, gb, shift, ALU.add))
            link(dve.tensor_tensor(four[1], gb, used, ALU.mult))
            link(dve.tensor_scalar(four[2], four[0], float(GE), float(LAST), ALU.mult, ALU.min))
            link(dve.tensor_scalar(used, used, -1.0, FAR, ALU.add, ALU.mult))
            link(dve.tensor_tensor(four[3], shift, used, ALU.add))
            for k in range(4):
                link(dve.tensor_scalar(XD[:, k, :], ident[:, :], four[k], None, ALU.mult))
            assert steps[0] == SETUP_EXTRA
            dve.wait_ge(s_pe, 2)
            link(dve.tensor_copy(XI[0:1, :], PS[0:1, 2, 0:3 * P]))
            link(dve.tensor_copy(SHIFT[:, :], PS[:, 2, 3 * P:4 * P]))
            dve.wait_ge(s_pe, 3)
            link(dve.tensor_copy(WTR[0:D, :, 0:D + 1], PS[0:D, 3, 0:4 * P].rearrange("f (c k) -> f c k", c=4)[:, :, 0:D + 1]))
            assert steps[0] == SETUP_TURNED
            dve.wait_ge(s_pe, 4)
            for l in range(2):
                link(dve.tensor_copy(w_self[l], PS[0:D + 1, 4, l * D:(l + 1) * D]))
                link(dve.tensor_tensor(w_self[l][D:D + 1, :], w_self[l][D:D + 1, :], WR[D:D + 1, 8 + l, :], ALU.add))
                link(dve.tensor_copy(w_nb[l], PS[0:D + 1, 4, (2 + l) * D:(3 + l) * D]))
            link(dve.tensor_copy(identb[:, :], ident[:, :]))
            ms, md, f0, f1, f2, f3 = (v[0:MR, :] for v in (MS, MD, MF0, MF1, MF2, MF3))
            ms, md = ms.bitcast(I32), md.bitcast(I32)
            stt = dve.scalar_tensor_tensor
            dve.wait_ge(s_m, 32)
            link(dve.tensor_copy(f0, ms))
            link(dve.tensor_scalar(ms, md, 1023, None, ALU.bitwise_and))
            link(dve.tensor_copy(f1, ms))
            link(stt(out=f1, in0=f1, scalar=16384.0, in1=f0, op0=ALU.mult, op1=ALU.add))
            assert steps[0] == SETUP_KEYS
            link(dve.tensor_scalar(ms, f0, 0.01, None, ALU.mult))
            link(dve.tensor_copy(f2, ms))
            link(stt(out=f3, in0=f2, scalar=-float(NJ), in1=f0, op0=ALU.mult, op1=ALU.add))
            link(dve.tensor_scalar(f0, f3, 0.0, None, ALU.is_lt))
            link(dve.tensor_tensor(f2, f2, f0, ALU.subtract))
            link(stt(out=f3, in0=f0, scalar=float(NJ), in1=f3, op0=ALU.mult, op1=ALU.add))
            link(dve.tensor_scalar(f0, f3, float(NJ), None, ALU.is_ge))
            link(dve.tensor_tensor(f2, f2, f0, ALU.add))
            link(stt(out=f3, in0=f0, scalar=-float(NJ), in1=f3, op0=ALU.mult, op1=ALU.add))
            link(dve.tensor_scalar(ms, md, WIN - 1, None, ALU.bitwise_and))
            link(dve.tensor_copy(f0, ms))
            link(stt(out=f0, in0=f3, scalar=float(WIN), in1=f0, op0=ALU.mult, op1=ALU.add))
            link(stt(out=f0, in0=f2, scalar=float(NJ * WIN), in1=f0, op0=ALU.mult, op1=ALU.add))
            link(dve.tensor_scalar(ms, md, WIN.bit_length() - 1, None, ALU.arith_shift_right))
            link(dve.tensor_copy(f2, ms))
            link(dve.tensor_scalar(f2, f2, float(DB - 1), None, ALU.min))
            assert steps[0] == SETUP_PLACES
            for c, dst in enumerate((KEYC[:, :], MT[:, 0, :], MT[:, 1, :])):
                dve.wait_ge(s_pe, 5 + c)
                for b, (b0, b1) in enumerate(((0, 4), (4, MB))):
                    link(dve.tensor_copy(dst[:, b0 * MR:b1 * MR], PS[:, 2 * c + b, 0:(b1 - b0) * MR]))
            link(dve.tensor_scalar(MT[:, 1, :], MT[:, 1, :], float(P * NJ * WIN), None, ALU.mult))
            link(dve.tensor_copy(MT[:, 0, :].bitcast(I32), MT[:, 0, :]))
            link(dve.tensor_copy(MT[:, 1, :].bitcast(I32), MT[:, 1, :]))
            assert steps[0] == SETUP_ADDR
            gap, top, none, ok, mdeg = (okrow[:, k:k + 1] for k in range(5))
            link(dve.tensor_tensor(NE_ROW[:, 0:DG], BASE_F[:, 1:DG + 1], BASE_F[:, 0:DG], ALU.subtract))
            link(dve.reduce_max(gap, NE_ROW[:, 0:DG], AX))
            link(dve.tensor_scalar(gap, gap, 512.0, None, ALU.is_le))
            link(dve.tensor_scalar(top, BASE_F[:, DG:DG + 1], float(DB * WIN), None, ALU.is_lt))
            link(dve.tensor_scalar(none, C_ROW[:, GROUPS - 1:GROUPS], 0.0, None, ALU.is_equal))
            link(dve.tensor_tensor(ok, gap, top, ALU.mult))
            link(dve.tensor_tensor(ok, ok, none, ALU.mult))
            dve.wait_ge(s_addr, 1)
            dve.wait_ge(s_key, 48)
            for k in range(2):
                link(dve.memset(HTS[k][D:D + 1, :], 1.0))
            dve.sem_inc(s_ready, 1)

            assert steps[0] == SETUP_DONE

            count = {"chain": 0, "xc": 0, "tr": 0, "xl": 0}

            def node(phase):
                name = PHASES[phase] if phase < 7 else "fin"
                ch0, xc0, tr0 = count["chain"], count["xc"], count["tr"]
                q0, h0 = (phase - 1) * NCH, phase * NCH
                stats_n = {"in": 1, "l0a": 1, "l0b": 2, "l1": 1, "l2a": 0, "l2b": 0, "l2c": 1, "fin": 0}[name]
                turn = name in ("l1", "l2a", "l2b", "l2c")
                has_x = name in ("in", "l0b", "l1", "l2c", "fin")
                xl0 = count["xl"]

                chain_n = {"in": 3, "l0a": 3, "l0b": 7, "l1": 5, "l2a": 1, "l2b": 1, "l2c": 6, "fin": 0}[name]

                def chunk(i, k):
                    c = i * 2 + k
                    n = [0, 0]

                    def then(ins):
                        n[0] += 1
                        ins.then_inc(n_chain, 1)
                        dve.wait_ge(n_chain, c * chain_n + (ch0 + n[0]))

                    def stats(src, view):
                        n[1] += 1
                        v = c * stats_n + (xc0 + n[1])
                        mean = st[0][0:NP, 0:CH]
                        if view == 4:
                            then(dve.reduce_sum(mean.rearrange("p (b j) -> p b j", b=2), src, AX))
                        else:
                            then(dve.reduce_sum(mean, src, AX))
                        then(dve.tensor_scalar(mean, mean, -1.0 / D, None, ALU.mult))
                        if view == 4:
                            dve.tensor_tensor(c4(XC), src, per_block(mean), ALU.add).then_inc(n_xc, 1)
                        else:
                            dve.tensor_tensor(c3(XC), src, per_block3(mean), ALU.add).then_inc(n_xc, 1)
                        dve.wait_ge(n_sq, v)
                        dve.reduce_sum(st[1][0:NP, 0:CH], c3(SQ), AX).then_inc(n_var, 1)
                        dve.wait_ge(n_sd, v)
                        then(dve.reciprocal(st[3][0:NP, 0:CH], st[2][0:NP, 0:CH]))

                    def h_free():
                        dve.wait_ge(n_st, c + (h0 + 1))
                        dve.wait_ge(n_tr, c + (tr0 + 1) if turn else tr0 + 2)
                        dve.wait_ge(n_lo, c + (h0 + 1) if name != "fin" else h0 + 2)

                    inv = st[3][0:NP, 0:CH]
                    xk = XL[k][0:NP, :]
                    if has_x:
                        dve.wait_ge(n_xl[k], i * 16 + (xl0 + 16))
                    dinv = DINV[0:NP, bass.ds(c * CH, CH)]
                    if name != "in":
                        dve.wait_ge(n_out, c + (q0 + 3))
                        prod = banks(2 * k)
                    if name == "l0a":
                        stats(prod, 4)
                        h_free()
                        dve.tensor_tensor(c4(H[k]), prod, per_block(inv), ALU.mult).then_inc(n_h, 1)
                        dve.wait_ge(n_h, c + (h0 + 1))
                        dve.sem_inc(n_read, 1)
                    elif name == "fin":
                        h_free()
                        dve.tensor_tensor(c4(H[k]), xk.rearrange("p (b j f) -> p b j f", b=2, f=D), prod,
                                          ALU.add).then_inc(n_h, 1)
                        dve.wait_ge(n_h, c + (h0 + 1))
                        dve.sem_inc(n_read, 1)
                    else:
                        if name == "l0b":
                            stats(prod, 4)
                            dve.tensor_tensor(c4(XC), prod, per_block(inv), ALU.mult).then_inc(n_read, 1)
                        elif name == "l1":
                            dve.tensor_tensor(c4(XC), prod, per_block(RDEG[0:NP, bass.ds(c * CH, CH)]),
                                              ALU.mult).then_inc(n_read, 1)
                        elif name != "in":
                            dve.tensor_tensor(c4(XC), prod, per_block(dinv), ALU.mult).then_inc(n_read, 1)
                        if name != "in":
                            dve.wait_ge(n_read, c + (q0 + 3))
                        if name in ("l2a", "l2b", "l2c"):
                            bias = b_l2[("l2a", "l2b", "l2c").index(name)][0:NP, :]
                            then(dve.tensor_tensor(c3(XC), c3(XC), bias.unsqueeze(1).to_broadcast([NP, CH, D]),
                                                   ALU.add))
                        if name in ("l0b", "l1", "l2c"):
                            then(dve.tensor_tensor(xk, xk, XC[0:NP, :], ALU.add))
                        if name in ("l2a", "l2b"):
                            scale = dinv
                        else:
                            stats(xk.rearrange("p (j f) -> p j f", f=D), 3)
                            if name == "l1":
                                then(dve.tensor_tensor(inv, inv, dinv, ALU.mult))
                            scale = inv
                        h_free()
                        dve.scalar_tensor_tensor(out=c3(H[k]), in0=c3(XC), scalar=0.0, in1=per_block3(scale),
                                                 op0=ALU.max, op1=ALU.mult).then_inc(n_h, 1)
                        dve.wait_ge(n_h, c + (h0 + 1))
                        if name == "l2c":
                            dve.wait_ge(n_pq, c + 1)
                            dve.wait_ge(n_st, c + (h0 + 2))
                            dve.wait_ge(n_lo, c + (h0 + 3))
                            then(dve.tensor_copy(c4(H[k]), banks(2 * k)))
                            dve.tensor_copy(c4(QB), banks(4)).then_inc(n_pqc, 1)
                    assert n[0] == chain_n, (name, n[0])

                with dve.Fori(0, PAIRS) as i:
                    for k in range(2):
                        chunk(i, k)
                count["xl"] += has_x * PAIRS * 16
                count["chain"] += chain_n * NCH
                count["xc"] += stats_n * NCH
                count["tr"] += turn * NCH

            def one_hot(dst, rel):
                return dve.tensor_tensor(dst, IOF[:, 0:WIN].unsqueeze(1).to_broadcast([P, TPG, WIN]),
                                         rel.unsqueeze(2).to_broadcast([P, TPG, WIN]), ALU.is_equal)

            def accumulate(rows, base, sums):
                window = AGG[0:rows, bass.ds(base, WIN)]
                return dve.tensor_tensor(window, window, sums, ALU.add)

            def hidden_sum(k, v, q2e, done):
                for b in range(2):
                    dve.wait_ge(q2e, v + (b + 1))
                    dve.tensor_tensor(PRE[:, 4 * b:4 * b + 4, :],
                                      PS[:, Q_B[b], 0:4 * D].rearrange("p (i f) -> p i f", f=D),
                                      G[:, k, 4 * b:4 * b + 4, 0:D], ALU.add).then_inc(done, 1)

            def messages(k, v, outs, done):
                for b in range(2):
                    dve.wait_ge(outs, v + (b + 1))
                    dve.tensor_tensor(MSG[:, 4 * b:4 * b + 4, :],
                                      PS[:, OUT_B[b], 0:4 * D].rearrange("p (i f) -> p i f", f=D),
                                      ATTR[k][:, 4 * b * D:4 * (b + 1) * D].rearrange("p (i f) -> p i f", f=D),
                                      ALU.mult).then_inc(done, 1)

            def ready(a):
                dve.wait_ge(n_st, 2 + (a + 1) * NCH)
                dve.wait_ge(n_lo, 2 + (a + 1) * NCH)
                dve.wait_ge(n_tr, 2 + count["tr"])
                dve.wait_ge(n_ev, 1 + count["tr"])
                if a:
                    dve.wait_ge(n_cleared, {1: 1, 2: 2, 6: 3}.get(a, 2) * NCH)

            def make(g, k, when, used, done, first=0):
                dve.wait_ge(used, when)
                one_hot(OH[k], REL[:, bass.ds(g * TPG + first * TPG, TPG)]).then_inc(done, 1)

            def add(g, k, v, sums, accs, rows, net=False, first=0, dense=None):
                base = load(dve, ET.DVE, BASE_I[0:1, bass.ds(g + first, 1)], N - 1)
                dve.wait_ge(sums, v + 3)
                dve.wait_ge(accs, v + 2)
                if dense is not None:
                    dve.wait_ge(d_add, dense)
                accumulate(rows, base, EWIN if net else PS[0:rows, k, 0:WIN]).then_inc(accs, 1)

            def extras(a, rows, net=False):
                with dve.If(n_extra > 0):
                    with dve.Fori(0, EXTRA) as j:
                        v = j + (a * EXTRA + 1)
                        g = load(dve, ET.DVE, XI[0:1, bass.ds(j, 1)], GROUPS - 1)
                        base = load(dve, ET.DVE, XI[0:1, bass.ds(j + P, 1)], N - 1)
                        dve.wait_ge(x_acc, v)
                        dve.tensor_scalar(XREL[:, :], REL[:, bass.ds(g * TPG, TPG)], SHIFT[:, bass.ds(j, 1)], None,
                                          ALU.subtract).then_inc(x_sub, 1)
                        dve.wait_ge(x_sub, v)
                        one_hot(OH[0], XREL[:, :]).then_inc(x_oh, 1)
                        if net:
                            dve.wait_ge(x_rows[1], j * (16 * TPG) + (2 * EXTRA + 1) * 16 * TPG)
                            hidden_sum(0, j * 2, x_q2e, x_add)
                            dve.wait_ge(x_ld, j * 32 + 32)
                            messages(0, j * 2, x_out, x_msg)
                        dve.wait_ge(x_sum, v)
                        accumulate(rows, base, EWIN if net else PS[0:rows, 0, 0:WIN]).then_inc(x_acc, 1)
                    dve.wait_ge(x_acc, (a + 1) * EXTRA + 1)

            def first_aggregation():
                def values(i, k):
                    dve.wait_ge(s_kb[k], i * 16 + 16)
                    for n in range(TPG):
                        tile = i * (2 * TPG) + (k * TPG + n)
                        dve.wait_ge(s_cnt, tile + 2 * TPG)
                        dve.tensor_scalar(JUNK, KB[k][:, n * P:(n + 3) * P], KEYC[:, bass.ds(tile, 1)], None,
                                          ALU.is_equal, ALU.add, accum_out=MULT[:, bass.ds(tile, 1)]).then_inc(s_cnt, 1)

                ready(0)
                make(0, 0, 1, a_sum, a_oh)
                with dve.Fori(0, DG // 2) as i:
                    for k in range(2):
                        g = i * 2 + k
                        make(g + 1, 1 - k, g + 2, a_sum, a_oh)
                        add(g, k, g, a_sum, a_acc, D + 1)
                        values(i, k)
                with dve.Fori(DG // 2, GROUPS // 2 - 1) as i:
                    for k in range(2):
                        g = i * 2 + k
                        make(g + 1, 1 - k, g + 2, a_sum, a_oh)
                        add(g, k, g, a_sum, a_acc, D + 1)
                make(GROUPS - 1, 1, GROUPS, a_sum, a_oh)
                add(GROUPS - 2, 0, GROUPS - 2, a_sum, a_acc, D + 1)
                add(GROUPS - 1, 1, GROUPS - 1, a_sum, a_acc, D + 1)
                extras(0, D + 1)

            def aggregation(a):
                ready(a)
                with dve.If(fast > 0):
                    g0, b0 = (a - 1) * DG, (a - 1) * DB

                    def add_block(d, v):
                        block_cols = AGG[0:D, bass.ds(d * WIN, WIN)]
                        dve.wait_ge(d_turn, d + (b0 + 1))
                        dve.wait_ge(f_acc, v + 2)
                        dve.wait_ge(d_add, d + (b0 + 1))
                        dve.tensor_tensor(block_cols, block_cols, PS[0:D, 3, 0:WIN], ALU.add).then_inc(d_add, 1)

                    def pair(i, last=False):
                        g = i * 2
                        add(g, 0, g + g0, f_sum, f_acc, D, first=DG, dense=i + (b0 + 1))
                        if not last:
                            make(g + 2, 0, g + (g0 + 3), f_sum, f_oh, first=DG)
                        add_block(i, g + (g0 + 1))
                        add(g + 1, 1, g + (g0 + 1), f_sum, f_acc, D, first=DG, dense=i + (b0 + 2))
                        if not last:
                            make(g + 3, 1, g + (g0 + 4), f_sum, f_oh, first=DG)

                    make(0, 0, g0 + 1, f_sum, f_oh, first=DG)
                    make(1, 1, g0 + 2, f_sum, f_oh, first=DG)
                    with dve.Fori(0, DG // 2 - 1) as i:
                        pair(i)
                    pair(DG // 2 - 1, last=True)
                    add_block(DB - 1, g0 + DG)
                with dve.Else():
                    g0 = a * GROUPS
                    make(0, 0, g0 + 1, a_sum, a_oh)
                    with dve.Fori(0, GROUPS // 2 - 1) as i:
                        for k in range(2):
                            g = i * 2 + k
                            make(g + 1, 1 - k, g + (g0 + 2), a_sum, a_oh)
                            add(g, k, g + g0, a_sum, a_acc, D)
                    make(GROUPS - 1, 1, g0 + GROUPS, a_sum, a_oh)
                    add(GROUPS - 2, 0, g0 + GROUPS - 2, a_sum, a_acc, D)
                    add(GROUPS - 1, 1, g0 + GROUPS - 1, a_sum, a_acc, D)
                    extras(a, D)

            def edge_network():
                def hidden(g, k, pair):
                    dve.wait_ge(e_rows[k], pair * (16 * TPG) + 16 * TPG)
                    hidden_sum(k, g * 2, e_q2e, e_add)

                def message(g, k, pair):
                    dve.wait_ge(e_attr[k], pair * 16 + 16)
                    messages(k, g * 2, e_out, e_msg)

                ready(6)
                make(0, 0, 1, e_sum, e_oh)
                make(1, 1, 2, e_sum, e_oh)
                hidden(0, 0, 0)
                with dve.Fori(0, GROUPS // 2 - 1) as i:
                    for k in range(2):
                        g = i * 2 + k
                        message(g, k, i)
                        hidden(g + 1, 1 - k, i + k)
                        add(g, k, g, e_sum, e_acc, D, net=True)
                        make(g + 2, k, g + 3, e_sum, e_oh)
                message(GROUPS - 2, 0, GROUPS // 2 - 1)
                hidden(GROUPS - 1, 1, GROUPS // 2 - 1)
                add(GROUPS - 2, 0, GROUPS - 2, e_sum, e_acc, D, net=True)
                message(GROUPS - 1, 1, GROUPS // 2 - 1)
                add(GROUPS - 1, 1, GROUPS - 1, e_sum, e_acc, D, net=True)
                extras(6, D, net=True)

            node(0)
            n_extra = load(dve, ET.DVE, NX[0:1, 0:1], EXTRA)
            first_aggregation()
            dve.wait_ge(s_degl, 16)
            link(dve.reduce_max(col[0:NP, 5:6], DEG[0:NP, :], AX))
            link(dve.tensor_scalar(RDEG[0:NP, :], DEG[0:NP, :], 1.0, None, ALU.max))
            link(dve.reciprocal(RDEG[0:NP, :], RDEG[0:NP, :]))
            link(dve.tensor_scalar(DEG[0:NP, :], DEG[0:NP, :], 1.0, None, ALU.add))
            assert steps[0] == DEGREES
            dve.wait_ge(s_rt, 1)
            link(dve.reciprocal(DINV[0:NP, :], DINV[0:NP, :]))
            dve.wait_ge(s_pe, 8)
            link(dve.reduce_max(mdeg, PS[0:1, 7, 0:NP], AX))
            link(dve.tensor_scalar(mdeg, mdeg, float(P), None, ALU.is_le))
            link(dve.tensor_tensor(ok, ok, mdeg, ALU.mult))
            link(dve.tensor_copy(FAST[:, :], ok))
            dve.sem_inc(s_fast, 1)
            fast = load(dve, ET.DVE, FAST[0:1, 0:1], 1)
            for a in range(1, 6):
                if a == 4:
                    dve.wait_ge(s_w, 16 * 32)
                node(a)
                aggregation(a)
            node(6)
            edge_network()
            node(7)

        @block.tensor
        def _(pe):
            pe.sem_inc(n_out, 2)
            pe.sem_inc(n_tr, 2)
            for s, v in ((a_sum, 2), (e_sum, 2), (f_sum, 2), (d_mm, AC)):
                pe.sem_inc(s, v)
            pe.wait_ge(s_const, 11)
            pe.wait_ge(s_dv, SETUP_ROWS)
            pe.matmul(PS[:, 0, 0:2 * GROUPS], ones[0:1, :], rowf[:, 0:2 * GROUPS], start=True, stop=True)
            pe.matmul(PS[:, 1, 0:GROUPS], ones[0:1, :], BASE_F, start=True, stop=True).then_inc(s_pe, 1)
            pe.wait_ge(s_dv, SETUP_EXTRA)
            pe.matmul(PS[:, 2, :], ones[:, :], XD, start=True, stop=True).then_inc(s_pe, 1)
            pe.wait_ge(s_w, 16 * 32)
            for m in range(4):
                last = pe.transpose(PS[0:D, 3, m * P:m * P + D + 1], WR[0:D + 1, m, :], ident[0:D + 1, 0:D + 1])
            last.then_inc(s_pe, 1)
            pe.wait_ge(s_dv, SETUP_TURNED)
            for m in range(4):
                last = pe.matmul(PS[0:D + 1, 4, m * D:(m + 1) * D], WTR[0:D, m, 0:D + 1], WR[0:D, 4 + m, :],
                                 start=True, stop=True)
            last.then_inc(s_pe, 1)
            for c, (v, src) in enumerate(((SETUP_KEYS, MF1), (SETUP_PLACES, MF0), (SETUP_PLACES, MF2))):
                pe.wait_ge(s_dv, v)
                for b in range(MB):
                    last = pe.transpose(PS[:, 2 * c + b // 4, (b % 4) * MR:(b % 4 + 1) * MR],
                                        src[0:MR, b * P:(b + 1) * P], ident[0:MR, 0:MR])
                last.then_inc(s_pe, 1)
            pe.wait_ge(s_ready, 1)
            n_extra = load(pe, ET.PE, NX[0:1, 0:1], EXTRA)
            count = {"tr": 0, "uns": 0}

            def node(phase):
                name = PHASES[phase] if phase < 7 else "fin"
                q0, h0, tr0, uns0 = (phase - 1) * NCH, phase * NCH, count["tr"], count["uns"]
                turn = name in ("l1", "l2a", "l2b", "l2c")

                def unsplit(c):
                    pe.wait_ge(n_hts, c + (uns0 + 1))
                    for j in range(CH):
                        for m in range(3):
                            last = pe.matmul(PS[0:D, 4 + j // 4, (j % 4) * NP:(j % 4 + 1) * NP],
                                             PARTS[0:NP, bass.ds(c * (3 * CW) + (3 * j + m) * D, D)],
                                             identb[0:NP, 0:NP], start=(m == 0), stop=(m == 2))
                    last.then_inc(n_uns, 1)
                    pe.wait_ge(n_hts, c + (uns0 + 2))

                def product(c, k):
                    if name == "fin":
                        pe.wait_ge(n_rel, c + 1)
                        unsplit(c)
                        for b, n in ((0, 4), (1, 4), (2, 2)):
                            o = PS[0:D, 4 + b, 0:n * NP].rearrange("f (j p) -> f j p", j=n)
                            pe.matmul(o, w_u1[0], HTS[k][0:D, 4 * b * NP:(4 * b + n) * NP].rearrange(
                                "f (j p) -> f j p", j=n), start=True, stop=False)
                            last = pe.matmul(o, w_u1[1], cols(AGG[0:D], c * CH + 4 * b, n), start=False, stop=True)
                        last.then_inc(n_hid, 1)
                        pe.wait_ge(n_rel, c + 2)
                        parts = [(HTS[k], w_u2, D + 1)]
                    else:
                        if name in ("l0a", "l0b"):
                            unsplit(c)
                        pe.wait_ge(n_ags, c + (q0 + 1))
                        if name in ("l0a", "l0b"):
                            l = name == "l0b"
                            parts = [(HTS[k], w_self[l], D + 1), (AGS[k], w_nb[l], D + 1)]
                        elif name == "l1":
                            parts = [(AGS[k], w_l1, D + 1)]
                        else:
                            parts = [(AGS[k], w_l2[("l2a", "l2b", "l2c").index(name)], D)]
                    pe.wait_ge(n_read, c + (q0 + 1))
                    if name == "l2c":
                        pe.wait_ge(n_pqc, c + 1)
                    for j in range(CH):
                        o = PS[0:NP, 2 * k + j // 5, (j % 5) * D:(j % 5 + 1) * D]
                        for m, (stage, w, rows) in enumerate(parts):
                            last = pe.matmul(o, stage[0:rows, j * NP:(j + 1) * NP], w,
                                             start=(m == 0), stop=(m == len(parts) - 1))
                    last.then_inc(n_out, 1)

                def turned(c, k):
                    pe.wait_ge(n_h, c + (h0 + 1))
                    pe.wait_ge(n_ev, c + (tr0 + 1))
                    if name == "l2c":
                        pe.wait_ge(n_pqc, c + 2)
                    for j in range(CH):
                        last = pe.transpose(PS[0:D, 4 + j // 4, (j % 4) * NP:(j % 4 + 1) * NP],
                                            H[k][0:NP, j * D:(j + 1) * D], ident[0:NP, 0:NP])
                    last.then_inc(n_tr, 1)
                    if name == "l2c":
                        pe.wait_ge(n_ev, c + (tr0 + 2))
                        for half, b0 in ((0, 2 * k), (1, 4)):
                            for j in range(CH):
                                last = pe.matmul(PS[0:NP, b0 + j // 5, (j % 5) * D:(j % 5 + 1) * D],
                                                 HTS[k][0:D, j * NP:(j + 1) * NP],
                                                 w_m1[:, half * D:(half + 1) * D], start=True, stop=True)
                        last.then_inc(n_pq, 1)

                if name == "fin":
                    pe.wait_ge(e_acc, 2 + GROUPS)
                    with pe.If(n_extra > 0):
                        pe.wait_ge(x_acc, 1 + 7 * EXTRA)
                if not turn:
                    with pe.Fori(0, PAIRS) as i:
                        for k in range(2):
                            product(i * 2 + k, k)
                else:
                    product(0, 0)
                    with pe.Fori(0, PAIRS - 1) as i:
                        for k in range(2):
                            product(i * 2 + k + 1, 1 - k)
                            turned(i * 2 + k, k)
                    product(NCH - 1, 1)
                    turned(NCH - 2, 0)
                    turned(NCH - 1, 1)
                count["tr"] += turn * NCH
                count["uns"] += NCH * (name in ("l0a", "l0b", "fin"))

            def window_sums(k, rows, done):
                for i in range(TPG):
                    last = pe.matmul(PS[0:rows, k, 0:WIN], G[:, k, i, 0:rows], OH[k][:, i, :],
                                     start=(i == 0), stop=(i == TPG - 1))
                last.then_inc(done, 1)

            def turn_one_hots(k, done):
                for i in range(TPG):
                    last = pe.transpose(PS[:, TURN_B[i // 4], (i % 4) * P:(i % 4 + 1) * P], OH[k][:, i, :],
                                        ident[:, :])
                last.then_inc(done, 1)

            def q_to_edges(k, done):
                for i in range(TPG):
                    last = pe.matmul(PS[:, Q_B[i // 4], (i % 4) * D:(i % 4 + 1) * D], OHT[:, i * P:(i + 1) * P],
                                     QW[:, k, :], start=True, stop=True)
                    if i % 4 == 3:
                        last.then_inc(done, 1)

            def turn_hidden(v, added, done):
                for i in range(TPG):
                    if i % 4 == 0:
                        pe.wait_ge(added, v + (i // 4 + 1))
                    last = pe.transpose(PS[0:D, PRE_B[i // 4], (i % 4) * P:(i % 4 + 1) * P], PRE[:, i, :],
                                        ident[:, :])
                    if i % 4 == 3:
                        last.then_inc(done, 1)

            def edge_out(v, rel, done):
                for b in range(2):
                    pe.wait_ge(rel, v + (b + 1))
                    for i in range(4 * b, 4 * b + 4):
                        last = pe.matmul(PS[:, OUT_B[b], (i % 4) * D:(i % 4 + 1) * D], RT[:, i * P:(i + 1) * P],
                                         w_m2, start=True, stop=True)
                    last.then_inc(done, 1)

            def message_sums(k, v, msg, done):
                for i in range(TPG):
                    if i % 4 == 0:
                        pe.wait_ge(msg, v + (i // 4 + 1))
                    last = pe.matmul(EWIN, MSG[:, i, :], OH[k][:, i, :], start=(i == 0), stop=(i == TPG - 1))
                last.then_inc(done, 1)

            def group(k, v, landed, rows_sem, oh, sums, accs, rows):
                pe.wait_ge(oh, v + 1)
                pe.wait_ge(rows_sem, landed)
                pe.wait_ge(accs, v + 1)
                window_sums(k, rows, sums)

            def all_groups(a, rows):
                with pe.Fori(0, GROUPS // 2) as i:
                    for k in range(2):
                        group(k, i * 2 + (a * GROUPS + k), i * (16 * TPG) + (a % 4 * GROUPS // 2 + 1) * 16 * TPG,
                              a_rows[a // 4][k], a_oh, a_sum, a_acc, rows)
                with pe.If(n_extra > 0):
                    pe.wait_ge(a_acc, 2 + (a + 1) * GROUPS)
                    with pe.Fori(0, EXTRA) as j:
                        pe.wait_ge(x_oh, j + (a * EXTRA + 1))
                        pe.wait_ge(x_rows[a // 4], j * (16 * TPG) + (a % 4 * EXTRA + 1) * 16 * TPG)
                        window_sums(0, rows, x_sum)

            def with_dense(a):
                g0, b0 = (a - 1) * DG, (a - 1) * DB

                def gathered(i, k):
                    group(k, i * 2 + (g0 + k), i * (16 * TPG) + (g0 // 2 + 1) * 16 * TPG, f_rows[k], f_oh, f_sum,
                          f_acc, D)

                def dense(d, pieces, later=True):
                    for m in pieces:
                        pe.wait_ge(d_ld[m], d * 16 + (b0 + 1) * 16)
                        if m == 0 and later:
                            pe.wait_ge(d_cp, d + b0)
                        for jj in range(NJ // AC):
                            j = m * (NJ // AC) + jj
                            last = pe.matmul(PS[:, 2, 0:3 * D], AB[m][0:NP, jj * WIN:(jj + 1) * WIN],
                                             PARTS[0:NP, j * 3 * D:(j + 1) * 3 * D], start=(j == 0),
                                             stop=(j == NJ - 1))
                        last.then_inc(d_mm, 1)

                def turn_sums(d):
                    pe.wait_ge(d_cp, d + (b0 + 1))
                    pe.wait_ge(d_add, d + (b0 + 1))
                    for m in range(3):
                        last = pe.matmul(PS[0:D, 3, 0:WIN], DSB[:, m * D:(m + 1) * D], ident[:, :],
                                         start=(m == 0), stop=(m == 2))
                    last.then_inc(d_turn, 1)

                pe.wait_ge(n_lo, 2 + (a + 1) * NCH)
                pe.wait_ge(n_read, 2 + a * NCH)
                dense(0, range(AC), later=False)
                with pe.Fori(0, DG // 2) as i:
                    gathered(i, 0)
                    turn_sums(i)
                    dense(i + 1, range(3))
                    gathered(i, 1)
                    dense(i + 1, range(3, AC))
                turn_sums(DB - 1)

            def edge_network():
                def q_part(g, k, pair):
                    pe.wait_ge(e_oht, g + 1)
                    pe.wait_ge(e_q[k], pair * 16 + 16)
                    q_to_edges(k, e_q2e)

                def group(g, k, pair, last=False):
                    turn_hidden(g * 2, e_add, e_pre)
                    if not last:
                        pe.wait_ge(e_oh, g + 2)
                        turn_one_hots(1 - k, e_turn)
                    pe.wait_ge(e_acc, g + 2)
                    edge_out(g * 2, e_rel, e_out)
                    if not last:
                        q_part(g + 1, 1 - k, pair + k)
                    message_sums(k, g * 2, e_msg, e_sum)

                pe.wait_ge(e_oh, 1)
                turn_one_hots(0, e_turn)
                q_part(0, 0, 0)
                with pe.Fori(0, GROUPS // 2 - 1) as i:
                    for k in range(2):
                        group(i * 2 + k, k, i)
                group(GROUPS - 2, 0, GROUPS // 2 - 1)
                group(GROUPS - 1, 1, GROUPS // 2 - 1, last=True)
                with pe.If(n_extra > 0):
                    pe.wait_ge(e_acc, 2 + GROUPS)
                    with pe.Fori(0, EXTRA) as j:
                        pe.wait_ge(x_oh, j + (6 * EXTRA + 1))
                        turn_one_hots(0, x_turn)
                        pe.wait_ge(x_oht, j + 1)
                        pe.wait_ge(x_ld, j * 32 + 32)
                        q_to_edges(0, x_q2e)
                        turn_hidden(j * 2, x_add, x_pre)
                        edge_out(j * 2, x_rel, x_out)
                        message_sums(0, j * 2, x_msg, x_sum)

            all_groups(0, D + 1)
            pe.wait_ge(s_dv, DEGREES)
            pe.transpose(PS[0:1, 7, 0:NP], col[0:NP, 5:6], ident[0:NP, 0:NP]).then_inc(s_pe, 1)
            pe.wait_ge(s_fast, 1)
            fast = load(pe, ET.PE, FAST[0:1, 0:1], 1)
            for a in range(1, 6):
                node(a)
                with pe.If(fast > 0):
                    with_dense(a)
                with pe.Else():
                    all_groups(a, D)
            node(6)
            edge_network()
            node(7)


_INS = ["x", "src", "dst", "edge_attr_96", "L0_gnn_W0", "L0_gnn_b0", "L0_gnn_W1", "L0_gnn_b1", "L0_gnn_W2",
        "L0_gnn_b2", "L1_gnn_W", "L1_gnn_b", "L2_gnn_W1", "L2_gnn_b1", "L2_gnn_W2", "L2_gnn_b2", "L2_gnn_W3",
        "L2_gnn_b3", "L3_gnn_Wm1", "L3_gnn_bm1", "L3_gnn_Wm2", "L3_gnn_bm2", "L3_gnn_Wu1", "L3_gnn_bu1",
        "L3_gnn_Wu2", "L3_gnn_bu2"]


def kernel(**inputs):
    import numpy as _np
    import concourse.bacc as _bacc
    from concourse import mybir as _mybir
    from concourse.bass_utils import run_bass_kernel_spmd as _run

    nc = _bacc.Bacc("TRN2", target_bir_lowering=False, num_devices=1)
    arrays, tensors = {}, {}
    for name in _INS:
        a = _np.ascontiguousarray(inputs[name])
        arrays[f"in_{name}_dram"] = a
        tensors[name] = nc.dram_tensor(f"in_{name}_dram", a.shape, _mybir.dt.from_np(a.dtype),
                                       kind="ExternalInput").ap()
    out = nc.dram_tensor("out_0_dram", (N, D), F32, kind="ExternalOutput").ap()
    build(nc, tensors, out)
    r = _run(nc, [arrays], core_ids=[0])
    return r.results[0]["out_0_dram"]
```
